# Optimizing a Trainium2 kernel written in Bass

```python
import numpy as np
import jax
import jax.numpy as jnp

def _softmax(x, axis=-1):
    return jax.nn.softmax(x, axis=axis)

def _gelu(x):
    return jax.nn.gelu(x, approximate=True)

def _silu(x):
    return jax.nn.silu(x)

def _sigmoid(x):
    return jax.nn.sigmoid(x)

def _layernorm(x, axis=-1, eps=1e-05):
    m = jnp.mean(x, axis=axis, keepdims=True)
    v = jnp.var(x, axis=axis, keepdims=True)
    return (x - m) / jnp.sqrt(v + eps)

def _scatter_add(tgt, idx, src, axis=0):
    return tgt.at[idx].add(src)

def _segment_sum(src, seg, n):
    return jax.ops.segment_sum(src, seg, n)
kernel_name = 'mk_seq_postln_d1_jaxref_r8_7cd4f9'

def setup_inputs(seed: int=0):
    np.random.seed(seed)
    _w = jnp.asarray

    def _L0_attn_setup():
        import jax, jax.numpy as jnp
        import numpy as np
        B, S, D, H = (2, 256, 128, 16)
        DH = D // H
        EPS = 1e-05
        LAMBDA_INIT = 0.8
        key = jax.random.key(seed)
        ks = jax.random.split(key, 16)
        w_std = 1.0 / np.sqrt(D)
        lam_std = LAMBDA_INIT / np.sqrt(DH)
        return {'x': jax.random.normal(ks[0], (B, S, D), jnp.float32), 'Wq': jax.random.normal(ks[1], (D, D), jnp.float32) * w_std, 'bq': jax.random.normal(ks[2], (D,), jnp.float32) * 0.02, 'Wk': jax.random.normal(ks[3], (D, D), jnp.float32) * w_std, 'bk': jax.random.normal(ks[4], (D,), jnp.float32) * 0.02, 'Wv': jax.random.normal(ks[5], (D, D), jnp.float32) * w_std, 'bv': jax.random.normal(ks[6], (D,), jnp.float32) * 0.02, 'Wo': jax.random.normal(ks[7], (D, D), jnp.float32) * w_std, 'bo': jax.random.normal(ks[8], (D,), jnp.float32) * 0.02, 'lq1': jax.random.normal(ks[9], (H, DH), jnp.float32) * lam_std, 'lk1': jax.random.normal(ks[10], (H, DH), jnp.float32) * lam_std, 'lq2': jax.random.normal(ks[11], (H, DH), jnp.float32) * lam_std, 'lk2': jax.random.normal(ks[12], (H, DH), jnp.float32) * lam_std, 'gn_w': jnp.ones((H, DH), jnp.float32), 'gn_b': jnp.zeros((H, DH), jnp.float32)}
    _L0_attn_in = _L0_attn_setup()

    def _L0_ffn_setup():
        import math
        import jax
        import jax.numpy as jnp
        import numpy as np
        B, T, D = (1, 256, 128)
        H, KV, DH = (16, 4, 64)
        E, TOPK, DFF = (32, 4, 128)
        WINDOW = 128
        EPS = 1e-05
        ROPE_BASE = 150000.0
        ROPE_SCALE = 32.0

        def _rmsnorm(x, w):
            rms = jax.lax.rsqrt(jnp.mean(x * x, axis=-1, keepdims=True) + EPS)
            return w * (x * rms)

        def _apply_rope(x, sin, cos):
            x1, x2 = (x[..., ::2], x[..., 1::2])
            out = jnp.stack([x1 * cos - x2 * sin, x1 * sin + x2 * cos], axis=-1)
            return out.reshape(x.shape)
        key = jax.random.key(seed)
        ks = jax.random.split(key, 12)
        s = 0.02
        return {'x': jax.random.normal(ks[0], (B, T, D), jnp.float32), 'attn_norm_w': 1.0 + 0.02 * jax.random.normal(ks[1], (D,), jnp.float32), 'ffn_norm_w': 1.0 + 0.02 * jax.random.normal(ks[2], (D,), jnp.float32), 'qkv_w': s * jax.random.normal(ks[3], (D, H * DH + 2 * KV * DH), jnp.float32), 'qkv_b': s * jax.random.normal(ks[4], (H * DH + 2 * KV * DH,), jnp.float32), 'proj_w': s * jax.random.normal(ks[5], (H * DH, D), jnp.float32), 'proj_b': s * jax.random.normal(ks[6], (D,), jnp.float32), 'attn_sink': 0.5 * jax.random.normal(ks[7], (H,), jnp.float32), 'gate_w': s * jax.random.normal(ks[8], (D, E), jnp.float32), 'gate_b': s * jax.random.normal(ks[9], (E,), jnp.float32), 'W_up': s * jax.random.normal(ks[10], (E, D, 2 * DFF), jnp.float32), 'W_down': s * jax.random.normal(ks[11], (E, DFF, D), jnp.float32)}
    _L0_ffn_in = _L0_ffn_setup()
    _d = {'L0_attn_x': _L0_attn_in['x'], 'L0_attn_Wq': _L0_attn_in['Wq'], 'L0_attn_bq': _L0_attn_in['bq'], 'L0_attn_Wk': _L0_attn_in['Wk'], 'L0_attn_bk': _L0_attn_in['bk'], 'L0_attn_Wv': _L0_attn_in['Wv'], 'L0_attn_bv': _L0_attn_in['bv'], 'L0_attn_Wo': _L0_attn_in['Wo'], 'L0_attn_bo': _L0_attn_in['bo'], 'L0_attn_lq1': _L0_attn_in['lq1'], 'L0_attn_lk1': _L0_attn_in['lk1'], 'L0_attn_lq2': _L0_attn_in['lq2'], 'L0_attn_lk2': _L0_attn_in['lk2'], 'L0_attn_gn_w': _L0_attn_in['gn_w'], 'L0_attn_gn_b': _L0_attn_in['gn_b'], 'L0_ffn_attn_norm_w': _L0_ffn_in['attn_norm_w'], 'L0_ffn_ffn_norm_w': _L0_ffn_in['ffn_norm_w'], 'L0_ffn_qkv_w': _L0_ffn_in['qkv_w'], 'L0_ffn_qkv_b': _L0_ffn_in['qkv_b'], 'L0_ffn_proj_w': _L0_ffn_in['proj_w'], 'L0_ffn_proj_b': _L0_ffn_in['proj_b'], 'L0_ffn_attn_sink': _L0_ffn_in['attn_sink'], 'L0_ffn_gate_w': _L0_ffn_in['gate_w'], 'L0_ffn_gate_b': _L0_ffn_in['gate_b'], 'L0_ffn_W_up': _L0_ffn_in['W_up'], 'L0_ffn_W_down': _L0_ffn_in['W_down']}
    _x0 = _d['L0_attn_x']
    _d['L0_attn_x'] = jax.random.normal(jax.random.fold_in(jax.random.key(seed), 1), (2, 1024, 128), dtype=_x0.dtype)
    del _x0
    return _d

def reference(L0_attn_x, L0_attn_Wq, L0_attn_bq, L0_attn_Wk, L0_attn_bk, L0_attn_Wv, L0_attn_bv, L0_attn_Wo, L0_attn_bo, L0_attn_lq1, L0_attn_lk1, L0_attn_lq2, L0_attn_lk2, L0_attn_gn_w, L0_attn_gn_b, L0_ffn_attn_norm_w, L0_ffn_ffn_norm_w, L0_ffn_qkv_w, L0_ffn_qkv_b, L0_ffn_proj_w, L0_ffn_proj_b, L0_ffn_attn_sink, L0_ffn_gate_w, L0_ffn_gate_b, L0_ffn_W_up, L0_ffn_W_down):

    def _L0_attn_ref(x, Wq, bq, Wk, bk, Wv, bv, Wo, bo, lq1, lk1, lq2, lk2, gn_w, gn_b):
        import jax, jax.numpy as jnp
        import numpy as np
        B, S, D, H = (2, 256, 128, 16)
        DH = D // H
        EPS = 1e-05
        LAMBDA_INIT = 0.8
        b, s, d = x.shape
        h, dh = lq1.shape
        scale = dh ** (-0.5)
        q = (x @ Wq + bq).reshape(b, s, h, dh)
        k = (x @ Wk + bk).reshape(b, s, h, dh)
        v = (x @ Wv + bv).reshape(b, s, h, dh)
        lam = jnp.exp((lq1 * lk1).sum(-1)) - jnp.exp((lq2 * lk2).sum(-1)) + LAMBDA_INIT
        scores = jnp.einsum('bihd,bjhd->bhij', q, k) * scale * lam[None, :, None, None]
        attn = jax.nn.softmax(scores, axis=-1)
        out = jnp.einsum('bhij,bjhd->bihd', attn, v)
        mean = out.mean(axis=(1, 3), keepdims=True)
        var = out.var(axis=(1, 3), keepdims=True)
        normed = (out - mean) * jax.lax.rsqrt(var + EPS)
        normed = normed * gn_w[None, None, :, :] + gn_b[None, None, :, :]
        y = normed.reshape(b, s, d) @ Wo + bo
        return y

    def _L0_ffn_ref(x, attn_norm_w, ffn_norm_w, qkv_w, qkv_b, proj_w, proj_b, attn_sink, gate_w, gate_b, W_up, W_down):
        import math
        import jax
        import jax.numpy as jnp
        import numpy as np
        B, T, D = (1, 256, 128)
        H, KV, DH = (16, 4, 64)
        E, TOPK, DFF = (32, 4, 128)
        WINDOW = 128
        EPS = 1e-05
        ROPE_BASE = 150000.0
        ROPE_SCALE = 32.0

        def _rmsnorm(x, w):
            rms = jax.lax.rsqrt(jnp.mean(x * x, axis=-1, keepdims=True) + EPS)
            return w * (x * rms)

        def _apply_rope(x, sin, cos):
            x1, x2 = (x[..., ::2], x[..., 1::2])
            out = jnp.stack([x1 * cos - x2 * sin, x1 * sin + x2 * cos], axis=-1)
            return out.reshape(x.shape)
        Bx, Tx, Dx = x.shape
        h = _rmsnorm(x, attn_norm_w)
        qkv = h @ qkv_w + qkv_b
        q = qkv[..., :H * DH].reshape(Bx, Tx, H, DH).transpose(0, 2, 1, 3)
        k = qkv[..., H * DH:H * DH + KV * DH].reshape(Bx, Tx, KV, DH).transpose(0, 2, 1, 3)
        v = qkv[..., H * DH + KV * DH:].reshape(Bx, Tx, KV, DH).transpose(0, 2, 1, 3)
        pos = jnp.arange(Tx, dtype=jnp.float32) / ROPE_SCALE
        inv_freq = 1.0 / ROPE_BASE ** (jnp.arange(0, DH, 2, dtype=jnp.float32) / DH)
        freqs = pos[:, None] * inv_freq[None, :]
        sin, cos = (jnp.sin(freqs), jnp.cos(freqs))
        q = _apply_rope(q, sin, cos)
        k = _apply_rope(k, sin, cos)
        rep = H // KV
        k = jnp.repeat(k, rep, axis=1)
        v = jnp.repeat(v, rep, axis=1)
        logits = jnp.einsum('bhqd,bhkd->bhqk', q, k) / math.sqrt(DH)
        i = jnp.arange(Tx)[:, None]
        j = jnp.arange(Tx)[None, :]
        mask = (j > i) | (i - j > WINDOW)
        logits = jnp.where(mask, -jnp.inf, logits)
        lse = jax.nn.logsumexp(logits, axis=-1, keepdims=True)
        denom_log = jnp.logaddexp(lse, attn_sink.reshape(1, H, 1, 1))
        attn = jnp.exp(logits - denom_log)
        y = jnp.einsum('bhqk,bhkd->bhqd', attn, v)
        y = y.transpose(0, 2, 1, 3).reshape(Bx, Tx, H * DH)
        x = x + (y @ proj_w + proj_b)
        h2 = _rmsnorm(x, ffn_norm_w).reshape(Bx * Tx, Dx)
        glogits = h2 @ gate_w + gate_b
        topv, topi = jax.lax.top_k(glogits, TOPK)
        gw = jax.nn.softmax(topv, axis=-1)
        N = Bx * Tx
        combine = jnp.zeros((N, E), x.dtype).at[jnp.arange(N)[:, None], topi].add(gw)

        def body(acc, we):
            wu, wd, ce = we
            ug = h2 @ wu
            u, g = (ug[:, :DFF], ug[:, DFF:])
            return (acc + ce[:, None] * (jax.nn.silu(g) * u @ wd), None)
        y2, _ = jax.lax.scan(body, jnp.zeros_like(h2), (W_up, W_down, combine.T))
        return x + y2.reshape(Bx, Tx, Dx)
    x = L0_attn_x
    x = _layernorm(x + _L0_attn_ref(x, L0_attn_Wq, L0_attn_bq, L0_attn_Wk, L0_attn_bk, L0_attn_Wv, L0_attn_bv, L0_attn_Wo, L0_attn_bo, L0_attn_lq1, L0_attn_lk1, L0_attn_lq2, L0_attn_lk2, L0_attn_gn_w, L0_attn_gn_b), axis=-1)
    x = _layernorm(x + _L0_ffn_ref(x, L0_ffn_attn_norm_w, L0_ffn_ffn_norm_w, L0_ffn_qkv_w, L0_ffn_qkv_b, L0_ffn_proj_w, L0_ffn_proj_b, L0_ffn_attn_sink, L0_ffn_gate_w, L0_ffn_gate_b, L0_ffn_W_up, L0_ffn_W_down), axis=-1)
    return x

_drawn_inputs = setup_inputs


def setup_inputs(seed=0):
    import zlib

    import numpy as np

    out = dict(_drawn_inputs(seed))
    spreads = {'L0_attn_gn_w': (1.0, 0.2), 'L0_attn_gn_b': (0.0, 0.1)}
    factors = {'L0_attn_bq': 4.89,
     'L0_attn_bk': 8.0,
     'L0_attn_bo': 3.82,
     'L0_ffn_attn_norm_w': 8.0,
     'L0_ffn_ffn_norm_w': 8.0,
     'L0_ffn_qkv_b': 8.0,
     'L0_ffn_proj_b': 5.336,
     'L0_ffn_attn_sink': 8.0,
     'L0_ffn_gate_w': 8.0,
     'L0_ffn_gate_b': 8.0,
     'L0_ffn_W_up': 8.0,
     'L0_ffn_W_down': 8.0}
    for name, (base, spread) in spreads.items():
        noise = np.random.default_rng([zlib.crc32(name.encode()), seed]).standard_normal(out[name].shape)
        drawn = base * np.exp(spread * noise) if base else spread * noise
        out[name] = jnp.asarray(drawn.astype(out[name].dtype))
    for name, factor in factors.items():
        out[name] = (out[name] * factor).astype(out[name].dtype)
    return out
```

```python
from contextlib import ExitStack

import numpy as np

import concourse.bass as bass
from concourse import mybir

F32 = mybir.dt.float32
BF16 = mybir.dt.bfloat16
ALU = mybir.AluOpType
ACT = mybir.ActivationFunctionType
AX = mybir.AxisListType

B, S, D, H = 2, 1024, 128, 16
DH = D // H
P = 128
TILES = S // P
HG = 4
GROUPS = B * H // HG
EPS = 1e-5
LAMBDA_INIT = 0.8
QK_ROWS = 96
PARTS_Q = (0, 0, 1, 0, 2, 1)
PARTS_K = (0, 1, 0, 2, 0, 1)
SHIFT_ROW = len(PARTS_Q) * DH
STEPS = 2 * TILES
ds = bass.ds


def differential_attention(nc, t, x1, ident, ident16, ones_row, eps_unused=None):
    with ExitStack() as ctx:
        def sb(name, shape, dt=F32):
            return ctx.enter_context(nc.sbuf_tensor(name, shape, dt))

        def sem(name):
            return ctx.enter_context(nc.semaphore(name))

        qk_parts = nc.dram_tensor("qk_parts", [2, 3, P, B * S], BF16, kind="Internal")

        x_in = x1
        xT = sb("xT", [P, B * S])
        w_attn = sb("w_attn", [P, 4, D])
        head_mean = sb("head_mean", [P, P])
        cols = sb("cols", [P, 8])
        rows = sb("rows", [1, 2, D])
        lam = sb("lam", [P, 8])
        q_stack = sb("q_stack", [QK_ROWS, 2 * GROUPS, HG, 512], BF16)
        k_stack = sb("k_stack", [QK_ROWS, GROUPS, HG, S], BF16)
        v_all = sb("v_all", [P, TILES, GROUPS, HG * DH])
        v_stage = sb("v_stage", [P, TILES, HG, 32])
        e_ring = sb("e_ring", [P, 4, 2, 512])
        part = sb("part", [P, 2, 3, 512], BF16)
        fl = sb("fl", [P, 2, 512])
        max_parts = sb("max_parts", [P, 2, HG, 4, 2])
        shift = sb("shift", [P, HG, 4])
        shift_rest = sb("shift_rest", [P, HG, 4])
        shift16 = sb("shift16", [P, 2, HG, 4], BF16)
        shiftT = sb("shiftT", [2 * HG * 4, P], BF16)
        o_raw = sb("o_raw", [P, 512])
        o_inv = sb("o_inv", [P, 4, HG])
        o_all = sb("o_all", [P, TILES, GROUPS, HG * DH])
        normT = xT[:, 0:S]
        bn = sb("bn", [P, 2, 6])
        st = sb("st", [P, 16])
        bnt = sb("bnt", [P, TILES, 6])
        mv = sb("mv", [P, TILES, 2])
        rstd = sb("rstd", [P, TILES])
        eps_t = sb("eps_t", [P, TILES])
        half_t = sb("half_t", [P, TILES])

        ps = ctx.enter_context(nc.psum_tensor("ps", [P, 8, 512], F32))
        S_BANK = (0, 2)
        M_BANK = (4, 5)
        O_BANK = (6, 7)

        names = ("ld_x0 ld_x1 ld_ident stack0_ld ld_w ld_small idents stack_zero xT_ps xT_sb lam_ps lam_e lam_v lam_done dve_c proj_ps q32 parts parts_out0 parts_out1 "
                 "vps v_sb v_free stack_ld vst qk_done exp_done mx_done mx_read shift16_done "
                 "shiftT_ps shiftT_sb aug_ld pv_done o_raw_done oT_ps o_read gn_T gn_st gn_mm gn_mmr gn_pow gn_norm "
                 "y_ps y_ln y_read ln_pow x1_done outd fl_free part_free proj_free").split()
        z = {n: sem("s_" + n) for n in names}
        block = ctx.enter_context(nc.Block())
        NB = B * 2 * 2

        @block.sync
        def _(sp):
            for b in range(B):
                sp.dma_start(x_in[:, b * TILES:(b + 1) * TILES, :],
                             t["L0_attn_x"][b].rearrange("(t p) d -> p t d", p=P)).then_inc(z[f"ld_x{b}"], 16)
                if b == 0:
                    sp.dma_start(ident[:], t["ident"][:]).then_inc(z["ld_ident"], 16)
                    for n, w in enumerate(("Wq", "Wk", "Wv", "Wo")):
                        sp.dma_start(w_attn[:, n, :], t["L0_attn_" + w][:]).then_inc(z["ld_w"], 16)
            def stack(i, b, g):
                for s_ in range(len(PARTS_Q)):
                    for c in range(2):
                        src = qk_parts[0, PARTS_Q[s_], 32 * g:32 * g + 32, b * S + 512 * c:b * S + 512 * c + 512]
                        sp.dma_start(q_stack[8 * s_:8 * s_ + 8, 2 * i + c, :, :],
                                     src.rearrange("(j d) n -> d j n", d=DH)).then_inc(z["stack0_ld" if i == 0 else "stack_ld"], 16)
                    src = qk_parts[1, PARTS_K[s_], 32 * g:32 * g + 32, b * S:(b + 1) * S]
                    sp.dma_start(k_stack[8 * s_:8 * s_ + 8, i, :, :],
                                 src.rearrange("(j d) n -> d j n", d=DH)).then_inc(z["stack0_ld" if i == 0 else "stack_ld"], 16)

            for b in range(B):
                for c in range(2):
                    for side in range(2):
                        n = (b * 2 + c) * 2 + side
                        sp.wait_ge(z["parts"], n + 1)
                        sp.dma_start(qk_parts[side, :, :, b * S + c * 512:b * S + c * 512 + 512].rearrange("a p n -> p a n"),
                                     part[:, n % 2, :, :]).then_inc(z[f"parts_out{n % 2}"], 16)
                if b == 0:
                    for k in range(2):
                        sp.wait_ge(z[f"parts_out{k}"], 16 * 2)
                    sp.wait_ge(z["stack_zero"], 2)
                    sp.dma_start(k_stack[SHIFT_ROW:SHIFT_ROW + 2, :, :, :].rearrange("p a j n -> p (a j n)").bitcast(F32), t["ones16"][:]).then_inc(z["stack0_ld"], 16)
                    stack(0, 0, 0)
                    stack(1, 0, 1)
            for k in range(2):
                sp.wait_ge(z[f"parts_out{k}"], 16 * NB // 2)
            for i in range(2, GROUPS):
                sp.wait_ge(z["stack_zero"], 2)
                stack(i, i // 4, i % 4)

        @block.gpsimd
        def _(g):
            g.memset(k_stack[:].rearrange("p a j n -> p (a j n)").bitcast(F32), 0.0).then_inc(z["stack_zero"], 1)
            g.memset(v_stage[:], 0.0).then_inc(z["vst"], 1)
            g.wait_ge(z["vst"], 1)
            g.memset(v_stage[:, :, :, 8:9], 1.0).then_inc(z["vst"], 1)
            g.memset(eps_t[:], EPS).then_inc(z["vst"], 1)
            g.memset(half_t[:], -0.5).then_inc(z["vst"], 1)

            def refresh(i, kt):
                src = v_all[:, kt, i, :] if isinstance(i, int) else v_all[:, kt, ds(i, 1), :].rearrange("p a n -> p (a n)")
                g.tensor_copy(v_stage[:, kt, :, 0:DH], src.rearrange("p (j d) -> p j d", d=DH)).then_inc(z["vst"], 1)

            g.wait_ge(z["v_sb"], B * TILES // 4)
            for kt in range(TILES):
                refresh(0, kt)

            def body(i):
                for kt in range(TILES):
                    g.wait_ge(z["pv_done"], i * STEPS + TILES + kt + 1)
                    refresh(i + 1, kt)

            body(0)
            with g.Fori(1, GROUPS - 1) as i:
                body(i)
            for b in range(B):
                g.wait_ge(z["gn_st"], 4 * b + 4)
                g.tensor_tensor(st[:, 8:9], st[:, 7:8], half_t[:, 0:1], ALU.pow).then_inc(z["gn_pow"], 1)
                g.wait_ge(z["y_ln"], b + 1)
                g.tensor_tensor(rstd[:], mv[:, :, 1], half_t[:], ALU.pow).then_inc(z["ln_pow"], 1)

        @block.scalar
        def _(act):
            for n, w in enumerate(("bq", "bk", "lq1", "lk1", "lq2", "lk2", "gn_w", "gn_b")):
                a = t["L0_attn_" + w]
                src = a.rearrange("(p a) -> p a", a=1) if len(a.shape) == 1 else a.rearrange("h (d a) -> (h d) a", a=1)
                act.dma_start(cols[:, n:n + 1], src).then_inc(z["ld_small"], 16)
            act.dma_start(rows[:, 0, :], t["L0_attn_bv"].rearrange("(a n) -> a n", a=1)).then_inc(z["ld_small"], 16)
            act.dma_start(rows[:, 1, :], t["L0_attn_bo"].rearrange("(a n) -> a n", a=1)).then_inc(z["ld_small"], 16)
            act.dma_start(head_mean[:], t["head_mean"][:]).then_inc(z["ld_small"], 16)
            act.wait_ge(z["lam_ps"], 1)
            nc.scalar.activation(lam[:, 2:4], ps[:, 7, 0:2], ACT.Exp, scale=float(DH)).then_inc(z["lam_e"], 1)
            for b in range(B):
                for c in range(2):
                    act.wait_ge(z["xT_ps"], b * 2 + c + 1)
                    nc.scalar.copy(xT[:, b * S + c * 512:b * S + (c + 1) * 512], ps[:, c, :]).then_inc(z["xT_sb"], 1)
            act.wait_ge(z["lam_done"], 1)
            for n in range(NB):
                side = n % 2
                act.wait_ge(z["proj_ps"], n + 1)
                if n >= 2:
                    act.wait_ge(z["fl_free"], n - 1)
                if side == 0:
                    nc.scalar.activation(fl[:, n % 2, :], ps[:, 2 + n % 2, :], ACT.Identity, bias=lam[:, 6:7], scale=lam[:, 5:6]).then_inc(z["q32"], 1)
                else:
                    nc.scalar.activation(fl[:, n % 2, :], ps[:, 2 + n % 2, :], ACT.Identity, bias=cols[:, 1:2]).then_inc(z["q32"], 1)
            for m in range(B * TILES // 4):
                act.wait_ge(z["vps"], m + 1)
                nc.scalar.copy(v_all[:, 4 * (m % 2):4 * (m % 2) + 4, 4 * (m // 2):4 * (m // 2) + 4, :],
                               ps[:, m % 2, :].rearrange("p (t g n) -> p t g n", t=4, g=4)).then_inc(z["v_sb"], 1)

            def shifts(i, qc):
                h = 2 * i + qc
                act.wait_ge(z["shiftT_ps"], h + 1)
                if not isinstance(h, int) or h >= 1:
                    act.wait_ge(z["aug_ld"], 32 * h)
                b = O_BANK[qc]
                nc.scalar.copy(shiftT[:], ps[0:32, b, 0:64].bitcast(BF16)).then_inc(z["shiftT_sb"], 1)
                act.wait_ge(z["shiftT_sb"], h + 1)
                for w in range(2):
                    dst = q_stack[SHIFT_ROW + w:SHIFT_ROW + w + 1, ds(2 * i + qc, 1), :, :].rearrange("p a j n -> p (a j n)")
                    act.dma_start(dst, shiftT[16 * w:16 * w + 16, :]).then_inc(z["aug_ld"], 16)

            def raw(i, qc):
                h = 2 * i + qc
                act.wait_ge(z["pv_done"], TILES * (h + 1))
                if not isinstance(h, int) or h >= 1:
                    act.wait_ge(z["oT_ps"], h)
                nc.scalar.copy(o_raw[:], ps[:, O_BANK[qc], :]).then_inc(z["o_raw_done"], 1)

            def body(i, first, last):
                for s_ in range(STEPS):
                    qc, kt = divmod(s_, TILES)
                    gs = i * STEPS + s_
                    for p in range(2):
                        act.wait_ge(z["qk_done"], 2 * gs + p + 1)
                        if not (first and s_ < 2):
                            act.wait_ge(z["pv_done"], gs - 1)
                        nc.scalar.activation(e_ring[:, 2 * (s_ % 2) + p, :, :], ps[:, S_BANK[p]:S_BANK[p] + 2, :], ACT.Exp).then_inc(z["exp_done"], 1)
                    if kt == 1 and not (first and qc == 0):
                        raw(*((i, 0) if qc else (i - 1, 1)))
                    if kt == 5:
                        if qc == 0:
                            shifts(i, 1)
                        elif not last:
                            shifts(i + 1, 0)

            shifts(0, 0)
            body(0, True, False)
            with act.Fori(1, GROUPS - 1) as i:
                body(i, False, False)
            body(GROUPS - 1, False, True)
            raw(GROUPS - 1, 1)
            for b in range(B):
                act.wait_ge(z["gn_norm"], b + 1)
                for c in range(2):
                    nc.scalar.activation(normT[:, c * 512:(c + 1) * 512], ps[:, c, :], ACT.Identity, bias=st[:, 10:11], scale=st[:, 9:10]).then_inc(z["gn_mmr"], 1)

        @block.vector
        def _(v):
            cnt = [0]

            def chain(ins):
                cnt[0] += 1
                ins.then_inc(z["dve_c"], 1)
                v.wait_ge(z["dve_c"], cnt[0])

            v.memset(ones_row[:], 1.0).then_inc(z["idents"], 1)
            v.memset(q_stack[:].rearrange("p a j n -> p (a j n)").bitcast(F32), 0.0).then_inc(z["stack_zero"], 1)
            v.wait_ge(z["ld_small"], 16 * 11)
            v.tensor_tensor(lam[:, 0:1], cols[:, 2:3], cols[:, 3:4], ALU.mult).then_inc(z["lam_v"], 1)
            v.tensor_tensor(lam[:, 1:2], cols[:, 4:5], cols[:, 5:6], ALU.mult).then_inc(z["lam_v"], 1)
            v.wait_ge(z["ld_ident"], 16)
            v.tensor_copy(ident16[:], ident[:]).then_inc(z["idents"], 1)
            v.wait_ge(z["lam_e"], 1)
            chain(v.tensor_tensor(lam[:, 4:5], lam[:, 2:3], lam[:, 3:4], ALU.subtract))
            chain(v.tensor_scalar(lam[:, 5:6], lam[:, 4:5], LAMBDA_INIT, DH ** -0.5, ALU.add, ALU.mult))
            v.tensor_tensor(lam[:, 6:7], cols[:, 0:1], lam[:, 5:6], ALU.mult).then_inc(z["lam_done"], 1)
            for n in range(NB):
                v.wait_ge(z["q32"], n + 1)
                if n >= 2:
                    v.wait_ge(z[f"parts_out{n % 2}"], 16 * (n // 2))
                f = fl[:, n % 2, :]
                chain(v.tensor_copy(part[:, n % 2, 0, :], f))
                chain(v.tensor_tensor(f, f, part[:, n % 2, 0, :], ALU.subtract))
                chain(v.tensor_copy(part[:, n % 2, 1, :], f))
                last = v.tensor_tensor(part[:, n % 2, 2, :], f, part[:, n % 2, 1, :], ALU.subtract)
                last.then_inc(z["parts"], 1)
                v.wait_ge(z["parts"], n + 1)
                v.tensor_copy(st[:, 15:16], lam[:, 5:6]).then_inc(z["fl_free"], 1)

            def reduce(h, u):
                j, r = divmod(u, 8)
                q, c = divmod(r, 2)
                v.wait_ge(z["mx_done"], 32 * h + u + 1)
                v.tensor_reduce(max_parts[:, 0, j, q, c:c + 1], ps[:, M_BANK[u % 2], :], AX.X, ALU.max).then_inc(z["mx_read"], 1)

            def final(h, first):
                v.wait_ge(z["mx_read"], 32 * h + 32)
                if not first:
                    v.wait_ge(z["shiftT_ps"], h)
                v.tensor_reduce(shift[:], max_parts[:, 0, :, :, :], AX.X, ALU.max, negate=True).then_inc(z["shift16_done"], 1)
                v.wait_ge(z["shift16_done"], 4 * h + 1)
                v.tensor_copy(shift16[:, 0, :, :], shift[:]).then_inc(z["shift16_done"], 1)
                v.wait_ge(z["shift16_done"], 4 * h + 2)
                v.tensor_tensor(shift_rest[:], shift[:], shift16[:, 0, :, :], ALU.subtract).then_inc(z["shift16_done"], 1)
                v.wait_ge(z["shift16_done"], 4 * h + 3)
                v.tensor_copy(shift16[:, 1, :, :], shift_rest[:]).then_inc(z["shift16_done"], 1)

            def normalise(i, qc):
                h = 2 * i + qc
                v.wait_ge(z["oT_ps"], h + 1)
                src = ps[:, O_BANK[qc], :].rearrange("p (t j c) -> p t j c", t=4, j=HG)
                v.reciprocal(o_inv[:], src[:, :, :, DH]).then_inc(z["o_read"], 1)
                v.wait_ge(z["o_read"], 2 * h + 1)
                dst = o_all[:, 4 * qc:4 * qc + 4, i, :] if isinstance(i, int) else o_all[:, 4 * qc:4 * qc + 4, ds(i, 1), :].rearrange("p t a n -> p (t a) n")
                v.tensor_tensor(dst.rearrange("p t (j d) -> p t j d", j=HG), src[:, :, :, 0:DH],
                                o_inv[:].unsqueeze(3).broadcast_to([P, 4, HG, DH]), ALU.mult).then_inc(z["o_read"], 1)

            def body(i, first, last):
                for s_ in range(STEPS):
                    qc, kt = divmod(s_, TILES)
                    if not last:
                        for u in range(4 * kt, 4 * kt + 4):
                            reduce(2 * i + 2 + qc, u)
                    if kt == 3 and not (first and qc == 0):
                        normalise(*((i, 0) if qc else (i - 1, 1)))
                    if not last and kt == TILES - 1:
                        final(2 * i + 2 + qc, False)

            for qc in range(2):
                for u in range(32):
                    reduce(qc, u)
                final(qc, qc == 0)
            body(0, True, False)
            with v.Fori(1, GROUPS - 1) as i:
                body(i, False, False)
            body(GROUPS - 1, False, True)
            normalise(GROUPS - 1, 1)
            for b in range(B):
                v.wait_ge(z["gn_T"], b + 1)
                for c in range(2):
                    v.bn_stats(bn[:, c, :], ps[:, c, :]).then_inc(z["dve_c"], 1)
                cnt[0] += 2
                v.wait_ge(z["dve_c"], cnt[0])
                v.bn_aggr(st[:, 0:2], bn[:].rearrange("p a n -> p (a n)")).then_inc(z["gn_st"], 1)
                v.wait_ge(z["gn_mm"], 2 * b + 1)
                chain(v.tensor_copy(st[:, 2:3], ps[:, 2, 0:1]))
                chain(v.tensor_tensor(st[:, 3:4], st[:, 0:1], st[:, 2:3], ALU.subtract))
                v.scalar_tensor_tensor(st[:, 4:5], st[:, 3:4], st[:, 3:4], st[:, 1:2], ALU.mult, ALU.add).then_inc(z["gn_st"], 1)
                v.wait_ge(z["gn_mm"], 2 * b + 2)
                chain(v.tensor_copy(st[:, 5:6], ps[:, 2, 4:5]))
                v.tensor_scalar(st[:, 7:8], st[:, 5:6], EPS, None, ALU.add).then_inc(z["gn_st"], 1)
                v.wait_ge(z["gn_st"], 4 * b + 3)
                v.tensor_copy(st[:, 15:16], st[:, 7:8]).then_inc(z["gn_st"], 1)
                v.wait_ge(z["gn_pow"], b + 1)
                chain(v.tensor_tensor(st[:, 9:10], st[:, 8:9], cols[:, 6:7], ALU.mult))
                chain(v.tensor_tensor(st[:, 11:12], st[:, 2:3], st[:, 9:10], ALU.mult))
                v.tensor_tensor(st[:, 10:11], cols[:, 7:8], st[:, 11:12], ALU.subtract).then_inc(z["gn_norm"], 1)
                for n in range(TILES):
                    v.wait_ge(z["y_ps"], 2 * b + n // 4 + 1)
                    xt = x_in[:, b * TILES + n, :]
                    chain(v.tensor_tensor(xt, xt, ps[:, 3 + n // 4, (n % 4) * P:(n % 4 + 1) * P], ALU.add))
                    chain(v.bn_stats(bnt[:, n, :], xt))
                    chain(v.bn_aggr(mv[:, n, :], bnt[:, n, :]))
                chain(v.tensor_scalar(mv[:, :, 1], mv[:, :, 1], EPS, None, ALU.add))
                v.tensor_copy(st[:, 15:16], mv[:, 0, 1:2]).then_inc(z["y_ln"], 1)
                v.wait_ge(z["ln_pow"], b + 1)
                for n in range(TILES):
                    v.tensor_scalar(x1[:, b * TILES + n, :], x_in[:, b * TILES + n, :], mv[:, n, 0:1], rstd[:, n:n + 1],
                                    ALU.subtract, ALU.mult).then_inc(z["x1_done"], 1)

        @block.tensor
        def _(pe):
            mm = nc.tensor.matmul
            tr = nc.tensor.transpose
            pe.wait_ge(z["ld_small"], 16 * 11)
            pe.wait_ge(z["lam_v"], 2)
            mm(ps[:, 7, 0:2], head_mean[:], lam[:, 0:2], start=True, stop=True).then_inc(z["lam_ps"], 1)
            pe.wait_ge(z["ld_w"], 16 * 4)
            pe.wait_ge(z["ld_ident"], 16)
            for b in range(B):
                pe.wait_ge(z[f"ld_x{b}"], 16)
                for c in range(2):
                    if b:
                        pe.wait_ge(z["xT_sb"], c + 1)
                    for n in range(4):
                        m = tr(ps[:, c, n * P:(n + 1) * P], x_in[:, b * TILES + 4 * c + n, :], ident[:])
                    m.then_inc(z["xT_ps"], 1)
            for n in range(NB):
                c = n // 2
                pe.wait_ge(z["xT_sb"], c + 1)
                if n >= 2:
                    pe.wait_ge(z["q32"], n - 1)
                mm(ps[:, 2 + n % 2, :], w_attn[:, n % 2, :], xT[:, c * 512:(c + 1) * 512], start=True, stop=True).then_inc(z["proj_ps"], 1)
            pe.wait_ge(z["idents"], 2)
            for m_ in range(B * TILES // 4):
                if m_ < 2:
                    pe.wait_ge(z["xT_sb"], 4)
                else:
                    pe.wait_ge(z["v_sb"], m_ - 1)
                for n in range(4):
                    o = ps[:, m_ % 2, n * P:(n + 1) * P]
                    mm(o, xT[:, (4 * m_ + n) * P:(4 * m_ + n + 1) * P], w_attn[:, 2, :], start=True, stop=False)
                    m = mm(o, ones_row[:], rows[:, 0, :], start=False, stop=True)
                m.then_inc(z["vps"], 1)

            def ks(i, j, a, n):
                return k_stack[:, ds(i, 1), j, a:a + n].rearrange("p a n -> p (a n)")

            def qs(i, qc, j, a, n):
                return q_stack[:, ds(2 * i + qc, 1), j, a:a + n].rearrange("p a n -> p (a n)")

            def max_units(h, i, qc, us):
                for u in us:
                    j, r = divmod(u, 8)
                    q, c = divmod(r, 2)
                    if not isinstance(h, int) or 32 * h + u >= 2:
                        pe.wait_ge(z["mx_read"], 32 * h + u - 1)
                    mm(ps[:, M_BANK[u % 2], :], qs(i, qc, j, q * P, P), ks(i, j, c * 512, 512),
                       start=True, stop=True).then_inc(z["mx_done"], 1)

            def shifts(h, qc):
                pe.wait_ge(z["shift16_done"], 4 * h + 4)
                b = O_BANK[1 - qc]
                tr(ps[0:32, b, 0:64].bitcast(BF16), shift16[:].rearrange("p w j t -> p (w j t)"), ident16[:]).then_inc(z["shiftT_ps"], 1)

            def pv(i, s_, first, last=False):
                qc, kt = divmod(s_, TILES)
                gs = i * STEPS + s_
                pe.wait_ge(z["exp_done"], 2 * gs + 2)
                pe.wait_ge(z["vst"], 4 + (i * TILES if not first else 0) + kt + 1)
                for j in range(HG):
                    m = mm(ps[32 * j:32 * j + 32, O_BANK[qc], :], v_stage[:, kt, j, :], e_ring[:, 2 * (s_ % 2) + j // 2, j % 2, :],
                           start=(kt == 0), stop=(kt == TILES - 1))
                m.then_inc(z["pv_done"], 1)

            def o_turn(i, qc):
                h = 2 * i + qc
                pe.wait_ge(z["o_raw_done"], h + 1)
                for n in range(4):
                    m = tr(ps[:, O_BANK[qc], n * P:(n + 1) * P], o_raw[:, n * P:(n + 1) * P], ident[:])
                m.then_inc(z["oT_ps"], 1)

            def body(i, first, last):
                for s_ in range(STEPS):
                    qc, kt = divmod(s_, TILES)
                    gs = i * STEPS + s_
                    h = 2 * i + qc
                    if kt == 0:
                        pe.wait_ge(z["aug_ld"], 32 * h + 32)
                        if not (first and qc == 0):
                            pass
                    for p in range(2):
                        if not (first and s_ == 0):
                            pe.wait_ge(z["exp_done"], 2 * gs + p - 1)
                        for j in range(2):
                            m = mm(ps[:, S_BANK[p] + j, :], ks(i, 2 * p + j, kt * P, P), qs(i, qc, 2 * p + j, 0, 512),
                                   start=True, stop=True)
                        m.then_inc(z["qk_done"], 1)
                        if not last:
                            max_units(h + 2, i + 1, qc, range(4 * kt + 2 * p, 4 * kt + 2 * p + 2))
                    if s_ == 0:
                        if not first:
                            pv(i - 1, STEPS - 1, False)
                    else:
                        if kt == 1:
                            pe.wait_ge(z["shiftT_sb"], h + 1)
                        pv(i, s_ - 1, first)
                    if kt == 2 and not (first and qc == 0):
                        o_turn(*((i, 0) if qc else (i - 1, 1)))
                    if kt == 5:
                        if not (first and qc == 0):
                            pe.wait_ge(z["o_read"], 2 * h)
                        if qc == 0:
                            shifts(h + 1, 0)
                        elif not last:
                            shifts(h + 1, 1)

            pe.wait_ge(z["q32"], NB)
            pe.wait_ge(z["v_sb"], B * TILES // 4)
            pe.wait_ge(z["stack0_ld"], 16 * 19)
            max_units(0, 0, 0, range(32))
            pe.wait_ge(z["shift16_done"], 4)
            tr(ps[0:32, O_BANK[0], 0:64].bitcast(BF16), shift16[:].rearrange("p w j t -> p (w j t)"), ident16[:]).then_inc(z["shiftT_ps"], 1)
            max_units(1, 0, 1, range(32))
            pe.wait_ge(z["stack_ld"], 16 * 18 * (GROUPS - 1))
            body(0, True, False)
            with pe.Fori(1, GROUPS - 1) as i:
                body(i, False, False)
            body(GROUPS - 1, False, True)
            pv(GROUPS - 1, STEPS - 1, False)
            o_turn(GROUPS - 1, 1)
            for b in range(B):
                pe.wait_ge(z["o_read"], 4 * GROUPS)
                pe.wait_ge(z["exp_done"], 2 * STEPS * GROUPS)
                if b:
                    pe.wait_ge(z["gn_mmr"], 2 * b)
                for n in range(TILES):
                    m = tr(ps[:, n // 4, (n % 4) * P:(n % 4 + 1) * P], o_all[:, n, 4 * b:4 * b + 4, :].rearrange("p g n -> p (g n)"), ident[:])
                m.then_inc(z["gn_T"], 1)
                pe.wait_ge(z["gn_st"], 4 * b + 1)
                mm(ps[:, 2, 0:1], head_mean[:], st[:, 0:1], start=True, stop=True).then_inc(z["gn_mm"], 1)
                pe.wait_ge(z["gn_st"], 4 * b + 2)
                mm(ps[:, 2, 4:5], head_mean[:], st[:, 4:5], start=True, stop=True).then_inc(z["gn_mm"], 1)
                pe.wait_ge(z["gn_mmr"], 2 * b + 2)
                if b:
                    pe.wait_ge(z["y_ln"], b)
                for n in range(TILES):
                    o = ps[:, 3 + n // 4, (n % 4) * P:(n % 4 + 1) * P]
                    mm(o, normT[:, n * P:(n + 1) * P], w_attn[:, 3, :], start=True, stop=False)
                    m = mm(o, ones_row[:], rows[:, 1, :], start=False, stop=True)
                    if n % 4 == 3:
                        m.then_inc(z["y_ps"], 1)


FH, KV, FDH = 16, 4, 64
QKV = (FH + 2 * KV) * FDH
WINDOW = 128
NT = B * TILES
BATCHES = 4
MASKED = -1e30


def window_attention(nc, t, x1, x2, ident, ident16, ones_row):
    with ExitStack() as ctx:
        def sb(name, shape, dt=F32):
            return ctx.enter_context(nc.sbuf_tensor(name, shape, dt))

        w_qkv = sb("w_qkv", [P, QKV])
        b_qkv = sb("b_qkv", [1, QKV])
        w_proj = sb("w_proj", [P, 8, D])
        b_proj = sb("b_proj", [1, D])
        norm_w = sb("norm_w", [P, 1])
        sink = sb("sink", [P, FH])
        nsink = sb("nsink", [P, FH])
        rope_c = sb("rope_c", [P, TILES, FDH])
        rope_s = sb("rope_s", [P, TILES, FDH])
        mask = sb("mask", [P, TILES, 512], BF16)
        mask32 = sb("mask32", [P, 2, 512])
        sq = sb("sq", [P, D])
        rms = sb("rms", [P, NT])
        rms_in = sb("rms_in", [P, NT])
        neg_half = sb("neg_half", [P, NT])
        h_cur = sb("h_cur", [P, D])
        hT = sb("hT", [P, P])
        rot_a = sb("rot_a", [P, 2, 512])
        rot_b = sb("rot_b", [P, 2, 512])
        q_rot = sb("q_rot", [P, FH * FDH])
        k_pad = sb("k_pad", [P, KV, 2, P])
        qT = sb("qT", [P, 8, P])
        kT = sb("kT", [P, 2 * KV, (NT + 1) * P])
        v_win = sb("v_win", [P, NT + 1, KV * FDH])
        neg_max = sb("neg_max", [P, 4])
        bias = sb("bias", [P, 4, 4])
        sums = sb("sums", [P, 4, 4])
        sink_in = sb("sink_in", [P, 8])
        sink_e = sb("sink_e", [P, 8])
        den = sb("den", [P, 8])
        inv = sb("inv", [P, 8])
        probs = sb("probs", [P, 2, 4, 256])
        pT = sb("pT", [P, 2, 512])
        y_sb = sb("y_sb", [P, FH * FDH])
        yT = sb("yT", [P, 8, P])
        ps = ctx.enter_context(nc.psum_tensor("ps_w", [P, 8, 512], F32))
        Y_BANK, WORK = 6, 7

        names = ("ld act_ld init rms_in rms h_done hT_ps hT_sb qkv_ps rope_a rope_read rot v_sb qT_ps qT_sb kT_ps kT_sb "
                 "s_ps negmax bias exp sink_in sink_e den inv pT_ps pT_dve pT_act pv y_norm yT_ps yT_sb proj_ps x2 sq").split()
        z = {n: ctx.enter_context(nc.semaphore("w_" + n)) for n in names}
        block = ctx.enter_context(nc.Block())

        @block.sync
        def _(sp):
            sp.dma_start(w_qkv[:], t["L0_ffn_qkv_w"][:]).then_inc(z["ld"], 16)
            sp.dma_start(b_qkv[:], t["L0_ffn_qkv_b"].rearrange("(a n) -> a n", a=1)).then_inc(z["ld"], 16)
            sp.dma_start(norm_w[:], t["L0_ffn_attn_norm_w"].rearrange("(p a) -> p a", a=1)).then_inc(z["ld"], 16)
            sp.dma_start(rope_c[:], t["rope_c"][:]).then_inc(z["ld"], 16)
            sp.dma_start(rope_s[:], t["rope_s"][:]).then_inc(z["ld"], 16)
            sp.dma_start(mask32[:], t["mask"][:]).then_inc(z["ld"], 16)
            sp.dma_start(w_proj[:], t["L0_ffn_proj_w"].rearrange("(c p) n -> p c n", p=P)).then_inc(z["ld"], 16)
            sp.dma_start(b_proj[:], t["L0_ffn_proj_b"].rearrange("(a n) -> a n", a=1)).then_inc(z["ld"], 16)
            sp.dma_start(sink[:], t["L0_ffn_attn_sink"].rearrange("(a n) -> a n", a=1).broadcast_to([P, FH])).then_inc(z["ld"], 16)

        @block.gpsimd
        def _(g):
            g.memset(neg_half[:], -0.5).then_inc(z["init"], 1)
            g.memset(k_pad[:], 0.0).then_inc(z["init"], 1)
            g.memset(kT[:, :, 0:P], 0.0).then_inc(z["init"], 1)
            g.memset(v_win[:, 0, :], 0.0).then_inc(z["init"], 1)
            g.wait_ge(z["ld"], 16 * 9)
            g.tensor_scalar(nsink[:], sink[:], -1.0, None, ALU.mult).then_inc(z["init"], 1)
            g.tensor_copy(mask[:, 0, :], mask32[:, 0, :]).then_inc(z["init"], 1)
            g.tensor_copy(mask[:, 1:TILES, :], mask32[:, 1:2, :].broadcast_to([P, TILES - 1, 512])).then_inc(z["init"], 1)
            g.wait_ge(z["rms_in"], 1)
            g.wait_ge(z["init"], 7)
            g.tensor_tensor(rms[:], rms_in[:], neg_half[:], ALU.pow).then_inc(z["rms"], 1)

            def rotate(tile, c):
                g.wait_ge(z["rope_read"], 3 * tile + c + 1)
                a = c % 2
                if c < 2:
                    g.tensor_tensor(q_rot[:, 512 * c:512 * c + 512], rot_a[:, a, :], rot_b[:, a, :], ALU.add).then_inc(z["rot"], 1)
                else:
                    for e in range(2):
                        g.tensor_tensor(k_pad[:, :, e, FDH * e:FDH * e + FDH], rot_a[:, a, 0:256].rearrange("p (g d) -> p g d", g=KV),
                                        rot_b[:, a, 0:256].rearrange("p (g d) -> p g d", g=KV), ALU.add).then_inc(z["rot"], 1)

            def sinks(tile, hf, first):
                g.wait_ge(z["bias"], 4 * tile + 2 * hf + 2)
                g.tensor_tensor(sink_in[:], bias[:, 2 * hf:2 * hf + 2, :].rearrange("p a n -> p (a n)"), sink[:, 8 * hf:8 * hf + 8], ALU.add).then_inc(z["sink_in"], 1)
                g.wait_ge(z["sink_e"], 2 * tile + hf + 1)
                if not (first and hf == 0):
                    g.wait_ge(z["inv"], 2 * tile + hf)
                g.tensor_tensor(den[:], sink_e[:], sums[:, 2 * hf:2 * hf + 2, :].rearrange("p a n -> p (a n)"), ALU.add).then_inc(z["den"], 1)

            def prep(tile):
                for c in range(3):
                    rotate(tile, c)

            def body(tile, first, last):
                if not last:
                    rotate(tile + 1, 0)
                    rotate(tile + 1, 1)
                    rotate(tile + 1, 2)
                sinks(tile, 0, first)
                sinks(tile, 1, first)

            prep(0)
            body(0, True, False)
            with g.Fori(1, NT - 1) as tile:
                body(tile, False, False)
            body(NT - 1, False, True)

        @block.scalar
        def _(act):
            def hT_copy(tile):
                act.wait_ge(z["hT_ps"], tile + 1)
                nc.scalar.activation(hT[:], ps[:, WORK, 0:P], ACT.Copy, scale=norm_w[:, 0:1]).then_inc(z["hT_sb"], 1)

            def v_copy(tile):
                act.wait_ge(z["rope_read"], 3 * tile + 3)
                act.wait_ge(z["init"], 7)
                nc.scalar.copy(v_win[:, ds(tile + 1, 1), :].rearrange("p a n -> p (a n)"), ps[:, WORK, 256:512]).then_inc(z["v_sb"], 1)

            def qT_copy(tile, c):
                act.wait_ge(z["qT_ps"], 2 * tile + c + 1)
                nc.scalar.copy(qT[:, 4 * c:4 * c + 4, :].rearrange("p a n -> p (a n)"), ps[:, WORK, :]).then_inc(z["qT_sb"], 1)

            def kT_copy(tile, c):
                act.wait_ge(z["kT_ps"], 2 * tile + c + 1)
                nc.scalar.copy(kT[:, 4 * c:4 * c + 4, ds(tile * P + P, P)], ps[:, WORK, :].rearrange("p (a n) -> p a n", a=4)).then_inc(z["kT_sb"], 1)

            def exps(tile, k, js):
                kb = 4 * tile + k
                act.wait_ge(z["bias"], kb + 1)
                for j in js:
                    nc.scalar.activation(probs[:, k % 2, j, :], ps[:, 2 * (k % 2) + j // 2, 256 * (j % 2):256 * (j % 2) + 256], ACT.Exp,
                                         bias=bias[:, k, j:j + 1], scale=FDH ** -0.5, accum_out=sums[:, k, j:j + 1]).then_inc(z["exp"], 1)

            def pT_copy(tile, k):
                kb = 4 * tile + k
                act.wait_ge(z["pT_ps"], 2 * kb + 2)
                if not isinstance(kb, int) or kb:
                    act.wait_ge(z["pv"], 2 * kb)
                nc.scalar.copy(pT[:, 1, :], ps[:, 5, :]).then_inc(z["pT_act"], 1)

            def sinks(tile, hf):
                act.wait_ge(z["sink_in"], 2 * tile + hf + 1)
                nc.scalar.activation(sink_e[:], sink_in[:], ACT.Exp).then_inc(z["sink_e"], 1)

            def yT_copy(tile, c):
                act.wait_ge(z["yT_ps"], 2 * tile + c + 1)
                nc.scalar.copy(yT[:, 4 * c:4 * c + 4, :].rearrange("p a n -> p (a n)"), ps[:, WORK, :]).then_inc(z["yT_sb"], 1)

            def body(tile, first, last):
                def slot(k):
                    kb = 4 * tile + k
                    if not (first and k < 2):
                        act.wait_ge(z["pT_ps"], 2 * kb - 2)
                    if not first:
                        act.wait_ge(z["den"], 2 * tile + k // 2 - 1)
                slot(0)
                exps(tile, 0, (0, 1))
                if not last:
                    hT_copy(tile + 1)
                exps(tile, 0, (2, 3))
                pT_copy(tile, 0)
                if not first:
                    yT_copy(tile - 1, 0)
                    yT_copy(tile - 1, 1)
                slot(1)
                exps(tile, 1, range(4))
                if not last:
                    v_copy(tile + 1)
                pT_copy(tile, 1)
                sinks(tile, 0)
                slot(2)
                exps(tile, 2, range(4))
                if not last:
                    qT_copy(tile + 1, 0)
                pT_copy(tile, 2)
                if not last:
                    qT_copy(tile + 1, 1)
                    kT_copy(tile + 1, 0)
                    kT_copy(tile + 1, 1)
                slot(3)
                exps(tile, 3, range(4))
                pT_copy(tile, 3)
                sinks(tile, 1)

            act.wait_ge(z["ld"], 16 * 9)
            hT_copy(0)
            v_copy(0)
            for c in range(2):
                qT_copy(0, c)
            for c in range(2):
                kT_copy(0, c)
            body(0, True, False)
            with act.Fori(1, NT - 1) as tile:
                body(tile, False, False)
            body(NT - 1, False, True)
            for c in range(2):
                yT_copy(NT - 1, c)

        @block.vector
        def _(v):
            for n in range(NT):
                if n:
                    v.wait_ge(z["sq"], n)
                v.tensor_tensor_reduce(out=sq[:], in0=x1[:, n, :], in1=x1[:, n, :], scale=1.0, scalar=0.0, op0=ALU.mult, op1=ALU.add,
                                       accum_out=rms_in[:, n:n + 1]).then_inc(z["sq"], 1)
            v.wait_ge(z["sq"], NT)
            v.tensor_scalar(rms_in[:], rms_in[:], 1.0 / D, EPS, ALU.mult, ALU.add).then_inc(z["rms_in"], 1)
            v.wait_ge(z["rms"], 1)
            v.wait_ge(z["ld"], 16 * 9)

            def h_of(tile, first=False):
                if not first:
                    v.wait_ge(z["hT_ps"], tile)
                v.tensor_scalar(h_cur[:], x1[:, ds(tile, 1), :].rearrange("p a n -> p (a n)"), rms[:, ds(tile, 1)], None, ALU.mult).then_inc(z["h_done"], 1)

            def rope(tile, c, first=False):
                v.wait_ge(z["qkv_ps"], 3 * tile + c + 1)
                n = 512 if c < 2 else 256
                hs = n // FDH
                if not (first and c < 2):
                    v.wait_ge(z["rot"], (4 * tile, 4 * tile - 2, 4 * tile + 1)[c])
                tl = tile % TILES
                src = ps[:, WORK, 0:n].rearrange("p (h d) -> p h d", h=hs)
                ct = rope_c[:, ds(tl, 1), :].broadcast_to([P, hs, FDH])
                st = rope_s[:, ds(tl, 1), :].broadcast_to([P, hs, FDH])
                v.tensor_tensor(rot_a[:, c % 2, 0:n].rearrange("p (h d) -> p h d", h=hs), src, ct, ALU.mult).then_inc(z["rope_a"], 1)
                src = ps[:, WORK, 0:n].rearrange("p (h d e) -> p h d e", h=hs, e=2)
                dst = rot_b[:, c % 2, 0:n].rearrange("p (h d e) -> p h d e", h=hs, e=2)
                stp = st.rearrange("p h (d e) -> p h d e", e=2)
                v.tensor_tensor(dst[:, :, :, 0], src[:, :, :, 1], stp[:, :, :, 0], ALU.mult).then_inc(z["rope_a"], 1)
                v.tensor_tensor(dst[:, :, :, 1], src[:, :, :, 0], stp[:, :, :, 1], ALU.mult).then_inc(z["rope_read"], 1)

            def maxima(tile, k, first=False):
                kb = 4 * tile + k
                v.wait_ge(z["s_ps"], kb + 1)
                if not isinstance(kb, int) or kb:
                    v.wait_ge(z["bias"], kb)
                v.tensor_reduce(neg_max[:], ps[:, 2 * (k % 2):2 * (k % 2) + 2, :].rearrange("p b (e n) -> p (b e) n", e=2), AX.X, ALU.max,
                                negate=True).then_inc(z["negmax"], 1)
                v.wait_ge(z["negmax"], kb + 1)
                if not (first and k < 4):
                    v.wait_ge(z["den"], 2 * (tile - 1) + k // 2 + 1)
                v.scalar_tensor_tensor(bias[:, k, :], neg_max[:], FDH ** -0.5, nsink[:, 4 * k:4 * k + 4], ALU.mult, ALU.min).then_inc(z["bias"], 1)

            def pT_copy(tile, k):
                kb = 4 * tile + k
                v.wait_ge(z["pT_ps"], 2 * kb + 1)
                if not isinstance(kb, int) or kb:
                    v.wait_ge(z["pv"], 2 * kb - 1)
                v.tensor_copy(pT[:, 0, :], ps[:, 4, :]).then_inc(z["pT_dve"], 1)

            def y_norm(tile, hf):
                v.wait_ge(z["den"], 2 * tile + hf + 1)
                if not isinstance(tile, int) or 2 * tile + hf:
                    v.wait_ge(z["y_norm"], 2 * tile + hf)
                v.reciprocal(inv[:], den[:]).then_inc(z["inv"], 1)
                v.wait_ge(z["inv"], 2 * tile + hf + 1)
                v.wait_ge(z["pv"], 8 * tile + 4 * hf + 4)
                v.tensor_tensor(y_sb[:, 512 * hf:512 * hf + 512].rearrange("p (h d) -> p h d", h=8), ps[:, Y_BANK, :].rearrange("p (h d) -> p h d", h=8),
                                inv[:].unsqueeze(2).broadcast_to([P, 8, FDH]), ALU.mult).then_inc(z["y_norm"], 1)

            def residual(tile):
                v.wait_ge(z["proj_ps"], tile + 1)
                v.tensor_tensor(x2[:, ds(tile, 1), :].rearrange("p a n -> p (a n)"), ps[:, WORK, 0:P],
                                x1[:, ds(tile, 1), :].rearrange("p a n -> p (a n)"), ALU.add).then_inc(z["x2"], 1)

            def body(tile, first, last):
                if not first:
                    y_norm(tile - 1, 1)
                if not last:
                    h_of(tile + 1)
                maxima(tile, 1, first)
                if not last:
                    rope(tile + 1, 0)
                pT_copy(tile, 0)
                maxima(tile, 2, first)
                if not last:
                    rope(tile + 1, 1)
                    rope(tile + 1, 2)
                pT_copy(tile, 1)
                if not first:
                    residual(tile - 1)
                maxima(tile, 3, first)
                y_norm(tile, 0)
                pT_copy(tile, 2)
                if not last:
                    maxima(tile + 1, 0)
                pT_copy(tile, 3)

            h_of(0, True)
            for c in range(3):
                rope(0, c, True)
            maxima(0, 0, True)
            body(0, True, False)
            with v.Fori(1, NT - 1) as tile:
                body(tile, False, False)
            body(NT - 1, False, True)
            y_norm(NT - 1, 1)
            residual(NT - 1)

        @block.tensor
        def _(pe):
            mm = nc.tensor.matmul
            tr = nc.tensor.transpose

            def hT_of(tile):
                pe.wait_ge(z["h_done"], tile + 1)
                tr(ps[:, WORK, 0:P], h_cur[:], ident[:]).then_inc(z["hT_ps"], 1)

            def qkv(tile, c):
                if c == 0:
                    pe.wait_ge(z["hT_sb"], tile + 1)
                mm(ps[:, WORK, :], hT[:], w_qkv[:, 512 * c:512 * c + 512], start=True, stop=False)
                mm(ps[:, WORK, :], ones_row[:], b_qkv[:, 512 * c:512 * c + 512], start=False, stop=True).then_inc(z["qkv_ps"], 1)

            def qT_of(tile, c):
                pe.wait_ge(z["rot"], 4 * tile + 2)
                for n in range(4):
                    m = tr(ps[:, WORK, n * P:(n + 1) * P], q_rot[:, (4 * c + n) * P:(4 * c + n + 1) * P], ident[:])
                m.then_inc(z["qT_ps"], 1)

            def kT_of(tile, c):
                pe.wait_ge(z["rot"], 4 * tile + 4)
                for n in range(4):
                    m = tr(ps[:, WORK, n * P:(n + 1) * P], k_pad[:, 2 * c + n // 2, n % 2, :], ident[:])
                m.then_inc(z["kT_ps"], 1)

            def scores(tile, k, first=False):
                kb = 4 * tile + k
                if not (first and k < 2):
                    pe.wait_ge(z["exp"], 4 * kb - 4)
                pe.wait_ge(z["qT_sb"], 2 * tile + 2)
                pe.wait_ge(z["kT_sb"], 2 * tile + 2)
                for n in range(2):
                    o = ps[:, 2 * (k % 2) + n, :]
                    mm(o, qT[:, 2 * k + n, :], kT[:, 2 * k:2 * k + 2, ds(tile * P, 2 * P)], start=True, stop=False)
                    m = mm(o, ident16[:], mask[:, ds(tile % TILES, 1), :].rearrange("p a n -> p (a n)"), start=False, stop=True)
                m.then_inc(z["s_ps"], 1)

            def turn_probs(tile, k):
                kb = 4 * tile + k
                for c in range(2):
                    pe.wait_ge(z["exp"], 4 * kb + 2 * c + 2)
                    if not isinstance(kb, int) or kb:
                        pe.wait_ge(z["pT_act" if c else "pT_dve"], kb)
                    for n in range(4):
                        m = tr(ps[:, 4 + c, n * P:(n + 1) * P], probs[:, k % 2, 2 * c + n // 2, (n % 2) * P:(n % 2 + 1) * P], ident[:])
                    m.then_inc(z["pT_ps"], 1)

            def pv(tile, k):
                kb = 4 * tile + k
                if k % 2 == 0 and (not isinstance(kb, int) or kb):
                    pe.wait_ge(z["y_norm"], 2 * tile + k // 2)
                for c in range(2):
                    pe.wait_ge(z["pT_act" if c else "pT_dve"], kb + 1)
                    for j in range(2):
                        h = 4 * (k % 2) + 2 * c + j
                        for w in range(2):
                            m = mm(ps[:, Y_BANK, h * FDH:(h + 1) * FDH], pT[:, c, (2 * j + w) * P:(2 * j + w + 1) * P],
                                   v_win[:, ds(tile + w, 1), k * FDH:(k + 1) * FDH].rearrange("p a n -> p (a n)"), start=(w == 0), stop=(w == 1))
                    m.then_inc(z["pv"], 1)

            def yT_of(tile, c):
                pe.wait_ge(z["y_norm"], 2 * tile + 2)
                for n in range(4):
                    m = tr(ps[:, WORK, n * P:(n + 1) * P], y_sb[:, (4 * c + n) * P:(4 * c + n + 1) * P], ident[:])
                m.then_inc(z["yT_ps"], 1)

            def project(tile):
                pe.wait_ge(z["yT_sb"], 2 * tile + 2)
                for c in range(8):
                    mm(ps[:, WORK, 0:P], yT[:, c, :], w_proj[:, c, :], start=(c == 0), stop=False)
                mm(ps[:, WORK, 0:P], ones_row[:], b_proj[:], start=False, stop=True).then_inc(z["proj_ps"], 1)

            def body(tile, first, last):
                scores(tile, 1, first)
                if not last:
                    pe.wait_ge(z["kT_sb"], 2 * tile + 2)
                    hT_of(tile + 1)
                    qkv(tile + 1, 0)
                turn_probs(tile, 0)
                if not first:
                    if not last:
                        pe.wait_ge(z["rope_read"], 3 * tile + 4)
                    yT_of(tile - 1, 0)
                    pe.wait_ge(z["yT_sb"], 2 * tile - 1)
                    yT_of(tile - 1, 1)
                pv(tile, 0)
                scores(tile, 2, first)
                if not last:
                    if first:
                        pe.wait_ge(z["rope_read"], 3 * tile + 4)
                    else:
                        pe.wait_ge(z["yT_sb"], 2 * tile)
                    qkv(tile + 1, 1)
                    pe.wait_ge(z["rope_read"], 3 * tile + 5)
                    qkv(tile + 1, 2)
                turn_probs(tile, 1)
                if not last:
                    pe.wait_ge(z["rope_read"], 3 * tile + 6)
                    pe.wait_ge(z["v_sb"], tile + 2)
                if not first:
                    project(tile - 1)
                pv(tile, 1)
                scores(tile, 3, first)
                if not last:
                    if not first:
                        pe.wait_ge(z["x2"], tile)
                    qT_of(tile + 1, 0)
                turn_probs(tile, 2)
                if not last:
                    pe.wait_ge(z["qT_sb"], 2 * tile + 3)
                    qT_of(tile + 1, 1)
                    pe.wait_ge(z["qT_sb"], 2 * tile + 4)
                    kT_of(tile + 1, 0)
                pv(tile, 2)
                if not last:
                    pe.wait_ge(z["kT_sb"], 2 * tile + 3)
                    kT_of(tile + 1, 1)
                    scores(tile + 1, 0)
                turn_probs(tile, 3)
                pv(tile, 3)

            pe.wait_ge(z["ld"], 16 * 9)
            pe.wait_ge(z["init"], 7)
            hT_of(0)
            qkv(0, 0)
            pe.wait_ge(z["rope_read"], 1)
            qkv(0, 1)
            pe.wait_ge(z["rope_read"], 2)
            qkv(0, 2)
            pe.wait_ge(z["rope_read"], 3)
            pe.wait_ge(z["v_sb"], 1)
            qT_of(0, 0)
            pe.wait_ge(z["qT_sb"], 1)
            qT_of(0, 1)
            pe.wait_ge(z["qT_sb"], 2)
            kT_of(0, 0)
            pe.wait_ge(z["kT_sb"], 1)
            kT_of(0, 1)
            scores(0, 0, True)
            body(0, True, False)
            with pe.Fori(1, NT - 1) as tile:
                body(tile, False, False)
            body(NT - 1, False, True)
            pe.wait_ge(z["x2"], NT - 1)
            yT_of(NT - 1, 0)
            pe.wait_ge(z["yT_sb"], 2 * NT - 1)
            yT_of(NT - 1, 1)
            pe.wait_ge(z["yT_sb"], 2 * NT)
            project(NT - 1)


E, TOPK, DFF = 32, 4, 128
PAIRS = E // 2


def experts(nc, t, x1, x2, ident, ones_row, out):
    with ExitStack() as ctx:
        def sb(name, shape, dt=F32):
            return ctx.enter_context(nc.sbuf_tensor(name, shape, dt))

        w_up = sb("w_up", [P, E, 2 * DFF])
        w_down = sb("w_down", [P, E, D])
        w_gate = sb("w_gate", [P, E])
        b_gate = sb("b_gate", [1, E])
        norm_w = sb("norm_w2", [P, 1])
        expert_id = sb("expert_id", [P, E])
        sq = sb("sq2", [P, 2, D])
        ms = sb("ms2", [P, NT])
        rms = sb("rms2", [P, NT])
        neg_half = sb("neg_half2", [P, NT])
        h2 = sb("h2", [P, NT, D])
        h2T = sb("h2T", [P, NT * P])
        logits = sb("logits", [P, NT, E])
        top = sb("top", [P, NT, 8])
        top_i = sb("top_i", [P, NT, 8], mybir.dt.uint32)
        top_f = sb("top_f", [P, NT, 8])
        gates = sb("gates", [P, NT, TOPK])
        gate_sum = sb("gate_sum", [P, NT])
        hit = sb("hit", [P, 2, NT, E])
        share = sb("share", [P, NT, E])
        h2T_cur = sb("h2T_cur", [P, P])
        share_cur = sb("share_cur", [P, E])
        silu = sb("silu", [P, 2, 2, DFF])
        act = sb("act", [P, 2, 2, DFF])
        actT = sb("actT", [P, 2, 2, P])
        stats = sb("stats2", [P, NT, 6])
        mv = sb("mv2", [P, NT, 2])
        rstd = sb("rstd2", [P, NT])
        ps = ctx.enter_context(nc.psum_tensor("ps_e", [P, 8, 512], F32))
        UP, TURN, Y, MISC = (0, 1, 2), (3, 4), (5, 6), 7

        names = ("ld ld_w init sq ms rms h2 h2T_ps h2T_sb logits_ps logits top chain gexp gates share cur_h up silu act turn actT down "
                 "x12 x3 stats var rstd final outd").split()
        z = {n: ctx.enter_context(nc.semaphore("e_" + n)) for n in names}
        block = ctx.enter_context(nc.Block())

        @block.sync
        def _(sp):
            sp.dma_start(w_gate[:], t["L0_ffn_gate_w"][:]).then_inc(z["ld"], 16)
            sp.dma_start(b_gate[:], t["L0_ffn_gate_b"].rearrange("(a n) -> a n", a=1)).then_inc(z["ld"], 16)
            sp.dma_start(norm_w[:], t["L0_ffn_ffn_norm_w"].rearrange("(p a) -> p a", a=1)).then_inc(z["ld"], 16)
            sp.dma_start(expert_id[:], t["expert_id"][:]).then_inc(z["ld"], 16)
            sp.dma_start(w_up[:], t["L0_ffn_W_up"].rearrange("e p n -> p e n")).then_inc(z["ld_w"], 16)
            sp.dma_start(w_down[:], t["L0_ffn_W_down"].rearrange("e p n -> p e n")).then_inc(z["ld_w"], 16)
            for n in range(NT):
                sp.wait_ge(z["final"], n + 1)
                sp.dma_start(out[n // TILES, (n % TILES) * P:(n % TILES + 1) * P, :], x2[:, n, :]).then_inc(z["outd"], 16)
            sp.wait_ge(z["outd"], 16 * NT)

        @block.gpsimd
        def _(g):
            g.memset(neg_half[:], -0.5).then_inc(z["init"], 1)
            g.wait_ge(z["init"], 1)
            g.wait_ge(z["ms"], 1)
            g.tensor_tensor(rms[:], ms[:], neg_half[:], ALU.pow).then_inc(z["rms"], 1)
            g.wait_ge(z["h2"], NT)
            g.tensor_tensor(x2[:], x2[:], x1[:], ALU.add).then_inc(z["x12"], 1)
            g.wait_ge(z["share"], 1)
            g.wait_ge(z["h2T_sb"], 4)

            def stage(tile, first):
                if not first:
                    g.wait_ge(z["up"], PAIRS * tile)
                g.tensor_copy(h2T_cur[:], h2T[:, ds(tile * P, P)]).then_inc(z["cur_h"], 1)
                if not first:
                    g.wait_ge(z["act"], 2 * PAIRS * tile)
                g.tensor_copy(share_cur[:], share[:, ds(tile, 1), :].rearrange("p a n -> p (a n)")).then_inc(z["cur_h"], 1)

            stage(0, True)
            with g.Fori(1, NT) as tile:
                stage(tile, False)
            g.wait_ge(z["var"], 1)
            g.tensor_tensor(rstd[:], mv[:, :, 1], neg_half[:], ALU.pow).then_inc(z["rstd"], 1)

        @block.scalar
        def _(act_e):
            act_e.wait_ge(z["ld"], 64)
            for c in range(NT // 4):
                act_e.wait_ge(z["h2T_ps"], c + 1)
                nc.scalar.activation(h2T[:, 512 * c:512 * c + 512], ps[:, c % 2, :], ACT.Copy, scale=norm_w[:, 0:1]).then_inc(z["h2T_sb"], 1)
            act_e.wait_ge(z["gates"], 1)
            nc.scalar.activation(gates[:], gates[:], ACT.Exp).then_inc(z["gexp"], 1)

            def body(tile, first):
                for q in range(PAIRS + 1):
                    if q < PAIRS:
                        n = tile * PAIRS + q
                        act_e.wait_ge(z["up"], n + 1)
                        if not (first and q < 2):
                            act_e.wait_ge(z["act"], 2 * n - 2)
                        nc.scalar.activation(silu[:, q % 2, :, :], ps[:, UP[0] + q % 2, :].rearrange("p (e w n) -> p e w n", e=2, w=2)[:, :, 1, :], ACT.Silu)\
                            .then_inc(z["silu"], 1)
                    if q:
                        n = tile * PAIRS + q - 1
                        act_e.wait_ge(z["turn"], n + 1)
                        if not (first and q < 3):
                            act_e.wait_ge(z["down"], n - 1)
                        nc.scalar.copy(actT[:, (q - 1) % 2, :, :].rearrange("p e n -> p (e n)"), ps[:, TURN[(q - 1) % 2], 0:256]).then_inc(z["actT"], 1)

            body(0, True)
            with act_e.Fori(1, NT) as tile:
                body(tile, False)

        @block.vector
        def _(v):
            cnt = [0]

            def chain(ins):
                cnt[0] += 1
                ins.then_inc(z["chain"], 1)
                v.wait_ge(z["chain"], cnt[0])

            for n in range(NT):
                if n >= 2:
                    v.wait_ge(z["sq"], n - 1)
                v.tensor_tensor_reduce(out=sq[:, n % 2, :], in0=x2[:, n, :], in1=x2[:, n, :], scale=1.0, scalar=0.0, op0=ALU.mult, op1=ALU.add,
                                       accum_out=ms[:, n:n + 1]).then_inc(z["sq"], 1)
            v.wait_ge(z["sq"], NT)
            v.tensor_scalar(ms[:], ms[:], 1.0 / D, EPS, ALU.mult, ALU.add).then_inc(z["ms"], 1)
            v.wait_ge(z["rms"], 1)
            for n in range(NT):
                v.tensor_scalar(h2[:, n, :], x2[:, n, :], rms[:, n:n + 1], None, ALU.mult).then_inc(z["h2"], 1)
            v.wait_ge(z["logits_ps"], 1)
            chain(v.tensor_copy(logits[:].rearrange("p t e -> p (t e)"), ps[:, MISC, :]))
            for n in range(NT):
                v.max(top[:, n, :], logits[:, n, :]).then_inc(z["top"], 1)
            v.wait_ge(z["top"], NT)
            for n in range(NT):
                v.max_index(top_i[:, n, :], top[:, n, :], logits[:, n, :]).then_inc(z["top"], 1)
            v.wait_ge(z["top"], 2 * NT)
            v.tensor_tensor(gates[:], top[:, :, 0:TOPK], top[:, :, 0:1].broadcast_to([P, NT, TOPK]), ALU.subtract).then_inc(z["gates"], 1)
            chain(v.tensor_copy(top_f[:], top_i[:]))
            v.wait_ge(z["gexp"], 1)
            chain(v.tensor_reduce(gate_sum[:], gates[:], AX.X, ALU.add))
            chain(v.reciprocal(gate_sum[:], gate_sum[:]))
            chain(v.tensor_tensor(gates[:], gates[:], gate_sum[:].unsqueeze(2).broadcast_to([P, NT, TOPK]), ALU.mult))
            v.wait_ge(z["ld"], 64)
            for k in range(TOPK):
                chain(v.tensor_tensor(hit[:, 0, :, :], expert_id[:].unsqueeze(1).broadcast_to([P, NT, E]),
                                      top_f[:, :, k:k + 1].broadcast_to([P, NT, E]), ALU.is_equal))
                dst = share if k == 0 else hit[:, 1, :, :]
                last = v.tensor_tensor(dst[:], hit[:, 0, :, :], gates[:, :, k:k + 1].broadcast_to([P, NT, E]), ALU.mult)
                chain(last)
                if k:
                    last = v.tensor_tensor(share[:], share[:], hit[:, 1, :, :], ALU.add)
                    if k < TOPK - 1:
                        chain(last)
                    else:
                        last.then_inc(z["share"], 1)

            def body(tile, first):
                for q in range(PAIRS):
                    n = tile * PAIRS + q
                    if q == 0:
                        v.wait_ge(z["cur_h"], 2 * tile + 2)
                    v.wait_ge(z["silu"], n + 1)
                    if not (first and q < 2):
                        v.wait_ge(z["turn"], n - 1)
                    for e in range(2):
                        v.scalar_tensor_tensor(act[:, q % 2, e, :], silu[:, q % 2, e, :], share_cur[:, 2 * q + e:2 * q + e + 1],
                                               ps[:, UP[0] + q % 2, 256 * e:256 * e + 128], ALU.mult, ALU.mult).then_inc(z["act"], 1)
                    if q == 1 and not first:
                        finish(tile - 1)

            def finish(tile):
                v.wait_ge(z["down"], PAIRS * (tile + 1))
                x = x2[:, ds(tile, 1), :].rearrange("p a n -> p (a n)")
                v.tensor_tensor(x, x, ps[:, Y[0], 0:P], ALU.add).then_inc(z["x3"], 1)

            v.wait_ge(z["x12"], 1)
            body(0, True)
            with v.Fori(1, NT) as tile:
                body(tile, False)
            finish(NT - 1)
            v.wait_ge(z["x3"], NT)
            for n in range(NT):
                v.bn_stats(stats[:, n, :], x2[:, n, :]).then_inc(z["stats"], 1)
            v.wait_ge(z["stats"], NT)
            for n in range(NT):
                v.bn_aggr(mv[:, n, :], stats[:, n, :]).then_inc(z["stats"], 1)
            v.wait_ge(z["stats"], 2 * NT)
            v.tensor_scalar(mv[:, :, 1], mv[:, :, 1], EPS, None, ALU.add).then_inc(z["var"], 1)
            v.wait_ge(z["rstd"], 1)
            for n in range(NT):
                v.tensor_scalar(x2[:, n, :], x2[:, n, :], mv[:, n, 0:1], rstd[:, n:n + 1], ALU.subtract, ALU.mult).then_inc(z["final"], 1)

        @block.tensor
        def _(pe):
            mm = nc.tensor.matmul
            tr = nc.tensor.transpose
            for n in range(NT):
                if n % 4 == 0 and n >= 8:
                    pe.wait_ge(z["h2T_sb"], n // 4 - 1)
                pe.wait_ge(z["h2"], n + 1)
                m = tr(ps[:, (n // 4) % 2, (n % 4) * P:(n % 4 + 1) * P], h2[:, n, :], ident[:])
                if n % 4 == 3:
                    m.then_inc(z["h2T_ps"], 1)
            pe.wait_ge(z["h2T_sb"], 4)
            pe.wait_ge(z["ld"], 64)
            for n in range(NT):
                o = ps[:, MISC, n * E:(n + 1) * E]
                mm(o, h2T[:, n * P:(n + 1) * P], w_gate[:], start=True, stop=False)
                m = mm(o, ones_row[:], b_gate[:], start=False, stop=True)
            m.then_inc(z["logits_ps"], 1)
            pe.wait_ge(z["ld_w"], 32)

            def up(tile, q, first):
                n = tile * PAIRS + q
                if q == 0:
                    pe.wait_ge(z["cur_h"], 2 * tile + 1)
                if not (first and q < 2):
                    pe.wait_ge(z["act"], 2 * n - 2)
                mm(ps[:, UP[0] + q % 2, :], h2T_cur[:], w_up[:, 2 * q:2 * q + 2, :].rearrange("p e n -> p (e n)"), start=True, stop=True).then_inc(z["up"], 1)

            def turn(tile, q, first):
                n = tile * PAIRS + q
                pe.wait_ge(z["act"], 2 * n + 2)
                if not (first and q < 2):
                    pe.wait_ge(z["actT"], n - 1)
                for e in range(2):
                    m = tr(ps[:, TURN[q % 2], e * P:(e + 1) * P], act[:, q % 2, e, :], ident[:])
                m.then_inc(z["turn"], 1)

            def down(tile, q, first):
                n = tile * PAIRS + q
                pe.wait_ge(z["actT"], n + 1)
                if q == 0 and not first:
                    pe.wait_ge(z["x3"], tile)
                for e in range(2):
                    m = mm(ps[:, Y[0], 0:P], actT[:, q % 2, e, :], w_down[:, 2 * q + e, :], start=(q == 0 and e == 0), stop=(q == PAIRS - 1 and e == 1))
                m.then_inc(z["down"], 1)

            def body(tile, first):
                for q in range(PAIRS + 2):
                    if q < PAIRS:
                        up(tile, q, first)
                    if 0 <= q - 1 < PAIRS:
                        turn(tile, q - 1, first)
                    if 0 <= q - 2:
                        down(tile, q - 2, first)

            body(0, True)
            with pe.Fori(1, NT) as tile:
                body(tile, False)


def build(nc, t, out):
    with ExitStack() as ctx:
        def sb(name, shape, dt=F32):
            return ctx.enter_context(nc.sbuf_tensor(name, shape, dt))
        x1 = sb("x1", [P, B * TILES, D])
        ident = sb("ident", [P, P])
        ident16 = sb("ident16", [P, P], BF16)
        ones_row = sb("ones_row", [1, P])
        differential_attention(nc, t, x1, ident, ident16, ones_row)
        x2 = sb("x2", [P, B * TILES, D])
        window_attention(nc, t, x1, x2, ident, ident16, ones_row)
        experts(nc, t, x1, x2, ident, ones_row, out)


def constants():
    c = {}
    c["ident"] = np.eye(P, dtype=np.float32)
    c["head_mean"] = np.kron(np.eye(H, dtype=np.float32), np.full((DH, DH), 1.0 / DH, np.float32))
    c["ones16"] = np.full((2, GROUPS * HG * S // 2), 0x3F803F80, np.uint32).view(np.float32)
    pos = np.arange(S, dtype=np.float32) / np.float32(32.0)
    inv = (1.0 / np.float32(150000.0) ** (np.arange(0, FDH, 2, dtype=np.float32) / np.float32(FDH))).astype(np.float32)
    f = pos[:, None] * inv[None, :]
    cos = np.repeat(np.cos(f), 2, axis=1).astype(np.float32)
    sin = np.stack([-np.sin(f), np.sin(f)], axis=2).reshape(S, FDH).astype(np.float32)
    c["rope_c"] = cos.reshape(TILES, P, FDH).transpose(1, 0, 2)
    c["rope_s"] = sin.reshape(TILES, P, FDH).transpose(1, 0, 2)
    p, k = np.arange(P)[:, None], np.arange(2 * P)[None, :]
    seen = (k >= p) & (k <= p + WINDOW)
    first = seen & (k >= P)
    m = np.stack([np.where(x, 0.0, MASKED) for x in (first, first, seen, seen)], axis=1)
    c["mask"] = m.reshape(P, 2, 4 * P).astype(np.float32)
    c["expert_id"] = np.tile(np.arange(E, dtype=np.float32), (P, 1))
    return c


def kernel(**inputs):
    import concourse.bacc as bacc
    from concourse.bass_utils import run_bass_kernel_spmd

    nc = bacc.Bacc("TRN2", target_bir_lowering=False, num_devices=1)
    nc.disable_value_cache = True
    arrays, t = {}, {}
    for name, a in {**inputs, **constants()}.items():
        a = np.ascontiguousarray(a)
        arrays["in_" + name] = a
        t[name] = nc.dram_tensor("in_" + name, a.shape, mybir.dt.from_np(a.dtype), kind="ExternalInput").ap()
    out = nc.dram_tensor("out_dram", (B, S, D), F32, kind="ExternalOutput").ap()
    build(nc, t, out)
    r = run_bass_kernel_spmd(nc, [arrays], core_ids=[0])
    return r.results[0]["out_dram"]
```

```python
from contextlib import ExitStack

import numpy as np

import concourse.bass as bass
from concourse import mybir

F32 = mybir.dt.float32
BF16 = mybir.dt.bfloat16
ALU = mybir.AluOpType
ACT = mybir.ActivationFunctionType
AX = mybir.AxisListType

B, S, D, H = 2, 1024, 128, 16
DH = D // H
P = 128
TILES = S // P
HG = 4
GROUPS = B * H // HG
EPS = 1e-5
LAMBDA_INIT = 0.8
QK_ROWS = 96
PARTS_Q = (0, 0, 1, 0, 2, 1)
PARTS_K = (0, 1, 0, 2, 0, 1)
SHIFT_ROW = len(PARTS_Q) * DH
STEPS = 2 * TILES
ds = bass.ds


BIAS_AT, BIASES = {}, 0
for _name, _n in (("L0_attn_bv", D), ("L0_attn_bo", D), ("L0_ffn_qkv_b", 1536), ("L0_ffn_proj_b", D), ("L0_ffn_gate_b", 32)):
    BIAS_AT[_name] = (BIASES, _n)
    BIASES += _n


def bias_of(bias_rows, name, start=0, size=None):
    a, n = BIAS_AT[name]
    return bias_rows[:, a + start:a + start + (size or n)]


def differential_attention(nc, t, x1, ident, ident16, bias_sel, bias_rows):
    with ExitStack() as ctx:
        def sb(name, shape, dt=F32):
            return ctx.enter_context(nc.sbuf_tensor(name, shape, dt))

        def sem(name):
            return ctx.enter_context(nc.semaphore(name))

        qk_parts = nc.dram_tensor("qk_parts", [2, 3, P, B * S], BF16, kind="Internal")

        x_in = x1
        xT = sb("xT", [P, B * S])
        w_attn = sb("w_attn", [P, 4, D])
        head_mean = sb("head_mean", [P, P])
        cols = sb("cols", [P, 8])
        lam = sb("lam", [P, 8])
        q_stack = sb("q_stack", [QK_ROWS, 2 * GROUPS, HG, 512], BF16)
        k_stack = sb("k_stack", [QK_ROWS, GROUPS, HG, S], BF16)
        v_all = sb("v_all", [P, TILES, GROUPS, HG * DH])
        v_stage = sb("v_stage", [P, TILES, HG, 32])
        e_ring = sb("e_ring", [P, 4, 2, 512])
        part = sb("part", [P, 2, 3, 512], BF16)
        fl = sb("fl", [P, 2, 512])
        max_parts = sb("max_parts", [P, 2, HG, 4, 2])
        shift = sb("shift", [P, HG, 4])
        shift_rest = sb("shift_rest", [P, HG, 4])
        shift16 = sb("shift16", [P, 2, HG, 4], BF16)
        shiftT = sb("shiftT", [2 * HG * 4, P], BF16)
        o_raw = sb("o_raw", [P, 512])
        o_inv = sb("o_inv", [P, 4, HG])
        o_all = sb("o_all", [P, TILES, GROUPS, HG * DH])
        normT = xT[:, 0:S]
        bias_f = o_all[0:1].rearrange("p t g n -> p (t g n)")[:, 0:BIASES]
        bias_16 = e_ring[0:1].rearrange("p a b n -> p (a b n)")[:, 0:3 * BIASES // 2].bitcast(BF16).rearrange("p (a n) -> p a n", a=3)
        sel32 = o_raw[:, 0:P]
        bn = sb("bn", [P, 2, 6])
        st = sb("st", [P, 16])
        bnt = sb("bnt", [P, TILES, 6])
        mv = sb("mv", [P, TILES, 2])
        rstd = sb("rstd", [P, TILES])
        eps_t = sb("eps_t", [P, TILES])
        half_t = sb("half_t", [P, TILES])

        ps = ctx.enter_context(nc.psum_tensor("ps", [P, 8, 512], F32))
        S_BANK = (0, 2)
        M_BANK = (4, 5)
        O_BANK = (6, 7)

        names = ("bias_ld bias_split bias_zero bias_in ld_x0 ld_x1 ld_ident stack0_ld ld_w ld_small idents stack_zero xT_ps xT_sb lam_ps lam_e lam_v lam_done dve_c proj_ps q32 parts parts_out0 parts_out1 "
                 "vps v_sb v_free stack_ld vst qk_done exp_done mx_done mx_read shift16_done "
                 "shiftT_ps shiftT_sb aug_ld pv_done o_raw_done oT_ps o_read gn_T gn_st gn_mm gn_mmr gn_pow gn_norm "
                 "y_ps y_ln y_read ln_pow x1_done outd fl_free part_free proj_free").split()
        z = {n: sem("s_" + n) for n in names}
        block = ctx.enter_context(nc.Block())
        NB = B * 2 * 2

        @block.sync
        def _(sp):
            for b in range(B):
                sp.dma_start(x_in[:, b * TILES:(b + 1) * TILES, :],
                             t["L0_attn_x"][b].rearrange("(t p) d -> p t d", p=P)).then_inc(z[f"ld_x{b}"], 16)
                if b == 0:
                    sp.dma_start(ident[:], t["ident"][:]).then_inc(z["ld_ident"], 16)
                    for n, w in enumerate(("Wq", "Wk", "Wv", "Wo")):
                        sp.dma_start(w_attn[:, n, :], t["L0_attn_" + w][:]).then_inc(z["ld_w"], 16)
            for name, (a, n) in BIAS_AT.items():
                sp.dma_start(bias_f[:, a:a + n], t[name].rearrange("(a n) -> a n", a=1)).then_inc(z["bias_ld"], 16)
            sp.wait_ge(z["bias_zero"], 1)
            sp.wait_ge(z["bias_split"], 1)
            for r in range(3):
                sp.dma_start(bias_rows[r:r + 1, :], bias_16[:, r, :]).then_inc(z["bias_in"], 16)

            def stack(i, b, g):
                for s_ in range(len(PARTS_Q)):
                    for c in range(2):
                        src = qk_parts[0, PARTS_Q[s_], 32 * g:32 * g + 32, b * S + 512 * c:b * S + 512 * c + 512]
                        sp.dma_start(q_stack[8 * s_:8 * s_ + 8, 2 * i + c, :, :],
                                     src.rearrange("(j d) n -> d j n", d=DH)).then_inc(z["stack0_ld" if i == 0 else "stack_ld"], 16)
                    src = qk_parts[1, PARTS_K[s_], 32 * g:32 * g + 32, b * S:(b + 1) * S]
                    sp.dma_start(k_stack[8 * s_:8 * s_ + 8, i, :, :],
                                 src.rearrange("(j d) n -> d j n", d=DH)).then_inc(z["stack0_ld" if i == 0 else "stack_ld"], 16)

            for b in range(B):
                for c in range(2):
                    for side in range(2):
                        n = (b * 2 + c) * 2 + side
                        sp.wait_ge(z["parts"], n + 1)
                        sp.dma_start(qk_parts[side, :, :, b * S + c * 512:b * S + c * 512 + 512].rearrange("a p n -> p a n"),
                                     part[:, n % 2, :, :]).then_inc(z[f"parts_out{n % 2}"], 16)
                if b == 0:
                    for k in range(2):
                        sp.wait_ge(z[f"parts_out{k}"], 16 * 2)
                    sp.wait_ge(z["stack_zero"], 2)
                    sp.dma_start(k_stack[SHIFT_ROW:SHIFT_ROW + 2, :, :, :].rearrange("p a j n -> p (a j n)").bitcast(F32), t["ones16"][:]).then_inc(z["stack0_ld"], 16)
                    stack(0, 0, 0)
                    stack(1, 0, 1)
            for k in range(2):
                sp.wait_ge(z[f"parts_out{k}"], 16 * NB // 2)
            for i in range(2, GROUPS):
                sp.wait_ge(z["stack_zero"], 2)
                stack(i, i // 4, i % 4)

        @block.gpsimd
        def _(g):
            g.memset(bias_rows[:], 0.0).then_inc(z["bias_zero"], 1)
            g.memset(k_stack[:].rearrange("p a j n -> p (a j n)").bitcast(F32), 0.0).then_inc(z["stack_zero"], 1)
            g.memset(v_stage[:], 0.0).then_inc(z["vst"], 1)
            g.wait_ge(z["vst"], 1)
            g.memset(v_stage[:, :, :, 8:9], 1.0).then_inc(z["vst"], 1)
            g.memset(eps_t[:], EPS).then_inc(z["vst"], 1)
            g.memset(half_t[:], -0.5).then_inc(z["vst"], 1)

            def refresh(i, kt):
                src = v_all[:, kt, i, :] if isinstance(i, int) else v_all[:, kt, ds(i, 1), :].rearrange("p a n -> p (a n)")
                g.tensor_copy(v_stage[:, kt, :, 0:DH], src.rearrange("p (j d) -> p j d", d=DH)).then_inc(z["vst"], 1)

            g.wait_ge(z["v_sb"], B * TILES // 4)
            for kt in range(TILES):
                refresh(0, kt)

            def body(i):
                for kt in range(TILES):
                    g.wait_ge(z["pv_done"], i * STEPS + TILES + kt + 1)
                    refresh(i + 1, kt)

            body(0)
            with g.Fori(1, GROUPS - 1) as i:
                body(i)
            for b in range(B):
                g.wait_ge(z["gn_st"], 4 * b + 4)
                g.tensor_tensor(st[:, 8:9], st[:, 7:8], half_t[:, 0:1], ALU.pow).then_inc(z["gn_pow"], 1)
                g.wait_ge(z["y_ln"], b + 1)
                g.tensor_tensor(rstd[:], mv[:, :, 1], half_t[:], ALU.pow).then_inc(z["ln_pow"], 1)

        @block.scalar
        def _(act):
            for n, w in enumerate(("bq", "bk", "lq1", "lk1", "lq2", "lk2", "gn_w", "gn_b")):
                a = t["L0_attn_" + w]
                src = a.rearrange("(p a) -> p a", a=1) if len(a.shape) == 1 else a.rearrange("h (d a) -> (h d) a", a=1)
                act.dma_start(cols[:, n:n + 1], src).then_inc(z["ld_small"], 16)
            act.dma_start(sel32, t["bias_sel"][:]).then_inc(z["ld_small"], 16)
            act.dma_start(head_mean[:], t["head_mean"][:]).then_inc(z["ld_small"], 16)
            act.wait_ge(z["lam_ps"], 1)
            nc.scalar.activation(lam[:, 2:4], ps[:, 7, 0:2], ACT.Exp, scale=float(DH)).then_inc(z["lam_e"], 1)
            for b in range(B):
                for c in range(2):
                    act.wait_ge(z["xT_ps"], b * 2 + c + 1)
                    nc.scalar.copy(xT[:, b * S + c * 512:b * S + (c + 1) * 512], ps[:, c, :]).then_inc(z["xT_sb"], 1)
            act.wait_ge(z["lam_done"], 1)
            for n in range(NB):
                side = n % 2
                act.wait_ge(z["proj_ps"], n + 1)
                if n >= 2:
                    act.wait_ge(z["fl_free"], n - 1)
                if side == 0:
                    nc.scalar.activation(fl[:, n % 2, :], ps[:, 2 + n % 2, :], ACT.Identity, bias=lam[:, 6:7], scale=lam[:, 5:6]).then_inc(z["q32"], 1)
                else:
                    nc.scalar.activation(fl[:, n % 2, :], ps[:, 2 + n % 2, :], ACT.Identity, bias=cols[:, 1:2]).then_inc(z["q32"], 1)
            for m in range(B * TILES // 4):
                act.wait_ge(z["vps"], m + 1)
                nc.scalar.copy(v_all[:, 4 * (m % 2):4 * (m % 2) + 4, 4 * (m // 2):4 * (m // 2) + 4, :],
                               ps[:, m % 2, :].rearrange("p (t g n) -> p t g n", t=4, g=4)).then_inc(z["v_sb"], 1)

            def shifts(i, qc):
                h = 2 * i + qc
                act.wait_ge(z["shiftT_ps"], h + 1)
                if not isinstance(h, int) or h >= 1:
                    act.wait_ge(z["aug_ld"], 32 * h)
                b = O_BANK[qc]
                nc.scalar.copy(shiftT[:], ps[0:32, b, 0:64].bitcast(BF16)).then_inc(z["shiftT_sb"], 1)
                act.wait_ge(z["shiftT_sb"], h + 1)
                for w in range(2):
                    dst = q_stack[SHIFT_ROW + w:SHIFT_ROW + w + 1, ds(2 * i + qc, 1), :, :].rearrange("p a j n -> p (a j n)")
                    act.dma_start(dst, shiftT[16 * w:16 * w + 16, :]).then_inc(z["aug_ld"], 16)

            def raw(i, qc):
                h = 2 * i + qc
                act.wait_ge(z["pv_done"], TILES * (h + 1))
                if not isinstance(h, int) or h >= 1:
                    act.wait_ge(z["oT_ps"], h)
                nc.scalar.copy(o_raw[:], ps[:, O_BANK[qc], :]).then_inc(z["o_raw_done"], 1)

            def body(i, first, last):
                for s_ in range(STEPS):
                    qc, kt = divmod(s_, TILES)
                    gs = i * STEPS + s_
                    for p in range(2):
                        act.wait_ge(z["qk_done"], 2 * gs + p + 1)
                        if not (first and s_ < 2):
                            act.wait_ge(z["pv_done"], gs - 1)
                        nc.scalar.activation(e_ring[:, 2 * (s_ % 2) + p, :, :], ps[:, S_BANK[p]:S_BANK[p] + 2, :], ACT.Exp).then_inc(z["exp_done"], 1)
                    if kt == 1 and not (first and qc == 0):
                        raw(*((i, 0) if qc else (i - 1, 1)))
                    if kt == 5:
                        if qc == 0:
                            shifts(i, 1)
                        elif not last:
                            shifts(i + 1, 0)

            shifts(0, 0)
            body(0, True, False)
            with act.Fori(1, GROUPS - 1) as i:
                body(i, False, False)
            body(GROUPS - 1, False, True)
            raw(GROUPS - 1, 1)
            for b in range(B):
                act.wait_ge(z["gn_norm"], b + 1)
                for c in range(2):
                    nc.scalar.activation(normT[:, c * 512:(c + 1) * 512], ps[:, c, :], ACT.Identity, bias=st[:, 10:11], scale=st[:, 9:10]).then_inc(z["gn_mmr"], 1)

        @block.vector
        def _(v):
            cnt = [0]

            def chain(ins):
                cnt[0] += 1
                ins.then_inc(z["dve_c"], 1)
                v.wait_ge(z["dve_c"], cnt[0])

            v.wait_ge(z["bias_ld"], 16 * len(BIAS_AT))
            chain(v.tensor_copy(bias_16[:, 0, :], bias_f))
            chain(v.tensor_tensor(bias_f, bias_f, bias_16[:, 0, :], ALU.subtract))
            chain(v.tensor_copy(bias_16[:, 1, :], bias_f))
            v.tensor_tensor(bias_16[:, 2, :], bias_f, bias_16[:, 1, :], ALU.subtract).then_inc(z["bias_split"], 1)
            v.memset(q_stack[:].rearrange("p a j n -> p (a j n)").bitcast(F32), 0.0).then_inc(z["stack_zero"], 1)
            v.wait_ge(z["ld_small"], 16 * 10)
            v.tensor_tensor(lam[:, 0:1], cols[:, 2:3], cols[:, 3:4], ALU.mult).then_inc(z["lam_v"], 1)
            v.tensor_tensor(lam[:, 1:2], cols[:, 4:5], cols[:, 5:6], ALU.mult).then_inc(z["lam_v"], 1)
            v.wait_ge(z["ld_ident"], 16)
            v.tensor_copy(ident16[:], ident[:]).then_inc(z["idents"], 1)
            v.tensor_copy(bias_sel[:], sel32).then_inc(z["idents"], 1)
            v.wait_ge(z["lam_e"], 1)
            chain(v.tensor_tensor(lam[:, 4:5], lam[:, 2:3], lam[:, 3:4], ALU.subtract))
            chain(v.tensor_scalar(lam[:, 5:6], lam[:, 4:5], LAMBDA_INIT, DH ** -0.5, ALU.add, ALU.mult))
            v.tensor_tensor(lam[:, 6:7], cols[:, 0:1], lam[:, 5:6], ALU.mult).then_inc(z["lam_done"], 1)
            for n in range(NB):
                v.wait_ge(z["q32"], n + 1)
                if n >= 2:
                    v.wait_ge(z[f"parts_out{n % 2}"], 16 * (n // 2))
                f = fl[:, n % 2, :]
                chain(v.tensor_copy(part[:, n % 2, 0, :], f))
                chain(v.tensor_tensor(f, f, part[:, n % 2, 0, :], ALU.subtract))
                chain(v.tensor_copy(part[:, n % 2, 1, :], f))
                last = v.tensor_tensor(part[:, n % 2, 2, :], f, part[:, n % 2, 1, :], ALU.subtract)
                last.then_inc(z["parts"], 1)
                v.wait_ge(z["parts"], n + 1)
                v.tensor_copy(st[:, 15:16], lam[:, 5:6]).then_inc(z["fl_free"], 1)

            def reduce(h, u):
                j, r = divmod(u, 8)
                q, c = divmod(r, 2)
                v.wait_ge(z["mx_done"], 32 * h + u + 1)
                v.tensor_reduce(max_parts[:, 0, j, q, c:c + 1], ps[:, M_BANK[u % 2], :], AX.X, ALU.max).then_inc(z["mx_read"], 1)

            def final(h, first):
                v.wait_ge(z["mx_read"], 32 * h + 32)
                if not first:
                    v.wait_ge(z["shiftT_ps"], h)
                v.tensor_reduce(shift[:], max_parts[:, 0, :, :, :], AX.X, ALU.max, negate=True).then_inc(z["shift16_done"], 1)
                v.wait_ge(z["shift16_done"], 4 * h + 1)
                v.tensor_copy(shift16[:, 0, :, :], shift[:]).then_inc(z["shift16_done"], 1)
                v.wait_ge(z["shift16_done"], 4 * h + 2)
                v.tensor_tensor(shift_rest[:], shift[:], shift16[:, 0, :, :], ALU.subtract).then_inc(z["shift16_done"], 1)
                v.wait_ge(z["shift16_done"], 4 * h + 3)
                v.tensor_copy(shift16[:, 1, :, :], shift_rest[:]).then_inc(z["shift16_done"], 1)

            def normalise(i, qc):
                h = 2 * i + qc
                v.wait_ge(z["oT_ps"], h + 1)
                src = ps[:, O_BANK[qc], :].rearrange("p (t j c) -> p t j c", t=4, j=HG)
                v.reciprocal(o_inv[:], src[:, :, :, DH]).then_inc(z["o_read"], 1)
                v.wait_ge(z["o_read"], 2 * h + 1)
                dst = o_all[:, 4 * qc:4 * qc + 4, i, :] if isinstance(i, int) else o_all[:, 4 * qc:4 * qc + 4, ds(i, 1), :].rearrange("p t a n -> p (t a) n")
                v.tensor_tensor(dst.rearrange("p t (j d) -> p t j d", j=HG), src[:, :, :, 0:DH],
                                o_inv[:].unsqueeze(3).broadcast_to([P, 4, HG, DH]), ALU.mult).then_inc(z["o_read"], 1)

            def body(i, first, last):
                for s_ in range(STEPS):
                    qc, kt = divmod(s_, TILES)
                    if not last:
                        for u in range(4 * kt, 4 * kt + 4):
                            reduce(2 * i + 2 + qc, u)
                    if kt == 3 and not (first and qc == 0):
                        normalise(*((i, 0) if qc else (i - 1, 1)))
                    if not last and kt == TILES - 1:
                        final(2 * i + 2 + qc, False)

            for qc in range(2):
                for u in range(32):
                    reduce(qc, u)
                final(qc, qc == 0)
            body(0, True, False)
            with v.Fori(1, GROUPS - 1) as i:
                body(i, False, False)
            body(GROUPS - 1, False, True)
            normalise(GROUPS - 1, 1)
            for b in range(B):
                v.wait_ge(z["gn_T"], b + 1)
                for c in range(2):
                    v.bn_stats(bn[:, c, :], ps[:, c, :]).then_inc(z["dve_c"], 1)
                cnt[0] += 2
                v.wait_ge(z["dve_c"], cnt[0])
                v.bn_aggr(st[:, 0:2], bn[:].rearrange("p a n -> p (a n)")).then_inc(z["gn_st"], 1)
                v.wait_ge(z["gn_mm"], 2 * b + 1)
                chain(v.tensor_copy(st[:, 2:3], ps[:, 2, 0:1]))
                chain(v.tensor_tensor(st[:, 3:4], st[:, 0:1], st[:, 2:3], ALU.subtract))
                v.scalar_tensor_tensor(st[:, 4:5], st[:, 3:4], st[:, 3:4], st[:, 1:2], ALU.mult, ALU.add).then_inc(z["gn_st"], 1)
                v.wait_ge(z["gn_mm"], 2 * b + 2)
                chain(v.tensor_copy(st[:, 5:6], ps[:, 2, 4:5]))
                v.tensor_scalar(st[:, 7:8], st[:, 5:6], EPS, None, ALU.add).then_inc(z["gn_st"], 1)
                v.wait_ge(z["gn_st"], 4 * b + 3)
                v.tensor_copy(st[:, 15:16], st[:, 7:8]).then_inc(z["gn_st"], 1)
                v.wait_ge(z["gn_pow"], b + 1)
                chain(v.tensor_tensor(st[:, 9:10], st[:, 8:9], cols[:, 6:7], ALU.mult))
                chain(v.tensor_tensor(st[:, 11:12], st[:, 2:3], st[:, 9:10], ALU.mult))
                v.tensor_tensor(st[:, 10:11], cols[:, 7:8], st[:, 11:12], ALU.subtract).then_inc(z["gn_norm"], 1)
                for n in range(TILES):
                    v.wait_ge(z["y_ps"], 2 * b + n // 4 + 1)
                    xt = x_in[:, b * TILES + n, :]
                    chain(v.tensor_tensor(xt, xt, ps[:, 3 + n // 4, (n % 4) * P:(n % 4 + 1) * P], ALU.add))
                    chain(v.bn_stats(bnt[:, n, :], xt))
                    chain(v.bn_aggr(mv[:, n, :], bnt[:, n, :]))
                chain(v.tensor_scalar(mv[:, :, 1], mv[:, :, 1], EPS, None, ALU.add))
                v.tensor_copy(st[:, 15:16], mv[:, 0, 1:2]).then_inc(z["y_ln"], 1)
                v.wait_ge(z["ln_pow"], b + 1)
                for n in range(TILES):
                    v.tensor_scalar(x1[:, b * TILES + n, :], x_in[:, b * TILES + n, :], mv[:, n, 0:1], rstd[:, n:n + 1],
                                    ALU.subtract, ALU.mult).then_inc(z["x1_done"], 1)

        @block.tensor
        def _(pe):
            mm = nc.tensor.matmul
            tr = nc.tensor.transpose
            pe.wait_ge(z["ld_small"], 16 * 10)
            pe.wait_ge(z["lam_v"], 2)
            mm(ps[:, 7, 0:2], head_mean[:], lam[:, 0:2], start=True, stop=True).then_inc(z["lam_ps"], 1)
            pe.wait_ge(z["ld_w"], 16 * 4)
            pe.wait_ge(z["ld_ident"], 16)
            for b in range(B):
                pe.wait_ge(z[f"ld_x{b}"], 16)
                for c in range(2):
                    if b:
                        pe.wait_ge(z["xT_sb"], c + 1)
                    for n in range(4):
                        m = tr(ps[:, c, n * P:(n + 1) * P], x_in[:, b * TILES + 4 * c + n, :], ident[:])
                    m.then_inc(z["xT_ps"], 1)
            for n in range(NB):
                c = n // 2
                pe.wait_ge(z["xT_sb"], c + 1)
                if n >= 2:
                    pe.wait_ge(z["q32"], n - 1)
                mm(ps[:, 2 + n % 2, :], w_attn[:, n % 2, :], xT[:, c * 512:(c + 1) * 512], start=True, stop=True).then_inc(z["proj_ps"], 1)
            pe.wait_ge(z["idents"], 2)
            pe.wait_ge(z["bias_in"], 16 * 3)
            for m_ in range(B * TILES // 4):
                if m_ < 2:
                    pe.wait_ge(z["xT_sb"], 4)
                else:
                    pe.wait_ge(z["v_sb"], m_ - 1)
                for n in range(4):
                    o = ps[:, m_ % 2, n * P:(n + 1) * P]
                    mm(o, xT[:, (4 * m_ + n) * P:(4 * m_ + n + 1) * P], w_attn[:, 2, :], start=True, stop=False)
                    m = mm(o, bias_sel[:], bias_of(bias_rows, "L0_attn_bv"), start=False, stop=True)
                m.then_inc(z["vps"], 1)

            def ks(i, j, a, n):
                return k_stack[:, ds(i, 1), j, a:a + n].rearrange("p a n -> p (a n)")

            def qs(i, qc, j, a, n):
                return q_stack[:, ds(2 * i + qc, 1), j, a:a + n].rearrange("p a n -> p (a n)")

            def max_units(h, i, qc, us):
                for u in us:
                    j, r = divmod(u, 8)
                    q, c = divmod(r, 2)
                    if not isinstance(h, int) or 32 * h + u >= 2:
                        pe.wait_ge(z["mx_read"], 32 * h + u - 1)
                    mm(ps[:, M_BANK[u % 2], :], qs(i, qc, j, q * P, P), ks(i, j, c * 512, 512),
                       start=True, stop=True).then_inc(z["mx_done"], 1)

            def shifts(h, qc):
                pe.wait_ge(z["shift16_done"], 4 * h + 4)
                b = O_BANK[1 - qc]
                tr(ps[0:32, b, 0:64].bitcast(BF16), shift16[:].rearrange("p w j t -> p (w j t)"), ident16[:]).then_inc(z["shiftT_ps"], 1)

            def pv(i, s_, first, last=False):
                qc, kt = divmod(s_, TILES)
                gs = i * STEPS + s_
                pe.wait_ge(z["exp_done"], 2 * gs + 2)
                pe.wait_ge(z["vst"], 4 + (i * TILES if not first else 0) + kt + 1)
                for j in range(HG):
                    m = mm(ps[32 * j:32 * j + 32, O_BANK[qc], :], v_stage[:, kt, j, :], e_ring[:, 2 * (s_ % 2) + j // 2, j % 2, :],
                           start=(kt == 0), stop=(kt == TILES - 1))
                m.then_inc(z["pv_done"], 1)

            def o_turn(i, qc):
                h = 2 * i + qc
                pe.wait_ge(z["o_raw_done"], h + 1)
                for n in range(4):
                    m = tr(ps[:, O_BANK[qc], n * P:(n + 1) * P], o_raw[:, n * P:(n + 1) * P], ident[:])
                m.then_inc(z["oT_ps"], 1)

            def body(i, first, last):
                for s_ in range(STEPS):
                    qc, kt = divmod(s_, TILES)
                    gs = i * STEPS + s_
                    h = 2 * i + qc
                    if kt == 0:
                        pe.wait_ge(z["aug_ld"], 32 * h + 32)
                        if not (first and qc == 0):
                            pass
                    for p in range(2):
                        if not (first and s_ == 0):
                            pe.wait_ge(z["exp_done"], 2 * gs + p - 1)
                        for j in range(2):
                            m = mm(ps[:, S_BANK[p] + j, :], ks(i, 2 * p + j, kt * P, P), qs(i, qc, 2 * p + j, 0, 512),
                                   start=True, stop=True)
                        m.then_inc(z["qk_done"], 1)
                        if not last:
                            max_units(h + 2, i + 1, qc, range(4 * kt + 2 * p, 4 * kt + 2 * p + 2))
                    if s_ == 0:
                        if not first:
                            pv(i - 1, STEPS - 1, False)
                    else:
                        if kt == 1:
                            pe.wait_ge(z["shiftT_sb"], h + 1)
                        pv(i, s_ - 1, first)
                    if kt == 2 and not (first and qc == 0):
                        o_turn(*((i, 0) if qc else (i - 1, 1)))
                    if kt == 5:
                        if not (first and qc == 0):
                            pe.wait_ge(z["o_read"], 2 * h)
                        if qc == 0:
                            shifts(h + 1, 0)
                        elif not last:
                            shifts(h + 1, 1)

            pe.wait_ge(z["q32"], NB)
            pe.wait_ge(z["v_sb"], B * TILES // 4)
            pe.wait_ge(z["stack0_ld"], 16 * 19)
            max_units(0, 0, 0, range(32))
            pe.wait_ge(z["shift16_done"], 4)
            tr(ps[0:32, O_BANK[0], 0:64].bitcast(BF16), shift16[:].rearrange("p w j t -> p (w j t)"), ident16[:]).then_inc(z["shiftT_ps"], 1)
            max_units(1, 0, 1, range(32))
            pe.wait_ge(z["stack_ld"], 16 * 18 * (GROUPS - 1))
            body(0, True, False)
            with pe.Fori(1, GROUPS - 1) as i:
                body(i, False, False)
            body(GROUPS - 1, False, True)
            pv(GROUPS - 1, STEPS - 1, False)
            o_turn(GROUPS - 1, 1)
            for b in range(B):
                pe.wait_ge(z["o_read"], 4 * GROUPS)
                pe.wait_ge(z["exp_done"], 2 * STEPS * GROUPS)
                if b:
                    pe.wait_ge(z["gn_mmr"], 2 * b)
                for n in range(TILES):
                    m = tr(ps[:, n // 4, (n % 4) * P:(n % 4 + 1) * P], o_all[:, n, 4 * b:4 * b + 4, :].rearrange("p g n -> p (g n)"), ident[:])
                m.then_inc(z["gn_T"], 1)
                pe.wait_ge(z["gn_st"], 4 * b + 1)
                mm(ps[:, 2, 0:1], head_mean[:], st[:, 0:1], start=True, stop=True).then_inc(z["gn_mm"], 1)
                pe.wait_ge(z["gn_st"], 4 * b + 2)
                mm(ps[:, 2, 4:5], head_mean[:], st[:, 4:5], start=True, stop=True).then_inc(z["gn_mm"], 1)
                pe.wait_ge(z["gn_mmr"], 2 * b + 2)
                if b:
                    pe.wait_ge(z["y_ln"], b)
                for n in range(TILES):
                    o = ps[:, 3 + n // 4, (n % 4) * P:(n % 4 + 1) * P]
                    mm(o, normT[:, n * P:(n + 1) * P], w_attn[:, 3, :], start=True, stop=False)
                    m = mm(o, bias_sel[:], bias_of(bias_rows, "L0_attn_bo"), start=False, stop=True)
                    if n % 4 == 3:
                        m.then_inc(z["y_ps"], 1)


FH, KV, FDH = 16, 4, 64
QKV = (FH + 2 * KV) * FDH
WINDOW = 128
NT = B * TILES
BATCHES = 4
MASKED = -1e30


def window_attention(nc, t, x1, x2, ident, ident16, bias_sel, bias_rows):
    with ExitStack() as ctx:
        def sb(name, shape, dt=F32):
            return ctx.enter_context(nc.sbuf_tensor(name, shape, dt))

        w_qkv = sb("w_qkv", [P, QKV])
        w_proj = sb("w_proj", [P, 8, D])
        norm_w = sb("norm_w", [P, 1])
        sink = sb("sink", [P, FH])
        nsink = sb("nsink", [P, FH])
        rope_c = sb("rope_c", [P, TILES, FDH])
        rope_s = sb("rope_s", [P, TILES, FDH])
        mask = sb("mask", [P, 2, 512], BF16)
        sq = sb("sq", [P, D])
        rms = sb("rms", [P, NT])
        rms_in = sb("rms_in", [P, NT])
        neg_half = sb("neg_half", [P, NT])
        h_cur = sb("h_cur", [P, D])
        hT = sb("hT", [P, P])
        rot_a = sb("rot_a", [P, 2, 512])
        rot_b = sb("rot_b", [P, 2, 512])
        q_rot = sb("q_rot", [P, FH * FDH])
        k_pad = sb("k_pad", [P, KV, 2, P])
        qT = sb("qT", [P, 8, P])
        kT = sb("kT", [P, 2 * KV, (NT + 1) * P])
        v_win = sb("v_win", [P, NT + 1, KV * FDH])
        neg_max = sb("neg_max", [P, 4])
        bias = sb("bias", [P, 4, 4])
        sums = sb("sums", [P, 4, 4])
        sink_in = sb("sink_in", [P, 8])
        sink_e = sb("sink_e", [P, 8])
        den = sb("den", [P, 8])
        inv = sb("inv", [P, 8])
        probs = sb("probs", [P, 2, 4, 256])
        pT = sb("pT", [P, 2, 2, 512])
        y_sb = sb("y_sb", [P, FH * FDH])
        yT = sb("yT", [P, 8, P])
        ps = ctx.enter_context(nc.psum_tensor("ps_w", [P, 8, 512], F32))
        PROBS, Y_BANK = 4, 6
        A, W = 5, 7
        TURN = (2, 0, 1)
        QKV_BANK = (A, W, W)

        names = ("ld act_ld init rms_in rms h_done hT_ps hT_sb qkv_ps rope_a rope_read rot v_sb qT_ps qT_sb kT_ps kT_sb "
                 "s_ps negmax bias exp sink_in sink_e den inv pT_ps pT_dve pT_act pv y_norm yT_ps yT_sb proj_ps x2 sq").split()
        z = {n: ctx.enter_context(nc.semaphore("w_" + n)) for n in names}
        block = ctx.enter_context(nc.Block())

        @block.sync
        def _(sp):
            sp.dma_start(w_qkv[:], t["L0_ffn_qkv_w"][:]).then_inc(z["ld"], 16)
            sp.dma_start(norm_w[:], t["L0_ffn_attn_norm_w"].rearrange("(p a) -> p a", a=1)).then_inc(z["ld"], 16)
            sp.dma_start(rope_c[:], t["rope_c"][:]).then_inc(z["ld"], 16)
            sp.dma_start(rope_s[:], t["rope_s"][:]).then_inc(z["ld"], 16)
            sp.dma_start(mask[:, 0:2, :].rearrange("p a n -> p (a n)").bitcast(F32), t["mask"][:]).then_inc(z["ld"], 16)
            sp.dma_start(w_proj[:], t["L0_ffn_proj_w"].rearrange("(c p) n -> p c n", p=P)).then_inc(z["ld"], 16)
            sp.dma_start(sink[:], t["L0_ffn_attn_sink"].rearrange("(a n) -> a n", a=1).broadcast_to([P, FH])).then_inc(z["ld"], 16)

        @block.gpsimd
        def _(g):
            g.memset(neg_half[:], -0.5).then_inc(z["init"], 1)
            g.memset(k_pad[:], 0.0).then_inc(z["init"], 1)
            g.memset(kT[:, :, 0:P], 0.0).then_inc(z["init"], 1)
            g.memset(v_win[:, 0, :], 0.0).then_inc(z["init"], 1)
            g.wait_ge(z["ld"], 16 * 7)
            g.tensor_scalar(nsink[:], sink[:], -1.0, None, ALU.mult).then_inc(z["init"], 1)
            g.wait_ge(z["rms_in"], 1)
            g.wait_ge(z["init"], 5)
            g.tensor_tensor(rms[:], rms_in[:], neg_half[:], ALU.pow).then_inc(z["rms"], 1)

            def rotate(tile, c):
                at = TURN.index(c)
                g.wait_ge(z["rope_read"], 3 * tile + at + 1)
                a = at % 2
                if c < 2:
                    g.tensor_tensor(q_rot[:, 512 * c:512 * c + 512], rot_a[:, a, :], rot_b[:, a, :], ALU.add).then_inc(z["rot"], 1)
                else:
                    for e in range(2):
                        g.tensor_tensor(k_pad[:, :, e, FDH * e:FDH * e + FDH], rot_a[:, a, 0:256].rearrange("p (g d) -> p g d", g=KV),
                                        rot_b[:, a, 0:256].rearrange("p (g d) -> p g d", g=KV), ALU.add).then_inc(z["rot"], 1)

            def sinks(tile, hf, first):
                g.wait_ge(z["bias"], 4 * tile + 2 * hf + 2)
                g.tensor_tensor(sink_in[:], bias[:, 2 * hf:2 * hf + 2, :].rearrange("p a n -> p (a n)"), sink[:, 8 * hf:8 * hf + 8], ALU.add).then_inc(z["sink_in"], 1)
                g.wait_ge(z["sink_e"], 2 * tile + hf + 1)
                if not (first and hf == 0):
                    g.wait_ge(z["inv"], 2 * tile + hf)
                g.tensor_tensor(den[:], sink_e[:], sums[:, 2 * hf:2 * hf + 2, :].rearrange("p a n -> p (a n)"), ALU.add).then_inc(z["den"], 1)

            def prep(tile):
                for c in TURN:
                    rotate(tile, c)

            def body(tile, first, last):
                if not last:
                    rotate(tile + 1, 2)
                sinks(tile, 0, first)
                if not last:
                    rotate(tile + 1, 0)
                    rotate(tile + 1, 1)
                sinks(tile, 1, first)

            prep(0)
            body(0, True, False)
            with g.Fori(1, NT - 1) as tile:
                body(tile, False, False)
            body(NT - 1, False, True)

        @block.scalar
        def _(act):
            def hT_copy(tile):
                act.wait_ge(z["hT_ps"], tile + 1)
                nc.scalar.activation(hT[:], ps[:, A, 0:P], ACT.Copy, scale=norm_w[:, 0:1]).then_inc(z["hT_sb"], 1)

            def v_copy(tile):
                act.wait_ge(z["rope_read"], 3 * tile + 1)
                act.wait_ge(z["init"], 5)
                nc.scalar.copy(v_win[:, ds(tile + 1, 1), :].rearrange("p a n -> p (a n)"), ps[:, W, 256:512]).then_inc(z["v_sb"], 1)

            def qT_copy(tile, c):
                act.wait_ge(z["qT_ps"], 2 * tile + c + 1)
                nc.scalar.copy(qT[:, 4 * c:4 * c + 4, :].rearrange("p a n -> p (a n)"), ps[:, A, :]).then_inc(z["qT_sb"], 1)

            def kT_copy(tile, c):
                act.wait_ge(z["kT_ps"], 2 * tile + c + 1)
                nc.scalar.copy(kT[:, 4 * c:4 * c + 4, ds(tile * P + P, P)], ps[:, W, :].rearrange("p (a n) -> p a n", a=4)).then_inc(z["kT_sb"], 1)

            def exps(tile, k, js):
                kb = 4 * tile + k
                act.wait_ge(z["bias"], kb + 1)
                for j in js:
                    nc.scalar.activation(probs[:, k % 2, j, :], ps[:, 2 * (k % 2) + j // 2, 256 * (j % 2):256 * (j % 2) + 256], ACT.Exp,
                                         bias=bias[:, k, j:j + 1], scale=FDH ** -0.5, accum_out=sums[:, k, j:j + 1]).then_inc(z["exp"], 1)

            def pT_copy(tile, k):
                kb = 4 * tile + k
                act.wait_ge(z["pT_ps"], 2 * kb + 2)
                if not isinstance(kb, int) or kb > 1:
                    act.wait_ge(z["pv"], 2 * kb - 2)
                nc.scalar.copy(pT[:, k % 2, 1, :], ps[:, PROBS, :]).then_inc(z["pT_act"], 1)

            def sinks(tile, hf):
                act.wait_ge(z["sink_in"], 2 * tile + hf + 1)
                nc.scalar.activation(sink_e[:], sink_in[:], ACT.Exp).then_inc(z["sink_e"], 1)

            def yT_copy(tile, c):
                act.wait_ge(z["yT_ps"], 2 * tile + c + 1)
                nc.scalar.copy(yT[:, 4 * c:4 * c + 4, :].rearrange("p a n -> p (a n)"), ps[:, (W, A)[c], :]).then_inc(z["yT_sb"], 1)

            def body(tile, first, last):
                def slot(k):
                    kb = 4 * tile + k
                    if not (first and k < 2):
                        act.wait_ge(z["pT_ps"], 2 * kb - 2)
                    if not first:
                        act.wait_ge(z["den"], 2 * tile + k // 2 - 1)
                slot(0)
                exps(tile, 0, range(4))
                if not last:
                    hT_copy(tile + 1)
                slot(1)
                exps(tile, 1, range(4))
                pT_copy(tile, 0)
                if not last:
                    v_copy(tile + 1)
                sinks(tile, 0)
                slot(2)
                exps(tile, 2, range(4))
                pT_copy(tile, 1)
                if not first:
                    yT_copy(tile - 1, 0)
                    yT_copy(tile - 1, 1)
                slot(3)
                exps(tile, 3, range(4))
                pT_copy(tile, 2)
                sinks(tile, 1)
                if not last:
                    kT_copy(tile + 1, 0)
                    qT_copy(tile + 1, 0)
                pT_copy(tile, 3)
                if not last:
                    kT_copy(tile + 1, 1)
                    qT_copy(tile + 1, 1)

            act.wait_ge(z["ld"], 16 * 7)
            hT_copy(0)
            v_copy(0)
            for c in range(2):
                kT_copy(0, c)
                qT_copy(0, c)
            body(0, True, False)
            with act.Fori(1, NT - 1) as tile:
                body(tile, False, False)
            body(NT - 1, False, True)
            for c in range(2):
                yT_copy(NT - 1, c)

        @block.vector
        def _(v):
            for n in range(NT):
                if n:
                    v.wait_ge(z["sq"], n)
                v.tensor_tensor_reduce(out=sq[:], in0=x1[:, n, :], in1=x1[:, n, :], scale=1.0, scalar=0.0, op0=ALU.mult, op1=ALU.add,
                                       accum_out=rms_in[:, n:n + 1]).then_inc(z["sq"], 1)
            v.wait_ge(z["sq"], NT)
            v.tensor_scalar(rms_in[:], rms_in[:], 1.0 / D, EPS, ALU.mult, ALU.add).then_inc(z["rms_in"], 1)
            v.wait_ge(z["rms"], 1)
            v.wait_ge(z["ld"], 16 * 7)

            def h_of(tile, first=False):
                if not first:
                    v.wait_ge(z["hT_ps"], tile)
                v.tensor_scalar(h_cur[:], x1[:, ds(tile, 1), :].rearrange("p a n -> p (a n)"), rms[:, ds(tile, 1)], None, ALU.mult).then_inc(z["h_done"], 1)

            def rope(tile, c, first=False):
                at = TURN.index(c)
                v.wait_ge(z["qkv_ps"], 3 * tile + at + 1)
                n = 512 if c < 2 else 256
                hs = n // FDH
                a = at % 2
                if not (first and at < 2):
                    v.wait_ge(z["rot"], (4 * tile, 4 * tile - 1, 4 * tile + 2)[at])
                tl = tile % TILES
                src = ps[:, QKV_BANK[c], 0:n].rearrange("p (h d) -> p h d", h=hs)
                ct = rope_c[:, ds(tl, 1), :].broadcast_to([P, hs, FDH])
                st = rope_s[:, ds(tl, 1), :].broadcast_to([P, hs, FDH])
                v.tensor_tensor(rot_a[:, a, 0:n].rearrange("p (h d) -> p h d", h=hs), src, ct, ALU.mult).then_inc(z["rope_a"], 1)
                src = ps[:, QKV_BANK[c], 0:n].rearrange("p (h d e) -> p h d e", h=hs, e=2)
                dst = rot_b[:, a, 0:n].rearrange("p (h d e) -> p h d e", h=hs, e=2)
                stp = st.rearrange("p h (d e) -> p h d e", e=2)
                v.tensor_tensor(dst[:, :, :, 0], src[:, :, :, 1], stp[:, :, :, 0], ALU.mult).then_inc(z["rope_a"], 1)
                v.tensor_tensor(dst[:, :, :, 1], src[:, :, :, 0], stp[:, :, :, 1], ALU.mult).then_inc(z["rope_read"], 1)

            def maxima(tile, k, first=False):
                kb = 4 * tile + k
                v.wait_ge(z["s_ps"], kb + 1)
                if not isinstance(kb, int) or kb:
                    v.wait_ge(z["bias"], kb)
                v.tensor_reduce(neg_max[:], ps[:, 2 * (k % 2):2 * (k % 2) + 2, :].rearrange("p b (e n) -> p (b e) n", e=2), AX.X, ALU.max,
                                negate=True).then_inc(z["negmax"], 1)
                v.wait_ge(z["negmax"], kb + 1)
                if not (first and k < 4):
                    v.wait_ge(z["den"], 2 * (tile - 1) + k // 2 + 1)
                v.scalar_tensor_tensor(bias[:, k, :], neg_max[:], FDH ** -0.5, nsink[:, 4 * k:4 * k + 4], ALU.mult, ALU.min).then_inc(z["bias"], 1)

            def pT_copy(tile, k):
                kb = 4 * tile + k
                v.wait_ge(z["pT_ps"], 2 * kb + 1)
                if not isinstance(kb, int) or kb > 1:
                    v.wait_ge(z["pv"], 2 * kb - 3)
                v.tensor_copy(pT[:, k % 2, 0, :], ps[:, PROBS, :]).then_inc(z["pT_dve"], 1)

            def y_norm(tile, hf):
                v.wait_ge(z["den"], 2 * tile + hf + 1)
                if not isinstance(tile, int) or 2 * tile + hf:
                    v.wait_ge(z["y_norm"], 2 * tile + hf)
                v.reciprocal(inv[:], den[:]).then_inc(z["inv"], 1)
                v.wait_ge(z["inv"], 2 * tile + hf + 1)
                v.wait_ge(z["pv"], 8 * tile + 4 * hf + 4)
                v.tensor_tensor(y_sb[:, 512 * hf:512 * hf + 512].rearrange("p (h d) -> p h d", h=8), ps[:, Y_BANK, :].rearrange("p (h d) -> p h d", h=8),
                                inv[:].unsqueeze(2).broadcast_to([P, 8, FDH]), ALU.mult).then_inc(z["y_norm"], 1)

            def residual(tile):
                v.wait_ge(z["proj_ps"], tile + 1)
                v.tensor_tensor(x2[:, ds(tile, 1), :].rearrange("p a n -> p (a n)"), ps[:, A, 0:P],
                                x1[:, ds(tile, 1), :].rearrange("p a n -> p (a n)"), ALU.add).then_inc(z["x2"], 1)

            def body(tile, first, last):
                if not last:
                    h_of(tile + 1)
                maxima(tile, 1, first)
                if not first:
                    y_norm(tile - 1, 1)
                pT_copy(tile, 0)
                if not last:
                    rope(tile + 1, 2)
                maxima(tile, 2, first)
                pT_copy(tile, 1)
                if not last:
                    rope(tile + 1, 0)
                maxima(tile, 3, first)
                pT_copy(tile, 2)
                if not last:
                    rope(tile + 1, 1)
                y_norm(tile, 0)
                if not first:
                    residual(tile - 1)
                pT_copy(tile, 3)
                if not last:
                    maxima(tile + 1, 0)

            h_of(0, True)
            for c in TURN:
                rope(0, c, True)
            maxima(0, 0, True)
            body(0, True, False)
            with v.Fori(1, NT - 1) as tile:
                body(tile, False, False)
            body(NT - 1, False, True)
            y_norm(NT - 1, 1)
            residual(NT - 1)

        @block.tensor
        def _(pe):
            mm = nc.tensor.matmul
            tr = nc.tensor.transpose

            def hT_of(tile):
                pe.wait_ge(z["h_done"], tile + 1)
                tr(ps[:, A, 0:P], h_cur[:], ident[:]).then_inc(z["hT_ps"], 1)

            def qkv(tile, c):
                pe.wait_ge(z["hT_sb"], tile + 1)
                o = ps[:, QKV_BANK[c], :]
                mm(o, hT[:], w_qkv[:, 512 * c:512 * c + 512], start=True, stop=False)
                mm(o, bias_sel[:], bias_of(bias_rows, "L0_ffn_qkv_b", 512 * c, 512), start=False, stop=True).then_inc(z["qkv_ps"], 1)

            def qT_of(tile, c):
                pe.wait_ge(z["rot"], 4 * tile + 3 + c)
                for n in range(4):
                    m = tr(ps[:, A, n * P:(n + 1) * P], q_rot[:, (4 * c + n) * P:(4 * c + n + 1) * P], ident[:])
                m.then_inc(z["qT_ps"], 1)

            def kT_of(tile, c):
                pe.wait_ge(z["rot"], 4 * tile + 2)
                for n in range(4):
                    m = tr(ps[:, W, n * P:(n + 1) * P], k_pad[:, 2 * c + n // 2, n % 2, :], ident[:])
                m.then_inc(z["kT_ps"], 1)

            def scores(tile, k, first=False):
                kb = 4 * tile + k
                if not (first and k < 2):
                    pe.wait_ge(z["exp"], 4 * kb - 4)
                pe.wait_ge(z["qT_sb"], 2 * tile + 1 + k // 2)
                pe.wait_ge(z["kT_sb"], 2 * tile + 1 + k // 2)
                for n in range(2):
                    o = ps[:, 2 * (k % 2) + n, :]
                    mm(o, qT[:, 2 * k + n, :], kT[:, 2 * k:2 * k + 2, ds(tile * P, 2 * P)], start=True, stop=False)
                    m = mm(o, ident16[:], mask[:, ds((tile % TILES + TILES - 1) // TILES, 1), :].rearrange("p a n -> p (a n)"), start=False, stop=True)
                m.then_inc(z["s_ps"], 1)

            def turn_probs(tile, k, c):
                kb = 4 * tile + k
                pe.wait_ge(z["exp"], 4 * kb + 2 * c + 2)
                if c:
                    pe.wait_ge(z["pT_dve"], kb + 1)
                elif not isinstance(kb, int) or kb:
                    pe.wait_ge(z["pT_act"], kb)
                for n in range(4):
                    m = tr(ps[:, PROBS, n * P:(n + 1) * P], probs[:, k % 2, 2 * c + n // 2, (n % 2) * P:(n % 2 + 1) * P], ident[:])
                m.then_inc(z["pT_ps"], 1)

            def pv(tile, k, c):
                kb = 4 * tile + k
                if c == 0 and k % 2 == 0 and (not isinstance(kb, int) or kb):
                    pe.wait_ge(z["y_norm"], 2 * tile + k // 2)
                pe.wait_ge(z["pT_act" if c else "pT_dve"], kb + 1)
                for j in range(2):
                    h = 4 * (k % 2) + 2 * c + j
                    for w in range(2):
                        m = mm(ps[:, Y_BANK, h * FDH:(h + 1) * FDH], pT[:, k % 2, c, (2 * j + w) * P:(2 * j + w + 1) * P],
                               v_win[:, ds(tile + w, 1), k * FDH:(k + 1) * FDH].rearrange("p a n -> p (a n)"), start=(w == 0), stop=(w == 1))
                m.then_inc(z["pv"], 1)

            def yT_of(tile, c):
                pe.wait_ge(z["y_norm"], 2 * tile + 2)
                for n in range(4):
                    m = tr(ps[:, (W, A)[c], n * P:(n + 1) * P], y_sb[:, (4 * c + n) * P:(4 * c + n + 1) * P], ident[:])
                m.then_inc(z["yT_ps"], 1)

            def project(tile):
                pe.wait_ge(z["yT_sb"], 2 * tile + 2)
                for c in range(8):
                    mm(ps[:, A, 0:P], yT[:, c, :], w_proj[:, c, :], start=(c == 0), stop=False)
                mm(ps[:, A, 0:P], bias_sel[:], bias_of(bias_rows, "L0_ffn_proj_b"), start=False, stop=True).then_inc(z["proj_ps"], 1)

            def body(tile, first, last):
                nxt, prev = tile + 1, tile - 1
                scores(tile, 1, first)
                pe.wait_ge(z["qT_sb"], 2 * tile + 2)
                if not last:
                    hT_of(nxt)
                if not first:
                    pv(prev, 3, 0)
                    pv(prev, 3, 1)
                turn_probs(tile, 0, 0)
                pe.wait_ge(z["kT_sb"], 2 * tile + 2)
                if not last:
                    qkv(nxt, 2)
                turn_probs(tile, 0, 1)

                scores(tile, 2, first)
                if not last:
                    qkv(nxt, 0)
                turn_probs(tile, 1, 0)
                pv(tile, 0, 0)
                turn_probs(tile, 1, 1)
                pv(tile, 0, 1)
                if not last:
                    pe.wait_ge(z["rope_read"], 3 * nxt + 1)
                    pe.wait_ge(z["v_sb"], nxt + 1)
                if not first:
                    yT_of(prev, 0)

                scores(tile, 3, first)
                if not last:
                    pe.wait_ge(z["rope_read"], 3 * nxt + 2)
                if not first:
                    yT_of(prev, 1)
                turn_probs(tile, 2, 0)
                pv(tile, 1, 0)
                turn_probs(tile, 2, 1)
                if not last:
                    if not first:
                        pe.wait_ge(z["yT_sb"], 2 * prev + 1)
                    qkv(nxt, 1)
                pv(tile, 1, 1)
                if not first:
                    project(prev)

                if not last:
                    pe.wait_ge(z["rope_read"], 3 * nxt + 3)
                    kT_of(nxt, 0)
                turn_probs(tile, 3, 0)
                pv(tile, 2, 0)
                if not first:
                    pe.wait_ge(z["x2"], prev + 1)
                if not last:
                    qT_of(nxt, 0)
                turn_probs(tile, 3, 1)
                pv(tile, 2, 1)
                if not last:
                    pe.wait_ge(z["kT_sb"], 2 * nxt + 1)
                    kT_of(nxt, 1)
                    scores(nxt, 0)
                    pe.wait_ge(z["qT_sb"], 2 * nxt + 1)
                    qT_of(nxt, 1)

            pe.wait_ge(z["ld"], 16 * 7)
            pe.wait_ge(z["init"], 5)
            hT_of(0)
            qkv(0, 2)
            qkv(0, 0)
            pe.wait_ge(z["rope_read"], 1)
            pe.wait_ge(z["v_sb"], 1)
            qkv(0, 1)
            pe.wait_ge(z["rope_read"], 3)
            kT_of(0, 0)
            qT_of(0, 0)
            pe.wait_ge(z["kT_sb"], 1)
            kT_of(0, 1)
            scores(0, 0, True)
            pe.wait_ge(z["qT_sb"], 1)
            qT_of(0, 1)
            body(0, True, False)
            with pe.Fori(1, NT - 1) as tile:
                body(tile, False, False)
            body(NT - 1, False, True)
            pv(NT - 1, 3, 0)
            pv(NT - 1, 3, 1)
            yT_of(NT - 1, 0)
            yT_of(NT - 1, 1)
            project(NT - 1)


E, TOPK, DFF = 32, 4, 128
UP2 = 2 * DFF
BLK = 512
BT = BLK // P
BLOCKS = B * S // BLK
AHEAD = 4
PER_LOAD = 4
F32R = mybir.dt.float32r


def experts(nc, t, x1, x2, ident, ident16, bias_sel, bias_rows, out):
    with ExitStack() as ctx:
        def sb(name, shape, dt=F32):
            return ctx.enter_context(nc.sbuf_tensor(name, shape, dt))

        w_raw = sb("w_raw", [P, 2, PER_LOAD, UP2 + D])
        w_hi = sb("w_hi", [P, E, UP2 + D], F32R)
        w_lo = sb("w_lo", [P, E, UP2 + D], F32R)
        w_gate = sb("w_gate", [P, E])
        norm_w = sb("norm_w2", [P, 1])
        expert_id = sb("expert_id", [P, E])
        expert_sel = sb("expert_sel", [3 * E, E, P], BF16)
        sq = sb("sq2", [P, 2, D])
        ms = sb("ms2", [P, NT])
        rms = sb("rms2", [P, NT])
        neg_half = sb("neg_half2", [P, NT])
        h2 = sb("h2", [P, NT, D])
        h2T = sb("h2T", [P, B * S])
        h2T_hi = sb("h2T_hi", [P, B * S], F32R)
        h2T_lo = sb("h2T_lo", [P, B * S], F32R)
        logits = sb("logits", [P, NT, E])
        top = sb("top", [P, NT, 8])
        top_i = sb("top_i", [P, NT, 8], mybir.dt.uint32)
        top_f = sb("top_f", [P, NT, 8])
        gates = sb("gates", [P, NT, TOPK])
        gate_sum = sb("gate_sum", [P, NT])
        share = sb("share", [P, NT, E])
        share3 = sb("share3", [P, NT, 3, E], BF16)
        shareT = sb("shareT", [3 * E, B * S], BF16)
        act_hi = sb("act_hi", [P, 4, BLK], F32R)
        act_lo = sb("act_lo", [P, 4, BLK], F32R)
        hit = h2[:, 0:2 * NT * E // D, :].rearrange("p a d -> p (a d)").rearrange("p (a t e) -> p a t e", a=2, e=E)
        x1_free = x1[:].rearrange("p t d -> p (t d)").rearrange("p (a n) -> p a n", n=BLK)
        silu, act = x1_free[:, 0:2, :], x1_free[:, 2:4, :]
        h2T_free = h2T[:].rearrange("p (a n) -> p a n", n=BLK)
        gated, yT = h2T_free[:, 0:2, :], h2T_free[:, 2, :]
        stats = sb("stats2", [P, BT, 6])
        mv = sb("mv2", [P, BT, 2])
        rstd = sb("rstd2", [P, BT])
        ps = ctx.enter_context(nc.psum_tensor("ps_e", [P, 8, 512], F32))
        U, G, SH, Y, MISC = (0, 1), (2, 3), (4, 5), 6, 7

        names = ("ld_norm ld_gate ld_id ld_sel ld_w0 ld_w1 init sq ms rms h2 h2T_ps h2T_sb h2T_hi h2T_lo logits_ps top chain gexp gates "
                 "share3 shareT_ps shareT_sb w_hi w_lo g_ps sh_ps u_ps silu gated act act_hi act_lo down "
                 "yT y_ps x12 x3 stats var rstd final outd").split()
        z = {n: ctx.enter_context(nc.semaphore("e_" + n)) for n in names}
        block = ctx.enter_context(nc.Block())

        @block.sync
        def _(sp):
            sp.dma_start(norm_w[:], t["L0_ffn_ffn_norm_w"].rearrange("(p a) -> p a", a=1)).then_inc(z["ld_norm"], 16)
            sp.dma_start(w_gate[:], t["L0_ffn_gate_w"][:]).then_inc(z["ld_gate"], 16)
            sp.dma_start(expert_id[:], t["expert_id"][:]).then_inc(z["ld_id"], 16)
            for c in range(E // PER_LOAD):
                es = slice(c * PER_LOAD, (c + 1) * PER_LOAD)
                if c >= 2:
                    sp.wait_ge(z["w_lo"], (c - 1) * PER_LOAD)
                sp.dma_start(w_raw[:, c % 2, :, 0:UP2], t["L0_ffn_W_up"][es].rearrange("e p n -> p e n")).then_inc(z[f"ld_w{c % 2}"], 16)
                sp.dma_start(w_raw[:, c % 2, :, UP2:UP2 + D], t["L0_ffn_W_down"][es].rearrange("e p n -> p e n")).then_inc(z[f"ld_w{c % 2}"], 16)
                if c == 0:
                    sp.dma_start(expert_sel[:].rearrange("p e n -> p (e n)").bitcast(F32), t["expert_sel"][:]).then_inc(z["ld_sel"], 16)
            for b in range(BLOCKS):
                sp.wait_ge(z["final"], BT * (b + 1))
                sp.dma_start(out[b * BLK // S, b * BLK % S:b * BLK % S + BLK, :].rearrange("(t p) d -> p t d", p=P),
                             x2[:, b * BT:(b + 1) * BT, :]).then_inc(z["outd"], 16)
            sp.wait_ge(z["outd"], 16 * BLOCKS)

        @block.gpsimd
        def _(g):
            g.memset(neg_half[:], -0.5).then_inc(z["init"], 1)
            g.wait_ge(z["init"], 1)
            g.wait_ge(z["ms"], 1)
            g.tensor_tensor(rms[:], ms[:], neg_half[:], ALU.pow).then_inc(z["rms"], 1)
            g.wait_ge(z["h2"], NT)
            g.tensor_tensor(x2[:], x2[:], x1[:], ALU.add).then_inc(z["x12"], 1)

            def low(b, e, first):
                n = b * E + e
                g.wait_ge(z["act_hi"], n + 1)
                if not (first and e < 4):
                    g.wait_ge(z["down"], n - 3)
                g.tensor_tensor(act_lo[:, e % 4, :], act[:, e % 2, :], act_hi[:, e % 4, :], ALU.subtract).then_inc(z["act_lo"], 1)

            def norm(b):
                g.wait_ge(z["var"], b + 1)
                g.tensor_tensor(rstd[:], mv[:, :, 1], neg_half[:, 0:BT], ALU.pow).then_inc(z["rstd"], 1)

            def body(b, first):
                for e in range(E):
                    low(b, e, first)
                    if e == 7 and not first:
                        norm(b - 1)

            body(0, True)
            with g.Fori(1, BLOCKS) as b:
                body(b, False)
            norm(BLOCKS - 1)

        @block.scalar
        def _(act_e):
            def split(e):
                c = e // PER_LOAD
                act_e.wait_ge(z[f"ld_w{c % 2}"], 32 * (c // 2 + 1))
                nc.scalar.copy(w_hi[:, e, :], w_raw[:, c % 2, e % PER_LOAD, :]).then_inc(z["w_hi"], 1)

            act_e.wait_ge(z["ld_norm"], 16)
            for c in range(BLOCKS):
                act_e.wait_ge(z["h2T_ps"], c + 1)
                nc.scalar.activation(h2T[:, BLK * c:BLK * c + BLK], ps[:, c, :], ACT.Copy, scale=norm_w[:, 0:1]).then_inc(z["h2T_sb"], 1)
            for c in range(BLOCKS):
                act_e.wait_ge(z["h2T_sb"], c + 1)
                nc.scalar.copy(h2T_hi[:, BLK * c:BLK * c + BLK], h2T[:, BLK * c:BLK * c + BLK]).then_inc(z["h2T_hi"], 1)
            for e in range(AHEAD):
                split(e)
            act_e.wait_ge(z["gates"], 1)
            nc.scalar.activation(gates[:], gates[:], ACT.Exp).then_inc(z["gexp"], 1)
            for c in range(2):
                act_e.wait_ge(z["shareT_ps"], c + 1)
                nc.scalar.copy(shareT[:, 1024 * c:1024 * c + 1024], ps[0:3 * E, SH[c], :].bitcast(BF16)).then_inc(z["shareT_sb"], 1)

            act_e.wait_ge(z["x12"], 1)

            def high(n, e, first):
                act_e.wait_ge(z["act"], n + 1)
                if not (first and e < 4):
                    act_e.wait_ge(z["down"], n - 3)
                nc.scalar.copy(act_hi[:, e % 4, :], act[:, e % 2, :]).then_inc(z["act_hi"], 1)

            def y_copy(b):
                act_e.wait_ge(z["down"], E * (b + 1))
                if not isinstance(b, int) or b:
                    act_e.wait_ge(z["y_ps"], b)
                nc.scalar.copy(yT, ps[:, Y, :]).then_inc(z["yT"], 1)

            def body(b, first):
                for e in range(E):
                    n = b * E + e
                    act_e.wait_ge(z["g_ps"], n + 1)
                    if not (first and e < 2):
                        act_e.wait_ge(z["gated"], n - 1)
                    nc.scalar.activation(silu[:, e % 2, :], ps[:, G[e % 2], :], ACT.Silu).then_inc(z["silu"], 1)
                    if e == 2 and not first:
                        y_copy(b - 1)
                    if not (first and e == 0):
                        high(n - 1, (e - 1) % E, first)
                    if first and e + AHEAD < E:
                        split(e + AHEAD)

            body(0, True)
            with act_e.Fori(1, BLOCKS) as b:
                body(b, False)
            high(BLOCKS * E - 1, E - 1, False)
            y_copy(BLOCKS - 1)

        @block.vector
        def _(v):
            cnt = [0]

            def chain(ins):
                cnt[0] += 1
                ins.then_inc(z["chain"], 1)
                v.wait_ge(z["chain"], cnt[0])

            def split(e):
                v.wait_ge(z["w_hi"], e + 1)
                v.tensor_tensor(w_lo[:, e, :], w_raw[:, e // PER_LOAD % 2, e % PER_LOAD, :], w_hi[:, e, :], ALU.subtract).then_inc(z["w_lo"], 1)

            for n in range(NT):
                if n >= 2:
                    v.wait_ge(z["sq"], n - 1)
                v.tensor_tensor_reduce(out=sq[:, n % 2, :], in0=x2[:, n, :], in1=x2[:, n, :], scale=1.0, scalar=0.0, op0=ALU.mult, op1=ALU.add,
                                       accum_out=ms[:, n:n + 1]).then_inc(z["sq"], 1)
            v.wait_ge(z["sq"], NT)
            v.tensor_scalar(ms[:], ms[:], 1.0 / D, EPS, ALU.mult, ALU.add).then_inc(z["ms"], 1)
            v.wait_ge(z["rms"], 1)
            for n in range(NT):
                v.tensor_scalar(h2[:, n, :], x2[:, n, :], rms[:, n:n + 1], None, ALU.mult).then_inc(z["h2"], 1)
            for c in range(BLOCKS):
                v.wait_ge(z["h2T_hi"], c + 1)
                v.tensor_tensor(h2T_lo[:, BLK * c:BLK * c + BLK], h2T[:, BLK * c:BLK * c + BLK], h2T_hi[:, BLK * c:BLK * c + BLK],
                                ALU.subtract).then_inc(z["h2T_lo"], 1)
            v.wait_ge(z["logits_ps"], 1)
            chain(v.tensor_copy(logits[:].rearrange("p t e -> p (t e)"), ps[:, MISC, :]))
            for n in range(NT):
                v.max(top[:, n, :], logits[:, n, :]).then_inc(z["top"], 1)
            v.wait_ge(z["top"], NT)
            v.tensor_tensor(gates[:], top[:, :, 0:TOPK], top[:, :, 0:1].broadcast_to([P, NT, TOPK]), ALU.subtract).then_inc(z["gates"], 1)
            for n in range(NT):
                v.max_index(top_i[:, n, :], top[:, n, :], logits[:, n, :]).then_inc(z["top"], 1)
            v.wait_ge(z["top"], 2 * NT)
            chain(v.tensor_copy(top_f[:], top_i[:]))
            v.wait_ge(z["gexp"], 1)
            chain(v.tensor_reduce(gate_sum[:], gates[:], AX.X, ALU.add))
            chain(v.reciprocal(gate_sum[:], gate_sum[:]))
            chain(v.tensor_tensor(gates[:], gates[:], gate_sum[:].unsqueeze(2).broadcast_to([P, NT, TOPK]), ALU.mult))
            v.wait_ge(z["ld_id"], 16)
            for k in range(TOPK):
                chain(v.tensor_tensor(hit[:, 0, :, :], expert_id[:].unsqueeze(1).broadcast_to([P, NT, E]),
                                      top_f[:, :, k:k + 1].broadcast_to([P, NT, E]), ALU.is_equal))
                dst = share[:] if k == 0 else hit[:, 1, :, :]
                chain(v.tensor_tensor(dst, hit[:, 0, :, :], gates[:, :, k:k + 1].broadcast_to([P, NT, E]), ALU.mult))
                if k:
                    chain(v.tensor_tensor(share[:], share[:], hit[:, 1, :, :], ALU.add))
            chain(v.tensor_copy(share3[:, :, 0, :], share[:]))
            chain(v.tensor_tensor(share[:], share[:], share3[:, :, 0, :], ALU.subtract))
            chain(v.tensor_copy(share3[:, :, 1, :], share[:]))
            v.tensor_tensor(share3[:, :, 2, :], share[:], share3[:, :, 1, :], ALU.subtract).then_inc(z["share3"], 1)
            for e in range(AHEAD):
                split(e)

            def residual(b):
                v.wait_ge(z["y_ps"], b + 1)
                x = x2[:, ds(b * BT, BT), :].rearrange("p a n -> p (a n)")
                v.tensor_tensor(x, x, ps[:, MISC, :], ALU.add).then_inc(z["x3"], 1)

            def moments(b):
                v.wait_ge(z["x3"], b + 1)
                for k in range(BT):
                    v.bn_stats(stats[:, k, :], x2[:, ds(b * BT + k, 1), :].rearrange("p a n -> p (a n)")).then_inc(z["stats"], 1)

            def aggregate(b):
                for k in range(BT):
                    v.bn_aggr(mv[:, k, :], stats[:, k, :]).then_inc(z["stats"], 1)

            def variance(b):
                v.wait_ge(z["stats"], (2 * b + 2) * BT)
                v.tensor_scalar(mv[:, :, 1], mv[:, :, 1], EPS, None, ALU.add).then_inc(z["var"], 1)

            def normalise(b):
                v.wait_ge(z["rstd"], b + 1)
                for k in range(BT):
                    x = x2[:, ds(b * BT + k, 1), :].rearrange("p a n -> p (a n)")
                    v.tensor_scalar(x, x, mv[:, k, 0:1], rstd[:, k:k + 1], ALU.subtract, ALU.mult).then_inc(z["final"], 1)

            closing = {4: residual, 5: moments, 6: aggregate, 7: variance, 9: normalise}

            def body(b, first):
                for e in range(E):
                    n = b * E + e
                    if closing.get(e) is aggregate and not first:
                        v.wait_ge(z["stats"], (2 * b - 1) * BT)
                    v.wait_ge(z["silu"], n + 1)
                    v.wait_ge(z["sh_ps"], n + 1)
                    if not (first and e < 2):
                        v.wait_ge(z["act"], n - 1)
                    v.tensor_tensor(gated[:, e % 2, :], silu[:, e % 2, :], ps[:, SH[e % 2], :], ALU.mult).then_inc(z["gated"], 1)
                    v.wait_ge(z["gated"], n + 1)
                    v.wait_ge(z["u_ps"], n + 1)
                    if not (first and e < 2):
                        v.wait_ge(z["act_lo"], n - 1)
                    v.tensor_tensor(act[:, e % 2, :], gated[:, e % 2, :], ps[:, U[e % 2], :], ALU.mult).then_inc(z["act"], 1)
                    if first and e + AHEAD < E:
                        split(e + AHEAD)
                    if e in closing and not first:
                        closing[e](b - 1)

            v.wait_ge(z["x12"], 1)
            body(0, True)
            with v.Fori(1, BLOCKS) as b:
                body(b, False)
            for step in closing.values():
                if step is aggregate:
                    v.wait_ge(z["stats"], (2 * BLOCKS - 1) * BT)
                step(BLOCKS - 1)

        @block.tensor
        def _(pe):
            mm = nc.tensor.matmul
            tr = nc.tensor.transpose
            for n in range(NT):
                pe.wait_ge(z["h2"], n + 1)
                m = tr(ps[:, n // BT, (n % BT) * P:(n % BT + 1) * P], h2[:, n, :], ident[:])
                if n % BT == BT - 1:
                    m.then_inc(z["h2T_ps"], 1)
            pe.wait_ge(z["ld_gate"], 16)
            for n in range(NT):
                if n % BT == 0:
                    pe.wait_ge(z["h2T_sb"], n // BT + 1)
                o = ps[:, MISC, n * E:(n + 1) * E]
                mm(o, h2T[:, n * P:(n + 1) * P], w_gate[:], start=True, stop=False)
                m = mm(o, bias_sel[:], bias_of(bias_rows, "L0_ffn_gate_b"), start=False, stop=True)
            m.then_inc(z["logits_ps"], 1)
            pe.wait_ge(z["share3"], 1)
            for n in range(NT):
                m = tr(ps[0:3 * E, SH[n // 8], 64 * (n % 8):64 * (n % 8) + 64].bitcast(BF16), share3[:, n, :, :].rearrange("p a e -> p (a e)"), ident16[:])
                if n % 8 == 7:
                    m.then_inc(z["shareT_ps"], 1)
            pe.wait_ge(z["shareT_sb"], 2)
            pe.wait_ge(z["ld_sel"], 16)

            def up(b, e, w, bank, done):
                at = slice(w * DFF, w * DFF + DFF)
                hi, lo = h2T_hi[:, ds(b * BLK, BLK)], h2T_lo[:, ds(b * BLK, BLK)]
                o = ps[:, bank[e % 2], :]
                mm(o, w_hi[:, e, at], hi, start=True, stop=False)
                mm(o, w_hi[:, e, at], lo, start=False, stop=False)
                mm(o, w_lo[:, e, at], hi, start=False, stop=True).then_inc(z[done], 1)

            def down(n, e, first):
                pe.wait_ge(z["act_hi"], n + 1)
                w = slice(UP2, UP2 + D)
                mm(ps[:, Y, :], w_lo[:, e, w], act_hi[:, e % 4, :], start=(e == 0), stop=False)
                mm(ps[:, Y, :], w_hi[:, e, w], act_hi[:, e % 4, :], start=False, stop=False)
                pe.wait_ge(z["act_lo"], n + 1)
                mm(ps[:, Y, :], w_hi[:, e, w], act_lo[:, e % 4, :], start=False, stop=(e == E - 1)).then_inc(z["down"], 1)

            def turn(b):
                pe.wait_ge(z["yT"], b + 1)
                for k in range(BT):
                    m = tr(ps[:, MISC, k * P:(k + 1) * P], yT[:, k * P:(k + 1) * P], ident[:])
                m.then_inc(z["y_ps"], 1)

            def body(b, first):
                for e in range(E):
                    n = b * E + e
                    if first:
                        pe.wait_ge(z["w_lo"], e + 1)
                    if not (first and e < 2):
                        pe.wait_ge(z["silu"], n - 1)
                    up(b, e, 1, G, "g_ps")
                    if not (first and e < 2):
                        pe.wait_ge(z["gated"], n - 1)
                    mm(ps[:, SH[e % 2], :], expert_sel[:, e, :], shareT[:, ds(b * BLK, BLK)], start=True, stop=True).then_inc(z["sh_ps"], 1)
                    if not (first and e < 2):
                        pe.wait_ge(z["act"], n - 1)
                    up(b, e, 0, U, "u_ps")
                    if not (first and e < 2):
                        if e == 2 and not first:
                            pe.wait_ge(z["yT"], b)
                        down(n - 2, (e - 2) % E, first)
                    if e == 3 and not first:
                        if not isinstance(b, int):
                            pe.wait_ge(z["x3"], b - 1)
                        turn(b - 1)

            pe.wait_ge(z["h2T_lo"], BLOCKS)
            body(0, True)
            body(1, False)
            with pe.Fori(2, BLOCKS) as b:
                body(b, False)
            for n in (BLOCKS * E - 2, BLOCKS * E - 1):
                down(n, n % E, False)
            pe.wait_ge(z["x3"], BLOCKS - 1)
            turn(BLOCKS - 1)

def build(nc, t, out):
    with ExitStack() as ctx:
        def sb(name, shape, dt=F32):
            return ctx.enter_context(nc.sbuf_tensor(name, shape, dt))
        x1 = sb("x1", [P, B * TILES, D])
        ident = sb("ident", [P, P])
        ident16 = sb("ident16", [P, P], BF16)
        bias_sel = sb("bias_sel", [P, P], BF16)
        bias_rows = sb("bias_rows", [P, BIASES], BF16)
        differential_attention(nc, t, x1, ident, ident16, bias_sel, bias_rows)
        x2 = sb("x2", [P, B * TILES, D])
        window_attention(nc, t, x1, x2, ident, ident16, bias_sel, bias_rows)
        experts(nc, t, x1, x2, ident, ident16, bias_sel, bias_rows, out)


def constants():
    c = {}
    c["ident"] = np.eye(P, dtype=np.float32)
    c["head_mean"] = np.kron(np.eye(H, dtype=np.float32), np.full((DH, DH), 1.0 / DH, np.float32))
    c["bias_sel"] = np.repeat((np.arange(P) < 3).astype(np.float32)[:, None], P, axis=1)
    c["ones16"] = np.full((2, GROUPS * HG * S // 2), 0x3F803F80, np.uint32).view(np.float32)
    pos = np.arange(S, dtype=np.float32) / np.float32(32.0)
    inv = (1.0 / np.float32(150000.0) ** (np.arange(0, FDH, 2, dtype=np.float32) / np.float32(FDH))).astype(np.float32)
    f = pos[:, None] * inv[None, :]
    cos = np.repeat(np.cos(f), 2, axis=1).astype(np.float32)
    sin = np.stack([-np.sin(f), np.sin(f)], axis=2).reshape(S, FDH).astype(np.float32)
    c["rope_c"] = cos.reshape(TILES, P, FDH).transpose(1, 0, 2)
    c["rope_s"] = sin.reshape(TILES, P, FDH).transpose(1, 0, 2)
    p, k = np.arange(P)[:, None], np.arange(2 * P)[None, :]
    seen = (k >= p) & (k <= p + WINDOW)
    first = seen & (k >= P)
    masked = np.array(MASKED, np.float32).view(np.uint32) >> 16
    m = np.stack([np.where(x, 0, masked).astype(np.uint16) for x in (first, first, seen, seen)], axis=1)
    c["mask"] = m.reshape(P, 8 * P).view(np.float32)
    c["expert_id"] = np.tile(np.arange(E, dtype=np.float32), (P, 1))
    c["expert_sel"] = np.tile(np.repeat(np.eye(E, dtype=np.uint32) * np.uint32(0x3F803F80), P // 2, axis=1), (3, 1)).view(np.float32)
    return c


def kernel(**inputs):
    import concourse.bacc as bacc
    from concourse.bass_utils import run_bass_kernel_spmd

    nc = bacc.Bacc("TRN2", target_bir_lowering=False, num_devices=1)
    nc.disable_value_cache = True
    arrays, t = {}, {}
    for name, a in {**inputs, **constants()}.items():
        a = np.ascontiguousarray(a)
        arrays["in_" + name] = a
        t[name] = nc.dram_tensor("in_" + name, a.shape, mybir.dt.from_np(a.dtype), kind="ExternalInput").ap()
    out = nc.dram_tensor("out_dram", (B, S, D), F32, kind="ExternalOutput").ap()
    build(nc, t, out)
    r = run_bass_kernel_spmd(nc, [arrays], core_ids=[0])
    return r.results[0]["out_dram"]
```

```python
from contextlib import ExitStack

import numpy as np

import concourse.bass as bass
from concourse import mybir

F32 = mybir.dt.float32
BF16 = mybir.dt.bfloat16
F32R = mybir.dt.float32r
ALU = mybir.AluOpType
ACT = mybir.ActivationFunctionType
AX = mybir.AxisListType

B, S, D, H = 2, 1024, 128, 16
DH = D // H
P = 128
TILES = S // P
HG = 4
GROUPS = B * H // HG
EPS = 1e-5
LAMBDA_INIT = 0.8
QK_ROWS = 96
PARTS_Q = (0, 0, 1, 0, 2, 1)
PARTS_K = (0, 1, 0, 2, 0, 1)
SHIFT_ROW = len(PARTS_Q) * DH
STACK_LOADS = 1 + 3 * len(PARTS_Q)
SLOTS = 3
ONES = HG * S // 2
UNITS = HG * 8
UNITS_AHEAD = 16
STEPS = 2 * TILES
ds = bass.ds


BIAS_AT, BIASES = {}, 0
for _name, _n in (("L0_attn_bv", D), ("L0_attn_bo", D), ("L0_ffn_qkv_b", 1536), ("L0_ffn_proj_b", D), ("L0_ffn_gate_b", 32)):
    BIAS_AT[_name] = (BIASES, _n)
    BIASES += _n


def bias_of(bias_rows, name, start=0, size=None):
    a, n = BIAS_AT[name]
    return bias_rows[:, a + start:a + start + (size or n)]


def differential_attention(nc, t, x1, ident, ident16, bias_sel, bias_rows, load_next):
    with ExitStack() as ctx:
        def sb(name, shape, dt=F32):
            return ctx.enter_context(nc.sbuf_tensor(name, shape, dt))

        def sem(name):
            return ctx.enter_context(nc.semaphore(name))

        qk_parts = nc.dram_tensor("qk_parts", [2, 3, P, B * S], BF16, kind="Internal")

        x_in = x1
        xT = sb("xT", [P, B * S])
        w_attn = sb("w_attn", [P, 4, D])
        head_mean = sb("head_mean", [P, P])
        cols = sb("cols", [P, 8])
        lam = sb("lam", [P, 8])
        q_stack = sb("q_stack", [QK_ROWS, 2 * SLOTS, HG, 512], BF16)
        k_stack = sb("k_stack", [QK_ROWS, SLOTS, HG, S], BF16)
        v_all = sb("v_all", [P, TILES, GROUPS, HG * DH])
        v_stage = sb("v_stage", [P, TILES, HG, 32])
        e_ring = sb("e_ring", [P, 4, 2, 512])
        part = sb("part", [P, 2, 3, 512], BF16)
        fl = sb("fl", [P, 2, 512])
        max_parts = sb("max_parts", [P, 2, HG, 4, 2])
        shift = sb("shift", [P, HG, 4])
        shift_rest = sb("shift_rest", [P, HG, 4])
        shift16 = sb("shift16", [P, 2, HG, 4], BF16)
        shiftT = sb("shiftT", [2 * HG * 4, P], BF16)
        o_raw = sb("o_raw", [P, 512])
        o_inv = sb("o_inv", [P, 4, HG])
        o_all = sb("o_all", [P, TILES, GROUPS, HG * DH])
        normT = xT
        bias_f = o_all[0:1].rearrange("p t g n -> p (t g n)")[:, 0:BIASES]
        bias_16 = e_ring[0:1].rearrange("p a b n -> p (a b n)")[:, 0:3 * BIASES // 2].bitcast(BF16).rearrange("p (a n) -> p a n", a=3)
        sel32 = o_raw[:, 0:P]
        gn_stats = sb("gn_stats", [P, B, 2, 6])
        gn_mv = sb("gn_mv", [P, B, 2])
        gn_mean = sb("gn_mean", [P, B])
        gn_diff = sb("gn_diff", [P, B])
        gn_second = sb("gn_second", [P, B])
        gn_var = sb("gn_var", [P, B])
        gn_rstd = sb("gn_rstd", [P, B])
        gn_scale = sb("gn_scale", [P, B])
        gn_shift = sb("gn_shift", [P, B])
        ln_stats = sb("ln_stats", [P, B * TILES, 6])
        ln_mv = sb("ln_mv", [P, B * TILES, 2])
        rstd = sb("rstd", [P, B * TILES])
        neg_half = sb("neg_half_a", [P, B * TILES])

        ps = ctx.enter_context(nc.psum_tensor("ps", [P, 8, 512], F32))
        S_BANK = (0, 2)
        M_BANK = (4, 5)
        O_BANK = (6, 7)

        def maxima_at(i, s_, n, last, slot=0):
            qc, kt = divmod(s_, TILES)
            u = 4 * kt + n + UNITS_AHEAD
            away = 1 + u // UNITS
            if last and qc + away > 1:
                return None
            return 2 * i + qc + away, (slot + (qc + away) // 2) % SLOTS, (qc + away) % 2, u % UNITS

        names = ("bias_ld bias_split bias_zero bias_in ld_x0 ld_x1 ld_ident stack0_q stack0_k ld_w ld_small idents stack_zero xT_ps xT_sb lam_ps lam_e lam_v lam_done dve_c proj_ps q32 parts parts_out0 parts_out1 "
                 "vps v_sb v_free stack_ld vst qk_done exp_done mx_done mx_read shift16_done "
                 "shiftT_ps shiftT_sb aug_ld pv_done o_raw_done oT_ps o_read gn_T gn_mv_done gn_mm gn_second_done gn_var_done gn_pow gn_norm normT_done "
                 "y_ps y_add ln_st ln_ag y_ln ln_pow x1_done").split()
        z = {n: sem("s_" + n) for n in names}
        block = ctx.enter_context(nc.Block())
        NB = B * 2 * 2

        def stack_q(queue, i, loaded):
            for s_ in range(len(PARTS_Q)):
                for c in range(2):
                    src = qk_parts[0, PARTS_Q[s_], 32 * (i % 4):32 * (i % 4) + 32, i // 4 * S + 512 * c:i // 4 * S + 512 * c + 512]
                    queue.dma_start(q_stack[8 * s_:8 * s_ + 8, 2 * (i % SLOTS) + c, :, :], src.rearrange("(j d) n -> d j n", d=DH)).then_inc(loaded, 16)

        def stack_k(queue, i, loaded):
            for s_ in range(len(PARTS_K)):
                src = qk_parts[1, PARTS_K[s_], 32 * (i % 4):32 * (i % 4) + 32, i // 4 * S:(i // 4 + 1) * S]
                queue.dma_start(k_stack[8 * s_:8 * s_ + 8, i % SLOTS, :, :], src.rearrange("(j d) n -> d j n", d=DH)).then_inc(loaded, 16)

        @block.sync
        def _(sp):
            for b in range(B):
                sp.dma_start(x_in[:, b * TILES:(b + 1) * TILES, :],
                             t["L0_attn_x"][b].rearrange("(t p) d -> p t d", p=P)).then_inc(z[f"ld_x{b}"], 16)
                if b == 0:
                    sp.dma_start(ident[:], t["ident"][:]).then_inc(z["ld_ident"], 16)
                    for n, w in enumerate(("Wq", "Wk", "Wv", "Wo")):
                        sp.dma_start(w_attn[:, n, :], t["L0_attn_" + w][:]).then_inc(z["ld_w"], 16)
                    for name, (a, n) in BIAS_AT.items():
                        sp.dma_start(bias_f[:, a:a + n], t[name].rearrange("(a n) -> a n", a=1)).then_inc(z["bias_ld"], 16)
            sp.wait_ge(z["stack_zero"], 2)
            sp.dma_start(k_stack[SHIFT_ROW:SHIFT_ROW + 2, 0, :, :].rearrange("p j n -> p (j n)").bitcast(F32), t["ones16"][:]).then_inc(z["stack0_q"], 16)

            for b in range(B):
                for c in range(2):
                    for side in range(2):
                        n = (b * 2 + c) * 2 + side
                        sp.wait_ge(z["parts"], n + 1)
                        sp.dma_start(qk_parts[side, :, :, b * S + c * 512:b * S + c * 512 + 512].rearrange("a p n -> p a n"),
                                     part[:, n % 2, :, :]).then_inc(z[f"parts_out{n % 2}"], 16)
                        if n == 5:
                            sp.wait_ge(z["bias_zero"], 1)
                            sp.wait_ge(z["bias_split"], 1)
                            for r in range(3):
                                sp.dma_start(bias_rows[r:r + 1, :], bias_16[:, r, :]).then_inc(z["bias_in"], 16)
                if b == 0:
                    for k in range(2):
                        sp.wait_ge(z[f"parts_out{k}"], 16 * 2)
                    stack_q(sp, 0, z["stack0_q"])
            for k in range(2):
                sp.wait_ge(z[f"parts_out{k}"], 16 * NB // 2)
            for i in range(1, GROUPS):
                if i < SLOTS:
                    sp.wait_ge(z["stack_zero"], 2 * i + 2)
                else:
                    sp.wait_ge(z["qk_done"], 2 * STEPS * (i - SLOTS + 1))
                if i > 1:
                    sp.wait_ge(z["stack_ld"], 16 * STACK_LOADS * (i - 1))
                if i < SLOTS:
                    sp.dma_start(k_stack[SHIFT_ROW:SHIFT_ROW + 2, i, :, :].rearrange("p j n -> p (j n)").bitcast(F32), t["ones16"][:]).then_inc(z["stack_ld"], 16)
                else:
                    slot = i % SLOTS
                    sp.dma_start(q_stack[SHIFT_ROW:SHIFT_ROW + 2, 2 * slot:2 * slot + 2, :, :].rearrange("p a j n -> p (a j n)").bitcast(F32), t["zeros16"][:]).then_inc(z["stack_ld"], 16)
                stack_q(sp, i, z["stack_ld"])
                stack_k(sp, i, z["stack_ld"])
            load_next(sp)

        @block.gpsimd
        def _(g):
            g.memset(bias_rows[:], 0.0).then_inc(z["bias_zero"], 1)

            def clear(i):
                g.memset(k_stack[:, i, :, :].rearrange("p j n -> p (j n)").bitcast(F32), 0.0).then_inc(z["stack_zero"], 1)
                g.memset(q_stack[:, 2 * i:2 * i + 2, :, :].rearrange("p a j n -> p (a j n)").bitcast(F32), 0.0).then_inc(z["stack_zero"], 1)

            clear(0)
            g.memset(v_stage[:], 0.0).then_inc(z["vst"], 1)
            g.wait_ge(z["vst"], 1)
            g.memset(v_stage[:, :, :, 8:9], 1.0).then_inc(z["vst"], 1)
            g.memset(neg_half[:], -0.5).then_inc(z["vst"], 1)
            for i in range(1, SLOTS):
                clear(i)

            def refresh(i, kt):
                src = v_all[:, kt, i, :] if isinstance(i, int) else v_all[:, kt, ds(i, 1), :].rearrange("p a n -> p (a n)")
                g.tensor_copy(v_stage[:, kt, :, 0:DH], src.rearrange("p (j d) -> p j d", d=DH)).then_inc(z["vst"], 1)

            g.wait_ge(z["v_sb"], B * TILES // 4)
            for kt in range(TILES):
                refresh(0, kt)

            def body(i):
                for kt in range(TILES):
                    g.wait_ge(z["pv_done"], i * STEPS + TILES + kt + 1)
                    refresh(i + 1, kt)

            body(0)
            with g.Fori(1, GROUPS - 1) as i:
                body(i)
            g.wait_ge(z["gn_var_done"], 1)
            g.tensor_tensor(gn_rstd[:], gn_var[:], neg_half[:, 0:B], ALU.pow).then_inc(z["gn_pow"], 1)
            for b in range(B):
                g.wait_ge(z["y_ln"], b + 1)
                at = slice(b * TILES, (b + 1) * TILES)
                g.tensor_tensor(rstd[:, at], ln_mv[:, at, 1], neg_half[:, at], ALU.pow).then_inc(z["ln_pow"], 1)

        @block.scalar
        def _(act):
            for n, w in enumerate(("bq", "bk", "lq1", "lk1", "lq2", "lk2", "gn_w", "gn_b")):
                a = t["L0_attn_" + w]
                src = a.rearrange("(p a) -> p a", a=1) if len(a.shape) == 1 else a.rearrange("h (d a) -> (h d) a", a=1)
                act.dma_start(cols[:, n:n + 1], src).then_inc(z["ld_small"], 16)
            act.dma_start(sel32, t["bias_sel"][:]).then_inc(z["ld_small"], 16)
            act.dma_start(head_mean[:], t["head_mean"][:]).then_inc(z["ld_small"], 16)

            def xT_copy(b):
                for c in range(2):
                    act.wait_ge(z["xT_ps"], b * 2 + c + 1)
                    nc.scalar.copy(xT[:, b * S + c * 512:b * S + (c + 1) * 512], ps[:, c, :]).then_inc(z["xT_sb"], 1)

            def qk_copy(n):
                act.wait_ge(z["proj_ps"], n + 1)
                if n >= 2:
                    act.wait_ge(z["parts"], n - 1)
                if n % 2 == 0:
                    nc.scalar.activation(fl[:, 0, :], ps[:, 2, :], ACT.Identity, bias=lam[:, 6:7], scale=lam[:, 5:6]).then_inc(z["q32"], 1)
                else:
                    nc.scalar.activation(fl[:, 1, :], ps[:, 3, :], ACT.Identity, bias=cols[:, 1:2]).then_inc(z["q32"], 1)

            xT_copy(0)
            act.wait_ge(z["lam_ps"], 1)
            nc.scalar.activation(lam[:, 2:4], ps[:, 7, 0:2], ACT.Exp, scale=float(DH)).then_inc(z["lam_e"], 1)
            act.wait_ge(z["lam_done"], 1)
            for n in range(4):
                qk_copy(n)
            xT_copy(1)
            qk_copy(4)
            qk_copy(5)
            for k in range(2):
                act.wait_ge(z[f"parts_out{k}"], 16 * 2)
            act.wait_ge(z["stack_zero"], 2)
            stack_k(act, 0, z["stack0_k"])
            qk_copy(6)
            qk_copy(7)
            for m in range(B * TILES // 4):
                act.wait_ge(z["vps"], m + 1)
                nc.scalar.copy(v_all[:, 4 * (m % 2):4 * (m % 2) + 4, 4 * (m // 2):4 * (m // 2) + 4, :],
                               ps[:, m % 2, :].rearrange("p (t g n) -> p t g n", t=4, g=4)).then_inc(z["v_sb"], 1)

            def shifts(i, qc, slot):
                h = 2 * i + qc
                act.wait_ge(z["shiftT_ps"], h + 1)
                if not isinstance(h, int) or h >= 1:
                    act.wait_ge(z["aug_ld"], 32 * h)
                b = O_BANK[qc]
                nc.scalar.copy(shiftT[:], ps[0:32, b, 0:64].bitcast(BF16)).then_inc(z["shiftT_sb"], 1)
                act.wait_ge(z["shiftT_sb"], h + 1)
                for w in range(2):
                    dst = q_stack[SHIFT_ROW + w:SHIFT_ROW + w + 1, 2 * slot + qc, :, :].rearrange("p j n -> p (j n)")
                    act.dma_start(dst, shiftT[16 * w:16 * w + 16, :]).then_inc(z["aug_ld"], 16)

            def raw(i, qc):
                h = 2 * i + qc
                act.wait_ge(z["pv_done"], TILES * (h + 1))
                if not isinstance(h, int) or h >= 1:
                    act.wait_ge(z["oT_ps"], h)
                nc.scalar.copy(o_raw[:], ps[:, O_BANK[qc], :]).then_inc(z["o_raw_done"], 1)

            def body(i, slot, first, last):
                for s_ in range(STEPS):
                    qc, kt = divmod(s_, TILES)
                    gs = i * STEPS + s_
                    for p in range(2):
                        act.wait_ge(z["qk_done"], 2 * gs + p + 1)
                        if not (first and s_ < 2):
                            act.wait_ge(z["pv_done"], gs - 1)
                        nc.scalar.activation(e_ring[:, 2 * (s_ % 2) + p, :, :], ps[:, S_BANK[p]:S_BANK[p] + 2, :], ACT.Exp).then_inc(z["exp_done"], 1)
                    if kt == 1 and not (first and qc == 0):
                        raw(*((i, 0) if qc else (i - 1, 1)))
                    if kt == 5:
                        if qc == 0:
                            shifts(i, 1, slot)
                        elif not last:
                            shifts(i + 1, 0, (slot + 1) % SLOTS)

            shifts(0, 0, 0)
            body(0, 0, True, False)
            with act.Fori(0, (GROUPS - 2) // SLOTS) as r:
                for k in range(1, SLOTS + 1):
                    body(SLOTS * r + k, k % SLOTS, False, False)
            body(GROUPS - 1, (GROUPS - 1) % SLOTS, False, True)
            raw(GROUPS - 1, 1)
            act.wait_ge(z["gn_norm"], 1)
            for b in range(B):
                for c in range(2):
                    nc.scalar.activation(normT[:, b * S + c * 512:b * S + (c + 1) * 512], ps[:, 2 * b + c, :], ACT.Identity,
                                         bias=gn_shift[:, b:b + 1], scale=gn_scale[:, b:b + 1]).then_inc(z["normT_done"], 1)

        @block.vector
        def _(v):
            cnt = [0]

            def chain(ins):
                cnt[0] += 1
                ins.then_inc(z["dve_c"], 1)
                v.wait_ge(z["dve_c"], cnt[0])

            v.wait_ge(z["ld_small"], 16 * 10)
            v.tensor_tensor(lam[:, 0:1], cols[:, 2:3], cols[:, 3:4], ALU.mult).then_inc(z["lam_v"], 1)
            v.tensor_tensor(lam[:, 1:2], cols[:, 4:5], cols[:, 5:6], ALU.mult).then_inc(z["lam_v"], 1)
            v.wait_ge(z["ld_ident"], 16)
            v.tensor_copy(ident16[:], ident[:]).then_inc(z["idents"], 1)
            v.tensor_copy(bias_sel[:], sel32).then_inc(z["idents"], 1)
            v.wait_ge(z["lam_e"], 1)
            chain(v.tensor_tensor(lam[:, 4:5], lam[:, 2:3], lam[:, 3:4], ALU.subtract))
            chain(v.tensor_scalar(lam[:, 5:6], lam[:, 4:5], LAMBDA_INIT, DH ** -0.5, ALU.add, ALU.mult))
            v.tensor_tensor(lam[:, 6:7], cols[:, 0:1], lam[:, 5:6], ALU.mult).then_inc(z["lam_done"], 1)
            for n in range(NB):
                if n == 6:
                    v.wait_ge(z["bias_ld"], 16 * len(BIAS_AT))
                    chain(v.tensor_copy(bias_16[:, 0, :], bias_f))
                    chain(v.tensor_tensor(bias_f, bias_f, bias_16[:, 0, :], ALU.subtract))
                    chain(v.tensor_copy(bias_16[:, 1, :], bias_f))
                    v.tensor_tensor(bias_16[:, 2, :], bias_f, bias_16[:, 1, :], ALU.subtract).then_inc(z["bias_split"], 1)
                v.wait_ge(z["q32"], n + 1)
                if n >= 2:
                    v.wait_ge(z[f"parts_out{n % 2}"], 16 * (n // 2))
                f = fl[:, n % 2, :]
                chain(v.tensor_copy(part[:, n % 2, 0, :], f))
                chain(v.tensor_tensor(f, f, part[:, n % 2, 0, :], ALU.subtract))
                chain(v.tensor_copy(part[:, n % 2, 1, :], f))
                last = v.tensor_tensor(part[:, n % 2, 2, :], f, part[:, n % 2, 1, :], ALU.subtract)
                last.then_inc(z["parts"], 1)

            def reduce(h, half, u):
                j, r = divmod(u, 8)
                q, c = divmod(r, 2)
                v.wait_ge(z["mx_done"], UNITS * h + u + 1)
                v.tensor_reduce(max_parts[:, half, j, q, c:c + 1], ps[:, M_BANK[u % 2], :], AX.X, ALU.max).then_inc(z["mx_read"], 1)

            def final(h, half, step, first=False):
                if step == 0:
                    v.wait_ge(z["mx_read"], UNITS * h + UNITS)
                    if not first:
                        v.wait_ge(z["shiftT_ps"], h)
                    v.tensor_reduce(shift[:], max_parts[:, half, :, :, :], AX.X, ALU.max, negate=True).then_inc(z["shift16_done"], 1)
                    return
                v.wait_ge(z["shift16_done"], 4 * h + step)
                if step == 1:
                    v.tensor_copy(shift16[:, 0, :, :], shift[:]).then_inc(z["shift16_done"], 1)
                elif step == 2:
                    v.tensor_tensor(shift_rest[:], shift[:], shift16[:, 0, :, :], ALU.subtract).then_inc(z["shift16_done"], 1)
                else:
                    v.tensor_copy(shift16[:, 1, :, :], shift_rest[:]).then_inc(z["shift16_done"], 1)

            def normalise(i, qc, step):
                h = 2 * i + qc
                src = ps[:, O_BANK[qc], :].rearrange("p (t j c) -> p t j c", t=4, j=HG)
                if step == 0:
                    v.wait_ge(z["oT_ps"], h + 1)
                    v.reciprocal(o_inv[:], src[:, :, :, DH]).then_inc(z["o_read"], 1)
                else:
                    v.wait_ge(z["o_read"], 2 * h + 1)
                    dst = o_all[:, 4 * qc:4 * qc + 4, i, :] if isinstance(i, int) else o_all[:, 4 * qc:4 * qc + 4, ds(i, 1), :].rearrange("p t a n -> p (t a) n")
                    v.tensor_tensor(dst.rearrange("p t (j d) -> p t j d", j=HG), src[:, :, :, 0:DH],
                                    o_inv[:].unsqueeze(3).broadcast_to([P, 4, HG, DH]), ALU.mult).then_inc(z["o_read"], 1)

            def body(i, first, last):
                for s_ in range(STEPS):
                    qc, kt = divmod(s_, TILES)
                    for n in range(4):
                        at = maxima_at(i, s_, n, last)
                        if at:
                            reduce(at[0], at[2], at[3])
                        if kt == 3 and n < 2 and not (first and qc == 0):
                            normalise(*((i, 0) if qc else (i - 1, 1)), n)
                        if kt == 4 and not (last and qc):
                            final(2 * i + qc + 1, 1 - qc, n)

            for u in range(UNITS):
                reduce(0, 0, u)
            for n in range(4):
                final(0, 0, n, True)
            for u in range(UNITS_AHEAD):
                reduce(1, 1, u)
            body(0, True, False)
            with v.Fori(1, GROUPS - 1) as i:
                body(i, False, False)
            body(GROUPS - 1, False, True)
            for n in range(2):
                normalise(GROUPS - 1, 1, n)
            for b in range(B):
                v.wait_ge(z["gn_T"], b + 1)
                for c in range(2):
                    v.bn_stats(gn_stats[:, b, c, :], ps[:, 2 * b + c, :]).then_inc(z["dve_c"], 1)
            cnt[0] += 2 * B
            v.wait_ge(z["dve_c"], cnt[0])
            for b in range(B):
                v.bn_aggr(gn_mv[:, b, :], gn_stats[:, b, :, :].rearrange("p a n -> p (a n)")).then_inc(z["gn_mv_done"], 1)
            v.wait_ge(z["gn_mm"], 1)
            chain(v.tensor_copy(gn_mean[:], ps[:, 4, 0:B]))
            chain(v.tensor_tensor(gn_diff[:], gn_mv[:, :, 0], gn_mean[:], ALU.subtract))
            chain(v.tensor_tensor(gn_diff[:], gn_diff[:], gn_diff[:], ALU.mult))
            v.tensor_tensor(gn_second[:], gn_diff[:], gn_mv[:, :, 1], ALU.add).then_inc(z["gn_second_done"], 1)
            v.wait_ge(z["gn_mm"], 2)
            v.tensor_scalar(gn_var[:], ps[:, 4, 4:4 + B], EPS, None, ALU.add).then_inc(z["gn_var_done"], 1)
            v.wait_ge(z["gn_pow"], 1)
            chain(v.tensor_tensor(gn_scale[:], gn_rstd[:], cols[:, 6:7].broadcast_to([P, B]), ALU.mult))
            chain(v.tensor_tensor(gn_diff[:], gn_mean[:], gn_scale[:], ALU.mult))
            v.tensor_tensor(gn_shift[:], cols[:, 7:8].broadcast_to([P, B]), gn_diff[:], ALU.subtract).then_inc(z["gn_norm"], 1)
            for b in range(B):
                for c in range(2):
                    n = 2 * b + c
                    v.wait_ge(z["y_ps"], n + 1)
                    xt = x_in[:, 4 * n:4 * n + 4, :].rearrange("p t d -> p (t d)")
                    v.tensor_tensor(xt, xt, ps[:, 4 + n, :], ALU.add).then_inc(z["y_add"], 1)
                for c in range(2):
                    n = 2 * b + c
                    v.wait_ge(z["y_add"], n + 1)
                    for k in range(4 * n, 4 * n + 4):
                        v.bn_stats(ln_stats[:, k, :], x_in[:, k, :]).then_inc(z["ln_st"], 1)
                v.wait_ge(z["ln_st"], (b + 1) * TILES)
                at = slice(b * TILES, (b + 1) * TILES)
                for k in range(b * TILES, (b + 1) * TILES):
                    v.bn_aggr(ln_mv[:, k, :], ln_stats[:, k, :]).then_inc(z["ln_ag"], 1)
                v.wait_ge(z["ln_ag"], (b + 1) * TILES)
                v.tensor_scalar(ln_mv[:, at, 1], ln_mv[:, at, 1], EPS, None, ALU.add).then_inc(z["y_ln"], 1)
            for b in range(B):
                v.wait_ge(z["ln_pow"], b + 1)
                for k in range(b * TILES, (b + 1) * TILES):
                    v.tensor_scalar(x1[:, k, :], x_in[:, k, :], ln_mv[:, k, 0:1], rstd[:, k:k + 1], ALU.subtract, ALU.mult).then_inc(z["x1_done"], 1)

        @block.tensor
        def _(pe):
            mm = nc.tensor.matmul
            tr = nc.tensor.transpose

            def turn_x(b):
                pe.wait_ge(z[f"ld_x{b}"], 16)
                for c in range(2):
                    if b:
                        pe.wait_ge(z["xT_sb"], c + 1)
                    for n in range(4):
                        m = tr(ps[:, c, n * P:(n + 1) * P], x_in[:, b * TILES + 4 * c + n, :], ident[:])
                    m.then_inc(z["xT_ps"], 1)

            def project_qk(b):
                for n in range(4 * b, 4 * b + 4):
                    c = n // 2
                    pe.wait_ge(z["xT_sb"], c + 1)
                    if n >= 2:
                        pe.wait_ge(z["q32"], n - 1)
                    mm(ps[:, 2 + n % 2, :], w_attn[:, n % 2, :], xT[:, c * 512:(c + 1) * 512], start=True, stop=True).then_inc(z["proj_ps"], 1)

            pe.wait_ge(z["ld_ident"], 16)
            turn_x(0)
            pe.wait_ge(z["ld_small"], 16 * 10)
            pe.wait_ge(z["lam_v"], 2)
            mm(ps[:, 7, 0:2], head_mean[:], lam[:, 0:2], start=True, stop=True).then_inc(z["lam_ps"], 1)
            pe.wait_ge(z["ld_w"], 16 * 4)
            project_qk(0)
            turn_x(1)
            project_qk(1)
            def ks(slot, j, a, n):
                return k_stack[:, slot, j, a:a + n]

            def qs(slot, qc, j, a, n):
                return q_stack[:, 2 * slot + qc, j, a:a + n]

            def max_units(h, slot, qc, us):
                for u in us:
                    j, r = divmod(u, 8)
                    q, c = divmod(r, 2)
                    if not isinstance(h, int) or UNITS * h + u >= 2:
                        pe.wait_ge(z["mx_read"], UNITS * h + u - 1)
                    mm(ps[:, M_BANK[u % 2], :], qs(slot, qc, j, q * P, P), ks(slot, j, c * 512, 512),
                       start=True, stop=True).then_inc(z["mx_done"], 1)

            def maxima_of(i, s_, n, last, slot):
                at = maxima_at(i, s_, n, last, slot)
                if at:
                    max_units(*at[:3], (at[3],))

            def shifts(h, qc):
                pe.wait_ge(z["shift16_done"], 4 * h + 4)
                b = O_BANK[1 - qc]
                tr(ps[0:32, b, 0:64].bitcast(BF16), shift16[:].rearrange("p w j t -> p (w j t)"), ident16[:]).then_inc(z["shiftT_ps"], 1)

            def pv(i, s_, first, last=False):
                qc, kt = divmod(s_, TILES)
                gs = i * STEPS + s_
                pe.wait_ge(z["exp_done"], 2 * gs + 2)
                pe.wait_ge(z["vst"], 3 + (i * TILES if not first else 0) + kt + 1)
                for j in range(HG):
                    m = mm(ps[32 * j:32 * j + 32, O_BANK[qc], :], v_stage[:, kt, j, :], e_ring[:, 2 * (s_ % 2) + j // 2, j % 2, :],
                           start=(kt == 0), stop=(kt == TILES - 1))
                m.then_inc(z["pv_done"], 1)

            def o_turn(i, qc):
                h = 2 * i + qc
                pe.wait_ge(z["o_raw_done"], h + 1)
                for n in range(4):
                    m = tr(ps[:, O_BANK[qc], n * P:(n + 1) * P], o_raw[:, n * P:(n + 1) * P], ident[:])
                m.then_inc(z["oT_ps"], 1)

            def body(i, slot, first, last):
                for s_ in range(STEPS):
                    qc, kt = divmod(s_, TILES)
                    if s_ == 4 and not last:
                        pe.wait_ge(z["stack_ld"], 16 * STACK_LOADS * (i + 1))
                    gs = i * STEPS + s_
                    h = 2 * i + qc
                    if kt == 0:
                        pe.wait_ge(z["aug_ld"], 32 * h + 32)
                    for p in range(2):
                        maxima_of(i, s_, p, last, slot)
                        if not (first and s_ == 0):
                            pe.wait_ge(z["exp_done"], 2 * gs + p - 1)
                        for j in range(2):
                            m = mm(ps[:, S_BANK[p] + j, :], ks(slot, 2 * p + j, kt * P, P), qs(slot, qc, 2 * p + j, 0, 512),
                                   start=True, stop=True)
                        m.then_inc(z["qk_done"], 1)
                    maxima_of(i, s_, 2, last, slot)
                    maxima_of(i, s_, 3, last, slot)
                    if s_ == 0:
                        if not first:
                            pv(i - 1, STEPS - 1, False)
                    else:
                        if kt == 1:
                            pe.wait_ge(z["shiftT_sb"], h + 1)
                        pv(i, s_ - 1, first)
                    if kt == 2 and not (first and qc == 0):
                        o_turn(*((i, 0) if qc else (i - 1, 1)))
                    if kt == 5:
                        if not (first and qc == 0):
                            pe.wait_ge(z["o_read"], 2 * h)
                        if qc == 0:
                            shifts(h + 1, 0)
                        elif not last:
                            shifts(h + 1, 1)

            pe.wait_ge(z["stack0_q"], 16 * (1 + 2 * len(PARTS_Q)))
            pe.wait_ge(z["stack0_k"], 16 * len(PARTS_K))
            for m_ in range(B * TILES // 4):
                max_units(0, 0, 0, range(8 * m_, 8 * m_ + 8))
                pe.wait_ge(z["idents"], 2)
                pe.wait_ge(z["bias_in"], 16 * 3)
                if m_ < 2:
                    pe.wait_ge(z["xT_sb"], 4)
                else:
                    pe.wait_ge(z["v_sb"], m_ - 1)
                for n in range(4):
                    o = ps[:, m_ % 2, n * P:(n + 1) * P]
                    mm(o, xT[:, (4 * m_ + n) * P:(4 * m_ + n + 1) * P], w_attn[:, 2, :], start=True, stop=False)
                    m = mm(o, bias_sel[:], bias_of(bias_rows, "L0_attn_bv"), start=False, stop=True)
                m.then_inc(z["vps"], 1)
            max_units(1, 0, 1, range(2))
            shifts(0, 1)
            max_units(1, 0, 1, range(2, UNITS_AHEAD))
            pe.wait_ge(z["q32"], NB)
            pe.wait_ge(z["v_sb"], B * TILES // 4)
            body(0, 0, True, False)
            with pe.Fori(0, (GROUPS - 2) // SLOTS) as r:
                for k in range(1, SLOTS + 1):
                    body(SLOTS * r + k, k % SLOTS, False, False)
            body(GROUPS - 1, (GROUPS - 1) % SLOTS, False, True)
            pv(GROUPS - 1, STEPS - 1, False)
            o_turn(GROUPS - 1, 1)
            pe.wait_ge(z["exp_done"], 2 * STEPS * GROUPS)
            for b in range(B):
                if b == B - 1:
                    pe.wait_ge(z["o_read"], 4 * GROUPS)
                else:
                    pe.wait_ge(z["o_read"], 2 * GROUPS + 2)
                for n in range(TILES):
                    m = tr(ps[:, 2 * b + n // 4, (n % 4) * P:(n % 4 + 1) * P], o_all[:, n, 4 * b:4 * b + 4, :].rearrange("p g n -> p (g n)"), ident[:])
                m.then_inc(z["gn_T"], 1)
            pe.wait_ge(z["gn_mv_done"], B)
            mm(ps[:, 4, 0:B], head_mean[:], gn_mv[:, :, 0], start=True, stop=True).then_inc(z["gn_mm"], 1)
            pe.wait_ge(z["gn_second_done"], 1)
            mm(ps[:, 4, 4:4 + B], head_mean[:], gn_second[:], start=True, stop=True).then_inc(z["gn_mm"], 1)
            for n in range(B * TILES):
                if n % 4 == 0:
                    pe.wait_ge(z["normT_done"], n // 4 + 1)
                o = ps[:, 4 + n // 4, (n % 4) * P:(n % 4 + 1) * P]
                mm(o, normT[:, n * P:(n + 1) * P], w_attn[:, 3, :], start=True, stop=False)
                m = mm(o, bias_sel[:], bias_of(bias_rows, "L0_attn_bo"), start=False, stop=True)
                if n % 4 == 3:
                    m.then_inc(z["y_ps"], 1)


FH, KV, FDH = 16, 4, 64
QKV = (FH + 2 * KV) * FDH
WINDOW = 128
NT = B * TILES
BATCHES = 4
MASKED = -1e30


class WindowInputs:

    def __init__(self, nc, ctx, t):
        def sb(name, shape, dt=F32):
            return ctx.enter_context(nc.sbuf_tensor(name, shape, dt))

        self.t = t
        self.w_qkv = sb("w_qkv", [P, QKV])
        self.w_proj = sb("w_proj", [P, 8, D])
        self.norm_w = sb("norm_w", [P, 1])
        self.sink = sb("sink", [P, FH])
        self.rope_c = sb("rope_c", [P, TILES, FDH])
        self.rope_s = sb("rope_s", [P, TILES, FDH])
        self.mask = sb("mask", [P, 2, 512], BF16)
        self.loaded = ctx.enter_context(nc.semaphore("window_inputs"))
        self.loads = 7

    def load(self, sp):
        t, ld = self.t, self.loaded
        sp.dma_start(self.w_qkv[:], t["L0_ffn_qkv_w"][:]).then_inc(ld, 16)
        sp.dma_start(self.norm_w[:], t["L0_ffn_attn_norm_w"].rearrange("(p a) -> p a", a=1)).then_inc(ld, 16)
        sp.dma_start(self.rope_c[:], t["rope_c"][:]).then_inc(ld, 16)
        sp.dma_start(self.rope_s[:], t["rope_s"][:]).then_inc(ld, 16)
        sp.dma_start(self.mask[:].rearrange("p a n -> p (a n)").bitcast(F32), t["mask"][:]).then_inc(ld, 16)
        sp.dma_start(self.w_proj[:], t["L0_ffn_proj_w"].rearrange("(c p) n -> p c n", p=P)).then_inc(ld, 16)
        sp.dma_start(self.sink[:], t["L0_ffn_attn_sink"].rearrange("(a n) -> a n", a=1).broadcast_to([P, FH])).then_inc(ld, 16)


def window_attention(nc, inputs, x1, x2, ident, ident16, bias_sel, bias_rows):
    with ExitStack() as ctx:
        def sb(name, shape, dt=F32):
            return ctx.enter_context(nc.sbuf_tensor(name, shape, dt))

        w_qkv, w_proj, norm_w, sink = inputs.w_qkv, inputs.w_proj, inputs.norm_w, inputs.sink
        rope_c, rope_s, mask = inputs.rope_c, inputs.rope_s, inputs.mask
        nsink = sb("nsink", [P, FH])
        sq = sb("sq", [P, D])
        rms = sb("rms", [P, NT])
        rms_in = sb("rms_in", [P, NT])
        neg_half = sb("neg_half", [P, NT])
        h_cur = sb("h_cur", [P, D])
        hT = sb("hT", [P, P])
        hT_hi = sb("hT_hi", [P, P], F32R)
        hT_lo = sb("hT_lo", [P, P], F32R)
        w_hi = sb("w_qkv_hi", [P, QKV], F32R)
        w_lo = sb("w_qkv_lo", [P, QKV], F32R)
        rot_a = sb("rot_a", [P, 2, 512])
        rot_b = sb("rot_b", [P, 2, 512])
        q_rot = sb("q_rot", [P, FH, 2, FDH])
        k_rot = sb("k_rot", [P, KV, 2, FDH])
        q_hi = sb("q_hi", [P, FH, P], F32R)
        q_lo = sb("q_lo", [P, FH, P], F32R)
        kT = sb("kT", [P, KV, (NT + 1) * P], F32R)
        v_win = sb("v_win", [P, NT + 1, KV * FDH])
        neg_max = sb("neg_max", [P, 4])
        bias = sb("bias", [P, 4, 4])
        sums = sb("sums", [P, 4, 4])
        sink_in = sb("sink_in", [P, 8])
        sink_e = sb("sink_e", [P, 8])
        den = sb("den", [P, 8])
        inv = sb("inv", [P, 8])
        probs = sb("probs", [P, 2, 4, 256])
        pT = sb("pT", [P, 2, 2, 512])
        y_sb = sb("y_sb", [P, FH * FDH])
        yT = sb("yT", [P, 8, P])
        ps = ctx.enter_context(nc.psum_tensor("ps_w", [P, 8, 512], F32))
        PROBS, Y_BANK = 4, 6
        A, W = 5, 7
        TURN = (2, 0, 1)
        QKV_BANK = (A, W, W)
        Q_BANK = (A, W, A, A)

        names = ("init rms_in rms h_done w_hi w_lo hT_ps hT_sb hT_hi hT_lo qkv_ps rope_a rope_read rot v_sb qT_ps qT_hi qT_sb kT_ps kT_hi kT_sb "
                 "s_ps negmax bias exp sink_in sink_e den inv pT_ps pT_dve pT_act pv y_norm yT_ps yT_sb proj_ps x2 sq").split()
        z = {n: ctx.enter_context(nc.semaphore("w_" + n)) for n in names}
        block = ctx.enter_context(nc.Block())

        @block.gpsimd
        def _(g):
            g.memset(neg_half[:], -0.5).then_inc(z["init"], 1)
            g.memset(v_win[:, 0, :], 0.0).then_inc(z["init"], 1)
            g.wait_ge(z["init"], 2)
            for n in range(0, KV, 2):
                g.tensor_copy(kT[:, n:n + 2, 0:P], v_win[:, 0, :].rearrange("p (a n) -> p a n", a=2)).then_inc(z["init"], 1)
            g.wait_ge(inputs.loaded, 16 * inputs.loads)
            g.tensor_scalar(nsink[:], sink[:], -1.0, None, ALU.mult).then_inc(z["init"], 1)
            g.wait_ge(z["rms_in"], 1)
            g.wait_ge(z["init"], 5)
            g.tensor_tensor(rms[:], rms_in[:], neg_half[:], ALU.pow).then_inc(z["rms"], 1)

            def rotate(tile, c):
                at = TURN.index(c)
                g.wait_ge(z["rope_read"], 3 * tile + at + 1)
                a = at % 2
                dst, heads = (q_rot[:, 8 * c:8 * c + 8, :, :], 8) if c < 2 else (k_rot[:], KV)
                both = [r[:, a, 0:heads * FDH].rearrange("p (h d) -> p h d", h=heads).unsqueeze(2).broadcast_to([P, heads, 2, FDH]) for r in (rot_a, rot_b)]
                g.tensor_tensor(dst, both[0], both[1], ALU.add).then_inc(z["rot"], 1)

            def sinks(tile, hf, first):
                g.wait_ge(z["bias"], 4 * tile + 2 * hf + 2)
                g.tensor_tensor(sink_in[:], bias[:, 2 * hf:2 * hf + 2, :].rearrange("p a n -> p (a n)"), sink[:, 8 * hf:8 * hf + 8], ALU.add).then_inc(z["sink_in"], 1)
                g.wait_ge(z["sink_e"], 2 * tile + hf + 1)
                if not (first and hf == 0):
                    g.wait_ge(z["inv"], 2 * tile + hf)
                g.tensor_tensor(den[:], sink_e[:], sums[:, 2 * hf:2 * hf + 2, :].rearrange("p a n -> p (a n)"), ALU.add).then_inc(z["den"], 1)

            def prep(tile):
                for c in TURN:
                    rotate(tile, c)

            def body(tile, first, last):
                if not last:
                    rotate(tile + 1, 2)
                sinks(tile, 0, first)
                if not last:
                    rotate(tile + 1, 0)
                sinks(tile, 1, first)
                if not last:
                    rotate(tile + 1, 1)

            prep(0)
            body(0, True, False)
            with g.Fori(1, NT - 1) as tile:
                body(tile, False, False)
            body(NT - 1, False, True)

        @block.scalar
        def _(act):
            def hT_copy(tile):
                act.wait_ge(z["hT_ps"], tile + 1)
                nc.scalar.activation(hT[:], ps[:, W, 0:P], ACT.Copy, scale=norm_w[:, 0:1]).then_inc(z["hT_sb"], 1)
                act.wait_ge(z["hT_sb"], tile + 1)
                nc.scalar.copy(hT_hi[:], hT[:]).then_inc(z["hT_hi"], 1)

            def v_copy(tile):
                act.wait_ge(z["rope_read"], 3 * tile + 1)
                act.wait_ge(z["init"], 5)
                nc.scalar.copy(v_win[:, ds(tile + 1, 1), :].rearrange("p a n -> p (a n)"), ps[:, W, 256:512]).then_inc(z["v_sb"], 1)

            def qT_high(tile, c):
                act.wait_ge(z["qT_ps"], 4 * tile + c + 1)
                nc.scalar.copy(q_hi[:, 4 * c:4 * c + 4, :].rearrange("p a n -> p (a n)"), ps[:, Q_BANK[c], :]).then_inc(z["qT_hi"], 1)

            def kT_high(tile):
                act.wait_ge(z["kT_ps"], tile + 1)
                nc.scalar.copy(kT[:, :, ds(tile * P + P, P)], ps[:, W, :].rearrange("p (a n) -> p a n", a=KV)).then_inc(z["kT_hi"], 1)

            def exps(tile, k, js):
                kb = 4 * tile + k
                act.wait_ge(z["bias"], kb + 1)
                for j in js:
                    nc.scalar.activation(probs[:, k % 2, j, :], ps[:, 2 * (k % 2) + j // 2, 256 * (j % 2):256 * (j % 2) + 256], ACT.Exp,
                                         bias=bias[:, k, j:j + 1], scale=FDH ** -0.5, accum_out=sums[:, k, j:j + 1]).then_inc(z["exp"], 1)

            def pT_copy(tile, k):
                kb = 4 * tile + k
                act.wait_ge(z["pT_ps"], 2 * kb + 1)
                if not isinstance(kb, int) or kb > 1:
                    act.wait_ge(z["pv"], 2 * kb - 3)
                nc.scalar.copy(pT[:, k % 2, 0, :], ps[:, PROBS, :]).then_inc(z["pT_act"], 1)

            def sinks(tile, hf):
                act.wait_ge(z["sink_in"], 2 * tile + hf + 1)
                nc.scalar.activation(sink_e[:], sink_in[:], ACT.Exp).then_inc(z["sink_e"], 1)

            def yT_copy(tile, c):
                act.wait_ge(z["yT_ps"], 2 * tile + c + 1)
                nc.scalar.copy(yT[:, 4 * c:4 * c + 4, :].rearrange("p a n -> p (a n)"), ps[:, (W, A)[c], :]).then_inc(z["yT_sb"], 1)

            def body(tile, first, last):
                def slot(k):
                    kb = 4 * tile + k
                    if not (first and k < 2):
                        act.wait_ge(z["pT_ps"], 2 * kb - 2)
                    if not first:
                        act.wait_ge(z["den"], 2 * tile + k // 2 - 1)
                slot(0)
                exps(tile, 0, range(4))
                if not last:
                    hT_copy(tile + 1)
                qT_high(tile, 3)
                pT_copy(tile, 0)
                slot(1)
                exps(tile, 1, range(4))
                if not last:
                    v_copy(tile + 1)
                sinks(tile, 0)
                pT_copy(tile, 1)
                slot(2)
                exps(tile, 2, range(4))
                if not first:
                    yT_copy(tile - 1, 0)
                    yT_copy(tile - 1, 1)
                pT_copy(tile, 2)
                slot(3)
                exps(tile, 3, range(4))
                sinks(tile, 1)
                if not last:
                    kT_high(tile + 1)
                pT_copy(tile, 3)
                if not last:
                    qT_high(tile + 1, 0)
                    qT_high(tile + 1, 1)
                    qT_high(tile + 1, 2)

            act.wait_ge(inputs.loaded, 16 * inputs.loads)
            nc.scalar.copy(w_hi[:], w_qkv[:]).then_inc(z["w_hi"], 1)
            hT_copy(0)
            v_copy(0)
            kT_high(0)
            for c in range(3):
                qT_high(0, c)
            body(0, True, False)
            with act.Fori(1, NT - 1) as tile:
                body(tile, False, False)
            body(NT - 1, False, True)
            for c in range(2):
                yT_copy(NT - 1, c)

        @block.vector
        def _(v):
            for n in range(NT):
                if n:
                    v.wait_ge(z["sq"], n)
                v.tensor_tensor_reduce(out=sq[:], in0=x1[:, n, :], in1=x1[:, n, :], scale=1.0, scalar=0.0, op0=ALU.mult, op1=ALU.add,
                                       accum_out=rms_in[:, n:n + 1]).then_inc(z["sq"], 1)
            v.wait_ge(z["sq"], NT)
            v.tensor_scalar(rms_in[:], rms_in[:], 1.0 / D, EPS, ALU.mult, ALU.add).then_inc(z["rms_in"], 1)
            v.wait_ge(z["w_hi"], 1)
            v.tensor_tensor(w_lo[:], w_qkv[:], w_hi[:], ALU.subtract).then_inc(z["w_lo"], 1)
            v.wait_ge(z["rms"], 1)
            v.wait_ge(inputs.loaded, 16 * inputs.loads)

            def h_of(tile, first=False):
                if not first:
                    v.wait_ge(z["hT_ps"], tile)
                v.tensor_scalar(h_cur[:], x1[:, ds(tile % NT, 1), :].rearrange("p a n -> p (a n)"), rms[:, ds(tile % NT, 1)], None, ALU.mult).then_inc(z["h_done"], 1)

            def rope(tile, c, first=False):
                at = TURN.index(c)
                v.wait_ge(z["qkv_ps"], 3 * tile + at + 1)
                n = 512 if c < 2 else 256
                hs = n // FDH
                a = at % 2
                if not (first and at < 2):
                    v.wait_ge(z["rot"], (3 * tile, 3 * tile - 1, 3 * tile + 1)[at])
                tl = tile % TILES
                src = ps[:, QKV_BANK[c], 0:n].rearrange("p (h d) -> p h d", h=hs)
                ct = rope_c[:, ds(tl, 1), :].broadcast_to([P, hs, FDH])
                st = rope_s[:, ds(tl, 1), :].broadcast_to([P, hs, FDH])
                v.tensor_tensor(rot_a[:, a, 0:n].rearrange("p (h d) -> p h d", h=hs), src, ct, ALU.mult).then_inc(z["rope_a"], 1)
                src = ps[:, QKV_BANK[c], 0:n].rearrange("p (h d e) -> p h d e", h=hs, e=2)
                dst = rot_b[:, a, 0:n].rearrange("p (h d e) -> p h d e", h=hs, e=2)
                stp = st.rearrange("p h (d e) -> p h d e", e=2)
                v.tensor_tensor(dst[:, :, :, 0], src[:, :, :, 1], stp[:, :, :, 0], ALU.mult).then_inc(z["rope_a"], 1)
                v.tensor_tensor(dst[:, :, :, 1], src[:, :, :, 0], stp[:, :, :, 1], ALU.mult).then_inc(z["rope_read"], 1)

            def hT_low(tile):
                v.wait_ge(z["hT_hi"], tile + 1)
                v.tensor_tensor(hT_lo[:], hT[:], hT_hi[:], ALU.subtract).then_inc(z["hT_lo"], 1)

            def qT_low(tile, c):
                v.wait_ge(z["qT_hi"], 4 * tile + c + 1)
                v.tensor_tensor(q_lo[:, 4 * c:4 * c + 4, :].rearrange("p a n -> p (a n)"), ps[:, Q_BANK[c], :],
                                q_hi[:, 4 * c:4 * c + 4, :].rearrange("p a n -> p (a n)"), ALU.subtract).then_inc(z["qT_sb"], 1)

            def kT_low(tile):
                v.wait_ge(z["kT_hi"], tile + 1)
                low = kT[FDH:P, :, ds(tile * P + P, P)]
                v.tensor_tensor(low, ps[FDH:P, W, :].rearrange("p (a n) -> p a n", a=KV), low, ALU.subtract).then_inc(z["kT_sb"], 1)

            def maxima(tile, k, first=False):
                kb = 4 * tile + k
                v.wait_ge(z["s_ps"], kb + 1)
                if not isinstance(kb, int) or kb:
                    v.wait_ge(z["bias"], kb)
                v.tensor_reduce(neg_max[:], ps[:, 2 * (k % 2):2 * (k % 2) + 2, :].rearrange("p b (e n) -> p (b e) n", e=2), AX.X, ALU.max,
                                negate=True).then_inc(z["negmax"], 1)
                v.wait_ge(z["negmax"], kb + 1)
                if not (first and k < 4):
                    v.wait_ge(z["den"], 2 * (tile - 1) + k // 2 + 1)
                v.scalar_tensor_tensor(bias[:, k, :], neg_max[:], FDH ** -0.5, nsink[:, 4 * k:4 * k + 4], ALU.mult, ALU.min).then_inc(z["bias"], 1)

            def pT_copy(tile, k):
                kb = 4 * tile + k
                v.wait_ge(z["pT_ps"], 2 * kb + 2)
                if not isinstance(kb, int) or kb > 1:
                    v.wait_ge(z["pv"], 2 * kb - 2)
                v.tensor_copy(pT[:, k % 2, 1, :], ps[:, PROBS, :]).then_inc(z["pT_dve"], 1)

            def y_norm(tile, hf):
                v.wait_ge(z["den"], 2 * tile + hf + 1)
                if not isinstance(tile, int) or 2 * tile + hf:
                    v.wait_ge(z["y_norm"], 2 * tile + hf)
                v.reciprocal(inv[:], den[:]).then_inc(z["inv"], 1)
                v.wait_ge(z["inv"], 2 * tile + hf + 1)
                v.wait_ge(z["pv"], 8 * tile + 4 * hf + 4)
                v.tensor_tensor(y_sb[:, 512 * hf:512 * hf + 512].rearrange("p (h d) -> p h d", h=8), ps[:, Y_BANK, :].rearrange("p (h d) -> p h d", h=8),
                                inv[:].unsqueeze(2).broadcast_to([P, 8, FDH]), ALU.mult).then_inc(z["y_norm"], 1)

            def residual(tile):
                v.wait_ge(z["proj_ps"], tile + 1)
                v.tensor_tensor(x2[:, ds(tile, 1), :].rearrange("p a n -> p (a n)"), ps[:, A, 0:P],
                                x1[:, ds(tile, 1), :].rearrange("p a n -> p (a n)"), ALU.add).then_inc(z["x2"], 1)

            def body(tile, first, last):
                maxima(tile, 1, first)
                if not last:
                    hT_low(tile + 1)
                qT_low(tile, 3)
                if not first:
                    y_norm(tile - 1, 1)
                if not last:
                    rope(tile + 1, 2)
                pT_copy(tile, 0)
                maxima(tile, 2, first)
                if not last:
                    rope(tile + 1, 0)
                pT_copy(tile, 1)
                if not last:
                    h_of(tile + 2)
                maxima(tile, 3, first)
                pT_copy(tile, 2)
                if not last:
                    rope(tile + 1, 1)
                y_norm(tile, 0)
                if not first:
                    residual(tile - 1)
                if not last:
                    kT_low(tile + 1)
                    qT_low(tile + 1, 0)
                pT_copy(tile, 3)
                if not last:
                    qT_low(tile + 1, 1)
                    maxima(tile + 1, 0)
                    qT_low(tile + 1, 2)

            h_of(0, True)
            hT_low(0)
            for c in TURN:
                rope(0, c, True)
            h_of(1)
            kT_low(0)
            qT_low(0, 0)
            qT_low(0, 1)
            maxima(0, 0, True)
            qT_low(0, 2)
            body(0, True, False)
            with v.Fori(1, NT - 1) as tile:
                body(tile, False, False)
            body(NT - 1, False, True)
            y_norm(NT - 1, 1)
            residual(NT - 1)

        @block.tensor
        def _(pe):
            mm = nc.tensor.matmul
            tr = nc.tensor.transpose

            def hT_of(tile):
                pe.wait_ge(z["h_done"], tile + 1)
                tr(ps[:, W, 0:P], h_cur[:], ident[:]).then_inc(z["hT_ps"], 1)

            def qkv(tile, c):
                pe.wait_ge(z["hT_lo"], tile + 1)
                o = ps[:, QKV_BANK[c], :]
                at = slice(512 * c, 512 * c + 512)
                mm(o, hT_hi[:], w_hi[:, at], start=True, stop=False)
                mm(o, hT_hi[:], w_lo[:, at], start=False, stop=False)
                mm(o, hT_lo[:], w_hi[:, at], start=False, stop=False)
                mm(o, bias_sel[:], bias_of(bias_rows, "L0_ffn_qkv_b", 512 * c, 512), start=False, stop=True).then_inc(z["qkv_ps"], 1)

            def qT_of(tile, c):
                pe.wait_ge(z["rot"], 3 * tile + 2 + c // 2)
                for n in range(4):
                    h = 4 * c + n
                    m = tr(ps[:, Q_BANK[c], n * P:(n + 1) * P], q_rot[:, h, :, :].rearrange("p a d -> p (a d)"), ident[:])
                m.then_inc(z["qT_ps"], 1)

            def kT_of(tile):
                pe.wait_ge(z["rot"], 3 * tile + 1)
                for n in range(KV):
                    m = tr(ps[:, W, n * P:(n + 1) * P], k_rot[:, n, :, :].rearrange("p a d -> p (a d)"), ident[:])
                m.then_inc(z["kT_ps"], 1)

            def scores(tile, k, first=False):
                kb = 4 * tile + k
                if not (first and k < 2):
                    pe.wait_ge(z["exp"], 4 * kb - 4)
                pe.wait_ge(z["qT_sb"], 4 * tile + k + 1)
                pe.wait_ge(z["kT_sb"], tile + 1)
                keys = kT[:, k, ds(tile * P, 2 * P)]
                for n in range(2):
                    o = ps[:, 2 * (k % 2) + n, :]
                    mm(o, ident16[:], mask[:, ds((tile % TILES + TILES - 1) // TILES, 1), :].rearrange("p a n -> p (a n)"), start=True, stop=False)
                    for j in range(2):
                        h = 4 * k + 2 * n + j
                        mm(o[:, 256 * j:256 * j + 256], q_hi[:, h, :], keys, start=False, stop=False)
                        m = mm(o[:, 256 * j:256 * j + 256], q_lo[:, h, :], keys, start=False, stop=(j == 1))
                m.then_inc(z["s_ps"], 1)

            def turn_probs(tile, k, c):
                kb = 4 * tile + k
                pe.wait_ge(z["exp"], 4 * kb + 2 * c + 2)
                if c:
                    pe.wait_ge(z["pT_act"], kb + 1)
                elif not isinstance(kb, int) or kb:
                    pe.wait_ge(z["pT_dve"], kb)
                for n in range(4):
                    m = tr(ps[:, PROBS, n * P:(n + 1) * P], probs[:, k % 2, 2 * c + n // 2, (n % 2) * P:(n % 2 + 1) * P], ident[:])
                m.then_inc(z["pT_ps"], 1)

            def pv(tile, k, c):
                kb = 4 * tile + k
                if c == 0 and k % 2 == 0 and (not isinstance(kb, int) or kb):
                    pe.wait_ge(z["y_norm"], 2 * tile + k // 2)
                pe.wait_ge(z["pT_dve" if c else "pT_act"], kb + 1)
                for j in range(2):
                    h = 4 * (k % 2) + 2 * c + j
                    for w in range(2):
                        m = mm(ps[:, Y_BANK, h * FDH:(h + 1) * FDH], pT[:, k % 2, c, (2 * j + w) * P:(2 * j + w + 1) * P],
                               v_win[:, ds(tile + w, 1), k * FDH:(k + 1) * FDH].rearrange("p a n -> p (a n)"), start=(w == 0), stop=(w == 1))
                m.then_inc(z["pv"], 1)

            def yT_of(tile, c):
                pe.wait_ge(z["y_norm"], 2 * tile + 2)
                for n in range(4):
                    m = tr(ps[:, (W, A)[c], n * P:(n + 1) * P], y_sb[:, (4 * c + n) * P:(4 * c + n + 1) * P], ident[:])
                m.then_inc(z["yT_ps"], 1)

            def project(tile):
                pe.wait_ge(z["yT_sb"], 2 * tile + 2)
                for c in range(8):
                    mm(ps[:, A, 0:P], yT[:, c, :], w_proj[:, c, :], start=(c == 0), stop=False)
                mm(ps[:, A, 0:P], bias_sel[:], bias_of(bias_rows, "L0_ffn_proj_b"), start=False, stop=True).then_inc(z["proj_ps"], 1)

            def body(tile, first, last):
                nxt, prev = tile + 1, tile - 1
                scores(tile, 1, first)
                if not last:
                    hT_of(nxt)
                pe.wait_ge(z["qT_sb"], 4 * tile + 3)
                qT_of(tile, 3)
                if not first:
                    pv(prev, 3, 0)
                    pv(prev, 3, 1)
                turn_probs(tile, 0, 0)
                if not last:
                    qkv(nxt, 2)
                turn_probs(tile, 0, 1)

                scores(tile, 2, first)
                pe.wait_ge(z["qT_sb"], 4 * tile + 4)
                if not last:
                    qkv(nxt, 0)
                turn_probs(tile, 1, 0)
                pv(tile, 0, 0)
                turn_probs(tile, 1, 1)
                pv(tile, 0, 1)
                if not last:
                    pe.wait_ge(z["rope_read"], 3 * nxt + 1)
                    pe.wait_ge(z["v_sb"], nxt + 1)
                if not first:
                    yT_of(prev, 0)

                scores(tile, 3, first)
                if not last:
                    pe.wait_ge(z["rope_read"], 3 * nxt + 2)
                if not first:
                    yT_of(prev, 1)
                turn_probs(tile, 2, 0)
                pv(tile, 1, 0)
                turn_probs(tile, 2, 1)
                if not last:
                    if not first:
                        pe.wait_ge(z["yT_sb"], 2 * prev + 1)
                    qkv(nxt, 1)
                pv(tile, 1, 1)
                if not first:
                    project(prev)

                if not last:
                    pe.wait_ge(z["rope_read"], 3 * nxt + 3)
                    kT_of(nxt)
                turn_probs(tile, 3, 0)
                pv(tile, 2, 0)
                if not first:
                    pe.wait_ge(z["x2"], prev + 1)
                if not last:
                    qT_of(nxt, 0)
                turn_probs(tile, 3, 1)
                pv(tile, 2, 1)
                if not last:
                    pe.wait_ge(z["kT_sb"], nxt + 1)
                    qT_of(nxt, 1)
                    scores(nxt, 0)
                    qT_of(nxt, 2)

            pe.wait_ge(inputs.loaded, 16 * inputs.loads)
            pe.wait_ge(z["init"], 5)
            hT_of(0)
            pe.wait_ge(z["w_lo"], 1)
            qkv(0, 2)
            qkv(0, 0)
            pe.wait_ge(z["rope_read"], 1)
            pe.wait_ge(z["v_sb"], 1)
            qkv(0, 1)
            pe.wait_ge(z["rope_read"], 3)
            kT_of(0)
            qT_of(0, 0)
            pe.wait_ge(z["kT_sb"], 1)
            qT_of(0, 1)
            scores(0, 0, True)
            qT_of(0, 2)
            body(0, True, False)
            with pe.Fori(1, NT - 1) as tile:
                body(tile, False, False)
            body(NT - 1, False, True)
            pv(NT - 1, 3, 0)
            pv(NT - 1, 3, 1)
            yT_of(NT - 1, 0)
            yT_of(NT - 1, 1)
            project(NT - 1)


E, TOPK, DFF = 32, 4, 128
UP2 = 2 * DFF
BLK = 512
BT = BLK // P
BLOCKS = B * S // BLK
AHEAD = 4
PER_LOAD = 4


def experts(nc, t, x1, x2, ident, ident16, bias_sel, bias_rows, out):
    with ExitStack() as ctx:
        def sb(name, shape, dt=F32):
            return ctx.enter_context(nc.sbuf_tensor(name, shape, dt))

        w_raw = sb("w_raw", [P, 2, PER_LOAD, UP2 + D])
        w_hi = sb("w_hi", [P, E, UP2 + D], F32R)
        w_lo = sb("w_lo", [P, E, UP2 + D], F32R)
        w_gate = sb("w_gate", [P, E])
        norm_w = sb("norm_w2", [P, 1])
        expert_id = sb("expert_id", [P, E])
        expert_sel = sb("expert_sel", [3 * E, E, P], BF16)
        sq = sb("sq2", [P, 2, D])
        ms = sb("ms2", [P, NT])
        rms = sb("rms2", [P, NT])
        neg_half = sb("neg_half2", [P, NT])
        h2 = sb("h2", [P, NT, D])
        h2T = sb("h2T", [P, B * S])
        h2T_hi = sb("h2T_hi", [P, B * S], F32R)
        h2T_lo = sb("h2T_lo", [P, B * S], F32R)
        logits = sb("logits", [P, NT, E])
        top = sb("top", [P, NT, 8])
        top_i = sb("top_i", [P, NT, 8], mybir.dt.uint32)
        top_f = sb("top_f", [P, NT, 8])
        gates = sb("gates", [P, NT, TOPK])
        gate_sum = sb("gate_sum", [P, NT])
        share = sb("share", [P, NT, E])
        share3 = sb("share3", [P, NT, 3, E], BF16)
        shareT = sb("shareT", [3 * E, B * S], BF16)
        act_hi = sb("act_hi", [P, 4, BLK], F32R)
        act_lo = sb("act_lo", [P, 4, BLK], F32R)
        hit = h2[:, 0:2 * NT * E // D, :].rearrange("p a d -> p (a d)").rearrange("p (a t e) -> p a t e", a=2, e=E)
        x1_free = x1[:].rearrange("p t d -> p (t d)").rearrange("p (a n) -> p a n", n=BLK)
        silu, act = x1_free[:, 0:2, :], x1_free[:, 2:4, :]
        h2T_free = h2T[:].rearrange("p (a n) -> p a n", n=BLK)
        gated, yT = h2T_free[:, 0:2, :], h2T_free[:, 2, :]
        stats = sb("stats2", [P, BT, 6])
        mv = sb("mv2", [P, BT, 2])
        rstd = sb("rstd2", [P, BT])
        ps = ctx.enter_context(nc.psum_tensor("ps_e", [P, 8, 512], F32))
        U, G, SH, Y, MISC = (0, 1), (2, 3), (4, 5), 6, 7

        names = ("ld_norm ld_gate ld_id ld_sel ld_w0 ld_w1 init sq ms rms h2 h2T_ps h2T_sb h2T_hi h2T_lo logits_ps top chain gexp gates "
                 "share3 shareT_ps shareT_sb w_hi w_lo g_ps sh_ps u_ps silu gated act act_hi act_lo down "
                 "yT y_ps x12 x3 stats var rstd final outd").split()
        z = {n: ctx.enter_context(nc.semaphore("e_" + n)) for n in names}
        block = ctx.enter_context(nc.Block())

        @block.sync
        def _(sp):
            sp.dma_start(norm_w[:], t["L0_ffn_ffn_norm_w"].rearrange("(p a) -> p a", a=1)).then_inc(z["ld_norm"], 16)
            sp.dma_start(w_gate[:], t["L0_ffn_gate_w"][:]).then_inc(z["ld_gate"], 16)
            sp.dma_start(expert_id[:], t["expert_id"][:]).then_inc(z["ld_id"], 16)
            for c in range(E // PER_LOAD):
                es = slice(c * PER_LOAD, (c + 1) * PER_LOAD)
                if c >= 2:
                    sp.wait_ge(z["w_lo"], (c - 1) * PER_LOAD)
                sp.dma_start(w_raw[:, c % 2, :, 0:UP2], t["L0_ffn_W_up"][es].rearrange("e p n -> p e n")).then_inc(z[f"ld_w{c % 2}"], 16)
                sp.dma_start(w_raw[:, c % 2, :, UP2:UP2 + D], t["L0_ffn_W_down"][es].rearrange("e p n -> p e n")).then_inc(z[f"ld_w{c % 2}"], 16)
                if c == 0:
                    sp.dma_start(expert_sel[:].rearrange("p e n -> p (e n)").bitcast(F32), t["expert_sel"][:]).then_inc(z["ld_sel"], 16)
            for b in range(BLOCKS):
                sp.wait_ge(z["final"], BT * (b + 1))
                sp.dma_start(out[b * BLK // S, b * BLK % S:b * BLK % S + BLK, :].rearrange("(t p) d -> p t d", p=P),
                             x2[:, b * BT:(b + 1) * BT, :]).then_inc(z["outd"], 16)
            sp.wait_ge(z["outd"], 16 * BLOCKS)

        @block.gpsimd
        def _(g):
            g.memset(neg_half[:], -0.5).then_inc(z["init"], 1)
            g.wait_ge(z["init"], 1)
            g.wait_ge(z["ms"], 1)
            g.tensor_tensor(rms[:], ms[:], neg_half[:], ALU.pow).then_inc(z["rms"], 1)
            g.wait_ge(z["h2"], NT)
            g.tensor_tensor(x2[:], x2[:], x1[:], ALU.add).then_inc(z["x12"], 1)

            def low(b, e, first):
                n = b * E + e
                g.wait_ge(z["act_hi"], n + 1)
                if not (first and e < 4):
                    g.wait_ge(z["down"], n - 3)
                g.tensor_tensor(act_lo[:, e % 4, :], act[:, e % 2, :], act_hi[:, e % 4, :], ALU.subtract).then_inc(z["act_lo"], 1)

            def norm(b):
                g.wait_ge(z["var"], b + 1)
                g.tensor_tensor(rstd[:], mv[:, :, 1], neg_half[:, 0:BT], ALU.pow).then_inc(z["rstd"], 1)

            def body(b, first):
                for e in range(E):
                    low(b, e, first)
                    if e == 7 and not first:
                        norm(b - 1)

            body(0, True)
            with g.Fori(1, BLOCKS) as b:
                body(b, False)
            norm(BLOCKS - 1)

        @block.scalar
        def _(act_e):
            def split(e):
                c = e // PER_LOAD
                act_e.wait_ge(z[f"ld_w{c % 2}"], 32 * (c // 2 + 1))
                nc.scalar.copy(w_hi[:, e, :], w_raw[:, c % 2, e % PER_LOAD, :]).then_inc(z["w_hi"], 1)

            act_e.wait_ge(z["ld_norm"], 16)
            for c in range(BLOCKS):
                act_e.wait_ge(z["h2T_ps"], c + 1)
                nc.scalar.activation(h2T[:, BLK * c:BLK * c + BLK], ps[:, c, :], ACT.Copy, scale=norm_w[:, 0:1]).then_inc(z["h2T_sb"], 1)
            for c in range(BLOCKS):
                act_e.wait_ge(z["h2T_sb"], c + 1)
                nc.scalar.copy(h2T_hi[:, BLK * c:BLK * c + BLK], h2T[:, BLK * c:BLK * c + BLK]).then_inc(z["h2T_hi"], 1)
            for e in range(AHEAD):
                split(e)
            act_e.wait_ge(z["gates"], 1)
            nc.scalar.activation(gates[:], gates[:], ACT.Exp).then_inc(z["gexp"], 1)
            for c in range(2):
                act_e.wait_ge(z["shareT_ps"], c + 1)
                nc.scalar.copy(shareT[:, 1024 * c:1024 * c + 1024], ps[0:3 * E, SH[c], :].bitcast(BF16)).then_inc(z["shareT_sb"], 1)

            act_e.wait_ge(z["x12"], 1)

            def high(n, e, first):
                act_e.wait_ge(z["act"], n + 1)
                if not (first and e < 4):
                    act_e.wait_ge(z["down"], n - 3)
                nc.scalar.copy(act_hi[:, e % 4, :], act[:, e % 2, :]).then_inc(z["act_hi"], 1)

            def y_copy(b):
                act_e.wait_ge(z["down"], E * (b + 1))
                if not isinstance(b, int) or b:
                    act_e.wait_ge(z["y_ps"], b)
                nc.scalar.copy(yT, ps[:, Y, :]).then_inc(z["yT"], 1)

            def body(b, first):
                for e in range(E):
                    n = b * E + e
                    act_e.wait_ge(z["g_ps"], n + 1)
                    if not (first and e < 2):
                        act_e.wait_ge(z["gated"], n - 1)
                    nc.scalar.activation(silu[:, e % 2, :], ps[:, G[e % 2], :], ACT.Silu).then_inc(z["silu"], 1)
                    if e == 2 and not first:
                        y_copy(b - 1)
                    if not (first and e == 0):
                        high(n - 1, (e - 1) % E, first)
                    if first and e + AHEAD < E:
                        split(e + AHEAD)

            body(0, True)
            with act_e.Fori(1, BLOCKS) as b:
                body(b, False)
            high(BLOCKS * E - 1, E - 1, False)
            y_copy(BLOCKS - 1)

        @block.vector
        def _(v):
            cnt = [0]

            def chain(ins):
                cnt[0] += 1
                ins.then_inc(z["chain"], 1)
                v.wait_ge(z["chain"], cnt[0])

            def split(e):
                v.wait_ge(z["w_hi"], e + 1)
                v.tensor_tensor(w_lo[:, e, :], w_raw[:, e // PER_LOAD % 2, e % PER_LOAD, :], w_hi[:, e, :], ALU.subtract).then_inc(z["w_lo"], 1)

            for n in range(NT):
                if n >= 2:
                    v.wait_ge(z["sq"], n - 1)
                v.tensor_tensor_reduce(out=sq[:, n % 2, :], in0=x2[:, n, :], in1=x2[:, n, :], scale=1.0, scalar=0.0, op0=ALU.mult, op1=ALU.add,
                                       accum_out=ms[:, n:n + 1]).then_inc(z["sq"], 1)
            v.wait_ge(z["sq"], NT)
            v.tensor_scalar(ms[:], ms[:], 1.0 / D, EPS, ALU.mult, ALU.add).then_inc(z["ms"], 1)
            v.wait_ge(z["rms"], 1)
            for n in range(NT):
                v.tensor_scalar(h2[:, n, :], x2[:, n, :], rms[:, n:n + 1], None, ALU.mult).then_inc(z["h2"], 1)
            for c in range(BLOCKS):
                v.wait_ge(z["h2T_hi"], c + 1)
                v.tensor_tensor(h2T_lo[:, BLK * c:BLK * c + BLK], h2T[:, BLK * c:BLK * c + BLK], h2T_hi[:, BLK * c:BLK * c + BLK],
                                ALU.subtract).then_inc(z["h2T_lo"], 1)
            v.wait_ge(z["logits_ps"], 1)
            chain(v.tensor_copy(logits[:].rearrange("p t e -> p (t e)"), ps[:, MISC, :]))
            for n in range(NT):
                v.max(top[:, n, :], logits[:, n, :]).then_inc(z["top"], 1)
            v.wait_ge(z["top"], NT)
            v.tensor_tensor(gates[:], top[:, :, 0:TOPK], top[:, :, 0:1].broadcast_to([P, NT, TOPK]), ALU.subtract).then_inc(z["gates"], 1)
            for n in range(NT):
                v.max_index(top_i[:, n, :], top[:, n, :], logits[:, n, :]).then_inc(z["top"], 1)
            v.wait_ge(z["top"], 2 * NT)
            chain(v.tensor_copy(top_f[:], top_i[:]))
            v.wait_ge(z["gexp"], 1)
            chain(v.tensor_reduce(gate_sum[:], gates[:], AX.X, ALU.add))
            chain(v.reciprocal(gate_sum[:], gate_sum[:]))
            chain(v.tensor_tensor(gates[:], gates[:], gate_sum[:].unsqueeze(2).broadcast_to([P, NT, TOPK]), ALU.mult))
            v.wait_ge(z["ld_id"], 16)
            for k in range(TOPK):
                chain(v.tensor_tensor(hit[:, 0, :, :], expert_id[:].unsqueeze(1).broadcast_to([P, NT, E]),
                                      top_f[:, :, k:k + 1].broadcast_to([P, NT, E]), ALU.is_equal))
                dst = share[:] if k == 0 else hit[:, 1, :, :]
                chain(v.tensor_tensor(dst, hit[:, 0, :, :], gates[:, :, k:k + 1].broadcast_to([P, NT, E]), ALU.mult))
                if k:
                    chain(v.tensor_tensor(share[:], share[:], hit[:, 1, :, :], ALU.add))
            chain(v.tensor_copy(share3[:, :, 0, :], share[:]))
            chain(v.tensor_tensor(share[:], share[:], share3[:, :, 0, :], ALU.subtract))
            chain(v.tensor_copy(share3[:, :, 1, :], share[:]))
            v.tensor_tensor(share3[:, :, 2, :], share[:], share3[:, :, 1, :], ALU.subtract).then_inc(z["share3"], 1)
            for e in range(AHEAD):
                split(e)

            def residual(b):
                v.wait_ge(z["y_ps"], b + 1)
                x = x2[:, ds(b * BT, BT), :].rearrange("p a n -> p (a n)")
                v.tensor_tensor(x, x, ps[:, MISC, :], ALU.add).then_inc(z["x3"], 1)

            def moments(b):
                v.wait_ge(z["x3"], b + 1)
                for k in range(BT):
                    v.bn_stats(stats[:, k, :], x2[:, ds(b * BT + k, 1), :].rearrange("p a n -> p (a n)")).then_inc(z["stats"], 1)

            def aggregate(b):
                for k in range(BT):
                    v.bn_aggr(mv[:, k, :], stats[:, k, :]).then_inc(z["stats"], 1)

            def variance(b):
                v.wait_ge(z["stats"], (2 * b + 2) * BT)
                v.tensor_scalar(mv[:, :, 1], mv[:, :, 1], EPS, None, ALU.add).then_inc(z["var"], 1)

            def normalise(b):
                v.wait_ge(z["rstd"], b + 1)
                for k in range(BT):
                    x = x2[:, ds(b * BT + k, 1), :].rearrange("p a n -> p (a n)")
                    v.tensor_scalar(x, x, mv[:, k, 0:1], rstd[:, k:k + 1], ALU.subtract, ALU.mult).then_inc(z["final"], 1)

            closing = {4: residual, 5: moments, 6: aggregate, 7: variance, 9: normalise}

            def body(b, first):
                for e in range(E):
                    n = b * E + e
                    if closing.get(e) is aggregate and not first:
                        v.wait_ge(z["stats"], (2 * b - 1) * BT)
                    v.wait_ge(z["silu"], n + 1)
                    v.wait_ge(z["sh_ps"], n + 1)
                    if not (first and e < 2):
                        v.wait_ge(z["act"], n - 1)
                    v.tensor_tensor(gated[:, e % 2, :], silu[:, e % 2, :], ps[:, SH[e % 2], :], ALU.mult).then_inc(z["gated"], 1)
                    v.wait_ge(z["gated"], n + 1)
                    v.wait_ge(z["u_ps"], n + 1)
                    if not (first and e < 2):
                        v.wait_ge(z["act_lo"], n - 1)
                    v.tensor_tensor(act[:, e % 2, :], gated[:, e % 2, :], ps[:, U[e % 2], :], ALU.mult).then_inc(z["act"], 1)
                    if first and e + AHEAD < E:
                        split(e + AHEAD)
                    if e in closing and not first:
                        closing[e](b - 1)

            v.wait_ge(z["x12"], 1)
            body(0, True)
            with v.Fori(1, BLOCKS) as b:
                body(b, False)
            for step in closing.values():
                if step is aggregate:
                    v.wait_ge(z["stats"], (2 * BLOCKS - 1) * BT)
                step(BLOCKS - 1)

        @block.tensor
        def _(pe):
            mm = nc.tensor.matmul
            tr = nc.tensor.transpose
            for n in range(NT):
                pe.wait_ge(z["h2"], n + 1)
                m = tr(ps[:, n // BT, (n % BT) * P:(n % BT + 1) * P], h2[:, n, :], ident[:])
                if n % BT == BT - 1:
                    m.then_inc(z["h2T_ps"], 1)
            pe.wait_ge(z["ld_gate"], 16)
            for n in range(NT):
                if n % BT == 0:
                    pe.wait_ge(z["h2T_sb"], n // BT + 1)
                o = ps[:, MISC, n * E:(n + 1) * E]
                mm(o, h2T[:, n * P:(n + 1) * P], w_gate[:], start=True, stop=False)
                m = mm(o, bias_sel[:], bias_of(bias_rows, "L0_ffn_gate_b"), start=False, stop=True)
            m.then_inc(z["logits_ps"], 1)
            pe.wait_ge(z["share3"], 1)
            for n in range(NT):
                m = tr(ps[0:3 * E, SH[n // 8], 64 * (n % 8):64 * (n % 8) + 64].bitcast(BF16), share3[:, n, :, :].rearrange("p a e -> p (a e)"), ident16[:])
                if n % 8 == 7:
                    m.then_inc(z["shareT_ps"], 1)
            pe.wait_ge(z["shareT_sb"], 2)
            pe.wait_ge(z["ld_sel"], 16)

            def up(b, e, w, bank, done):
                at = slice(w * DFF, w * DFF + DFF)
                hi, lo = h2T_hi[:, ds(b * BLK, BLK)], h2T_lo[:, ds(b * BLK, BLK)]
                o = ps[:, bank[e % 2], :]
                mm(o, w_hi[:, e, at], hi, start=True, stop=False)
                mm(o, w_hi[:, e, at], lo, start=False, stop=False)
                mm(o, w_lo[:, e, at], hi, start=False, stop=True).then_inc(z[done], 1)

            def down(n, e, first):
                pe.wait_ge(z["act_hi"], n + 1)
                w = slice(UP2, UP2 + D)
                mm(ps[:, Y, :], w_lo[:, e, w], act_hi[:, e % 4, :], start=(e == 0), stop=False)
                mm(ps[:, Y, :], w_hi[:, e, w], act_hi[:, e % 4, :], start=False, stop=False)
                pe.wait_ge(z["act_lo"], n + 1)
                mm(ps[:, Y, :], w_hi[:, e, w], act_lo[:, e % 4, :], start=False, stop=(e == E - 1)).then_inc(z["down"], 1)

            def turn(b):
                pe.wait_ge(z["yT"], b + 1)
                for k in range(BT):
                    m = tr(ps[:, MISC, k * P:(k + 1) * P], yT[:, k * P:(k + 1) * P], ident[:])
                m.then_inc(z["y_ps"], 1)

            def body(b, first):
                for e in range(E):
                    n = b * E + e
                    if first:
                        pe.wait_ge(z["w_lo"], e + 1)
                    if not (first and e < 2):
                        pe.wait_ge(z["silu"], n - 1)
                    up(b, e, 1, G, "g_ps")
                    if not (first and e < 2):
                        pe.wait_ge(z["gated"], n - 1)
                    mm(ps[:, SH[e % 2], :], expert_sel[:, e, :], shareT[:, ds(b * BLK, BLK)], start=True, stop=True).then_inc(z["sh_ps"], 1)
                    if not (first and e < 2):
                        pe.wait_ge(z["act"], n - 1)
                    up(b, e, 0, U, "u_ps")
                    if not (first and e < 2):
                        if e == 2 and not first:
                            pe.wait_ge(z["yT"], b)
                        down(n - 2, (e - 2) % E, first)
                    if e == 3 and not first:
                        if not isinstance(b, int):
                            pe.wait_ge(z["x3"], b - 1)
                        turn(b - 1)

            pe.wait_ge(z["h2T_lo"], BLOCKS)
            body(0, True)
            body(1, False)
            with pe.Fori(2, BLOCKS) as b:
                body(b, False)
            for n in (BLOCKS * E - 2, BLOCKS * E - 1):
                down(n, n % E, False)
            pe.wait_ge(z["x3"], BLOCKS - 1)
            turn(BLOCKS - 1)

def build(nc, t, out):
    with ExitStack() as ctx:
        def sb(name, shape, dt=F32):
            return ctx.enter_context(nc.sbuf_tensor(name, shape, dt))
        x1 = sb("x1", [P, B * TILES, D])
        ident = sb("ident", [P, P])
        ident16 = sb("ident16", [P, P], BF16)
        bias_sel = sb("bias_sel", [P, P], BF16)
        bias_rows = sb("bias_rows", [P, BIASES], BF16)
        x2 = sb("x2", [P, B * TILES, D])
        with ExitStack() as window:
            inputs = WindowInputs(nc, window, t)
            differential_attention(nc, t, x1, ident, ident16, bias_sel, bias_rows, inputs.load)
            window_attention(nc, inputs, x1, x2, ident, ident16, bias_sel, bias_rows)
        experts(nc, t, x1, x2, ident, ident16, bias_sel, bias_rows, out)


def constants():
    c = {}
    c["ident"] = np.eye(P, dtype=np.float32)
    c["head_mean"] = np.kron(np.eye(H, dtype=np.float32), np.full((DH, DH), 1.0 / DH, np.float32))
    c["bias_sel"] = np.repeat((np.arange(P) < 3).astype(np.float32)[:, None], P, axis=1)
    c["zeros16"] = np.zeros((2, ONES), np.float32)
    c["ones16"] = np.full((2, ONES), 0x3F803F80, np.uint32).view(np.float32)
    pos = np.arange(S, dtype=np.float32) / np.float32(32.0)
    inv = (1.0 / np.float32(150000.0) ** (np.arange(0, FDH, 2, dtype=np.float32) / np.float32(FDH))).astype(np.float32)
    f = pos[:, None] * inv[None, :]
    cos = np.repeat(np.cos(f), 2, axis=1).astype(np.float32)
    sin = np.stack([-np.sin(f), np.sin(f)], axis=2).reshape(S, FDH).astype(np.float32)
    c["rope_c"] = cos.reshape(TILES, P, FDH).transpose(1, 0, 2)
    c["rope_s"] = sin.reshape(TILES, P, FDH).transpose(1, 0, 2)
    p, k = np.arange(P)[:, None], np.arange(2 * P)[None, :]
    seen = (k >= p) & (k <= p + WINDOW)
    first = seen & (k >= P)
    masked = np.array(MASKED, np.float32).view(np.uint32) >> 16
    m = np.stack([np.where(x, 0, masked).astype(np.uint16) for x in (first, first, seen, seen)], axis=1)
    c["mask"] = m.reshape(P, 8 * P).view(np.float32)
    c["expert_id"] = np.tile(np.arange(E, dtype=np.float32), (P, 1))
    c["expert_sel"] = np.tile(np.repeat(np.eye(E, dtype=np.uint32) * np.uint32(0x3F803F80), P // 2, axis=1), (3, 1)).view(np.float32)
    return c


def kernel(**inputs):
    import concourse.bacc as bacc
    from concourse.bass_utils import run_bass_kernel_spmd

    nc = bacc.Bacc("TRN2", target_bir_lowering=False, num_devices=1)
    nc.disable_value_cache = True
    arrays, t = {}, {}
    for name, a in {**inputs, **constants()}.items():
        a = np.ascontiguousarray(a)
        arrays["in_" + name] = a
        t[name] = nc.dram_tensor("in_" + name, a.shape, mybir.dt.from_np(a.dtype), kind="ExternalInput").ap()
    out = nc.dram_tensor("out_dram", (B, S, D), F32, kind="ExternalOutput").ap()
    build(nc, t, out)
    r = run_bass_kernel_spmd(nc, [arrays], core_ids=[0])
    return r.results[0]["out_dram"]
```
